# Optimizing a Trainium2 kernel written in Bass

```python
import numpy as np
import jax
import jax.numpy as jnp

def _softmax(x, axis=-1):
    return jax.nn.softmax(x, axis=axis)

def _gelu(x):
    return jax.nn.gelu(x, approximate=True)

def _silu(x):
    return jax.nn.silu(x)

def _sigmoid(x):
    return jax.nn.sigmoid(x)

def _layernorm(x, axis=-1, eps=1e-05):
    m = jnp.mean(x, axis=axis, keepdims=True)
    v = jnp.var(x, axis=axis, keepdims=True)
    return (x - m) / jnp.sqrt(v + eps)

def _scatter_add(tgt, idx, src, axis=0):
    return tgt.at[idx].add(src)

def _segment_sum(src, seg, n):
    return jax.ops.segment_sum(src, seg, n)
kernel_name = 'mk_adaln_d1_jaxref_r8_2d4b5d'

def setup_inputs(seed: int=0):
    np.random.seed(seed)
    _w = jnp.asarray

    def _L0_attn_setup():
        import jax, jax.numpy as jnp
        import numpy as np
        B, S, H = (4, 256, 256)
        key = jax.random.key(seed)
        k1, k2, k3 = jax.random.split(key, 3)
        xav_qkv = float(np.sqrt(6.0 / (H + 3 * H)))
        xav_out = float(np.sqrt(6.0 / (H + H)))
        return {'hidden_states': jax.random.normal(k1, (B, S, H), dtype=jnp.float32), 'w_qkv': jax.random.uniform(k2, (3 * H, H), minval=-xav_qkv, maxval=xav_qkv, dtype=jnp.float32), 'b_qkv': jnp.zeros((3 * H,), dtype=jnp.float32), 'w_out': jax.random.uniform(k3, (H, H), minval=-xav_out, maxval=xav_out, dtype=jnp.float32), 'b_out': jnp.zeros((H,), dtype=jnp.float32)}
    _L0_attn_in = _L0_attn_setup()

    def _L0_ffn_setup():
        import jax, jax.numpy as jnp
        import numpy as np
        COST_LAMBDA = 1e-07
        HID = [128, 256, 384, 512, 128, 256, 384, 512]
        TOP_K = 2

        def _gelu(v):
            return jax.nn.gelu(v, approximate=False)

        def _forward(x, down_w, down_b, up_w, up_b, router_w, router_b, shared_w1, shared_b1, shared_w2, shared_b2, core_w, core_b, expert_params):
            E = len(expert_params)
            h = x @ down_w + down_b
            cost = jnp.array([w1.shape[0] * w1.shape[1] + w2.shape[0] * w2.shape[1] for w1, _, w2, _ in expert_params], jnp.float32)
            logits = x @ router_w + router_b - COST_LAMBDA * cost
            probs = jax.nn.softmax(logits, axis=-1)
            topv, topi = jax.lax.top_k(probs, TOP_K)
            gate = jax.nn.softmax(topv, axis=-1)
            out = jnp.zeros_like(h)
            for k in range(TOP_K):
                mask = jax.nn.one_hot(topi[..., k], E, dtype=h.dtype)
                acc = jnp.zeros_like(h)
                for e, (w1, b1, w2, b2) in enumerate(expert_params):
                    hm = h * mask[..., e:e + 1]
                    acc = acc + (_gelu(_gelu(hm) @ w1 + b1) @ w2 + b2)
                out = out + acc * gate[..., k:k + 1]
            out = out + 0.1 * (_gelu(_gelu(h) @ shared_w1 + shared_b1) @ shared_w2 + shared_b2)
            out = out @ up_w + up_b
            out = out + (_gelu(x) @ core_w + core_b)
            return out
        key = jax.random.key(seed)
        ks = iter(jax.random.split(key, 80))

        def W(shape):
            return jax.random.normal(next(ks), shape, jnp.float32) * 0.02
        B, T, D, L = (4, 256, 256, 128)
        inp = {'x': jax.random.normal(next(ks), (B, T, D), jnp.float32)}
        inp['down_w'] = W((D, L))
        inp['down_b'] = jnp.zeros((L,), jnp.float32)
        inp['up_w'] = W((L, D))
        inp['up_b'] = jnp.zeros((D,), jnp.float32)
        inp['router_w'] = W((D, len(HID)))
        inp['router_b'] = jnp.zeros((len(HID),), jnp.float32)
        inp['shared_w1'] = W((L, L))
        inp['shared_b1'] = jnp.zeros((L,), jnp.float32)
        inp['shared_w2'] = W((L, L))
        inp['shared_b2'] = jnp.zeros((L,), jnp.float32)
        inp['core_w'] = W((D, D))
        inp['core_b'] = jnp.zeros((D,), jnp.float32)
        for e, h in enumerate(HID):
            inp[f'e{e}_w1'] = W((L, h))
            inp[f'e{e}_b1'] = jnp.zeros((h,), jnp.float32)
            inp[f'e{e}_w2'] = W((h, L))
            inp[f'e{e}_b2'] = jnp.zeros((L,), jnp.float32)
        return inp
    _L0_ffn_in = _L0_ffn_setup()
    _L0_c = _w((lambda *s: np.random.randn(*s).astype(np.float32) * 0.05)(4, 256))
    _L0_wmod = _w((lambda *s: np.random.randn(*s).astype(np.float32) * 0.05)(256, 6 * 256) * 256 ** (-0.5))
    _d = {'L0_attn_hidden_states': _L0_attn_in['hidden_states'], 'L0_attn_w_qkv': _L0_attn_in['w_qkv'], 'L0_attn_b_qkv': _L0_attn_in['b_qkv'], 'L0_attn_w_out': _L0_attn_in['w_out'], 'L0_attn_b_out': _L0_attn_in['b_out'], 'L0_ffn_down_w': _L0_ffn_in['down_w'], 'L0_ffn_down_b': _L0_ffn_in['down_b'], 'L0_ffn_up_w': _L0_ffn_in['up_w'], 'L0_ffn_up_b': _L0_ffn_in['up_b'], 'L0_ffn_router_w': _L0_ffn_in['router_w'], 'L0_ffn_router_b': _L0_ffn_in['router_b'], 'L0_ffn_shared_w1': _L0_ffn_in['shared_w1'], 'L0_ffn_shared_b1': _L0_ffn_in['shared_b1'], 'L0_ffn_shared_w2': _L0_ffn_in['shared_w2'], 'L0_ffn_shared_b2': _L0_ffn_in['shared_b2'], 'L0_ffn_core_w': _L0_ffn_in['core_w'], 'L0_ffn_core_b': _L0_ffn_in['core_b'], 'L0_ffn_e0_w1': _L0_ffn_in['e0_w1'], 'L0_ffn_e0_b1': _L0_ffn_in['e0_b1'], 'L0_ffn_e0_w2': _L0_ffn_in['e0_w2'], 'L0_ffn_e0_b2': _L0_ffn_in['e0_b2'], 'L0_ffn_e1_w1': _L0_ffn_in['e1_w1'], 'L0_ffn_e1_b1': _L0_ffn_in['e1_b1'], 'L0_ffn_e1_w2': _L0_ffn_in['e1_w2'], 'L0_ffn_e1_b2': _L0_ffn_in['e1_b2'], 'L0_ffn_e2_w1': _L0_ffn_in['e2_w1'], 'L0_ffn_e2_b1': _L0_ffn_in['e2_b1'], 'L0_ffn_e2_w2': _L0_ffn_in['e2_w2'], 'L0_ffn_e2_b2': _L0_ffn_in['e2_b2'], 'L0_ffn_e3_w1': _L0_ffn_in['e3_w1'], 'L0_ffn_e3_b1': _L0_ffn_in['e3_b1'], 'L0_ffn_e3_w2': _L0_ffn_in['e3_w2'], 'L0_ffn_e3_b2': _L0_ffn_in['e3_b2'], 'L0_ffn_e4_w1': _L0_ffn_in['e4_w1'], 'L0_ffn_e4_b1': _L0_ffn_in['e4_b1'], 'L0_ffn_e4_w2': _L0_ffn_in['e4_w2'], 'L0_ffn_e4_b2': _L0_ffn_in['e4_b2'], 'L0_ffn_e5_w1': _L0_ffn_in['e5_w1'], 'L0_ffn_e5_b1': _L0_ffn_in['e5_b1'], 'L0_ffn_e5_w2': _L0_ffn_in['e5_w2'], 'L0_ffn_e5_b2': _L0_ffn_in['e5_b2'], 'L0_ffn_e6_w1': _L0_ffn_in['e6_w1'], 'L0_ffn_e6_b1': _L0_ffn_in['e6_b1'], 'L0_ffn_e6_w2': _L0_ffn_in['e6_w2'], 'L0_ffn_e6_b2': _L0_ffn_in['e6_b2'], 'L0_ffn_e7_w1': _L0_ffn_in['e7_w1'], 'L0_ffn_e7_b1': _L0_ffn_in['e7_b1'], 'L0_ffn_e7_w2': _L0_ffn_in['e7_w2'], 'L0_ffn_e7_b2': _L0_ffn_in['e7_b2'], 'L0_c': _L0_c, 'L0_wmod': _L0_wmod}
    _x0 = _d['L0_attn_hidden_states']
    _d['L0_attn_hidden_states'] = jax.random.normal(jax.random.fold_in(jax.random.key(seed), 1), (4, 1024, 256), dtype=_x0.dtype)
    del _x0
    return _d

def reference(L0_attn_hidden_states, L0_attn_w_qkv, L0_attn_b_qkv, L0_attn_w_out, L0_attn_b_out, L0_ffn_down_w, L0_ffn_down_b, L0_ffn_up_w, L0_ffn_up_b, L0_ffn_router_w, L0_ffn_router_b, L0_ffn_shared_w1, L0_ffn_shared_b1, L0_ffn_shared_w2, L0_ffn_shared_b2, L0_ffn_core_w, L0_ffn_core_b, L0_ffn_e0_w1, L0_ffn_e0_b1, L0_ffn_e0_w2, L0_ffn_e0_b2, L0_ffn_e1_w1, L0_ffn_e1_b1, L0_ffn_e1_w2, L0_ffn_e1_b2, L0_ffn_e2_w1, L0_ffn_e2_b1, L0_ffn_e2_w2, L0_ffn_e2_b2, L0_ffn_e3_w1, L0_ffn_e3_b1, L0_ffn_e3_w2, L0_ffn_e3_b2, L0_ffn_e4_w1, L0_ffn_e4_b1, L0_ffn_e4_w2, L0_ffn_e4_b2, L0_ffn_e5_w1, L0_ffn_e5_b1, L0_ffn_e5_w2, L0_ffn_e5_b2, L0_ffn_e6_w1, L0_ffn_e6_b1, L0_ffn_e6_w2, L0_ffn_e6_b2, L0_ffn_e7_w1, L0_ffn_e7_b1, L0_ffn_e7_w2, L0_ffn_e7_b2, L0_c, L0_wmod):

    def _L0_attn_ref(hidden_states, w_qkv, b_qkv, w_out, b_out):
        import jax, jax.numpy as jnp
        import numpy as np
        B, S, H = (4, 256, 256)
        Bc, Sc, Hc = hidden_states.shape
        scaling = jnp.sqrt(jnp.asarray(Hc, hidden_states.dtype))
        qkv = jnp.einsum('bsh,oh->bso', hidden_states, w_qkv) + b_qkv
        q, k, v = jnp.split(qkv, 3, axis=-1)
        scores = jnp.einsum('bqh,bkh->bqk', q, k) / scaling
        probs = jax.nn.softmax(scores, axis=-1)
        context = jnp.einsum('bqk,bkh->bqh', probs, v)
        out = jnp.einsum('bsh,oh->bso', context, w_out) + b_out
        return out

    def _L0_ffn_ref(x, down_w, down_b, up_w, up_b, router_w, router_b, shared_w1, shared_b1, shared_w2, shared_b2, core_w, core_b, e0_w1, e0_b1, e0_w2, e0_b2, e1_w1, e1_b1, e1_w2, e1_b2, e2_w1, e2_b1, e2_w2, e2_b2, e3_w1, e3_b1, e3_w2, e3_b2, e4_w1, e4_b1, e4_w2, e4_b2, e5_w1, e5_b1, e5_w2, e5_b2, e6_w1, e6_b1, e6_w2, e6_b2, e7_w1, e7_b1, e7_w2, e7_b2):
        import jax, jax.numpy as jnp
        import numpy as np
        COST_LAMBDA = 1e-07
        HID = [128, 256, 384, 512, 128, 256, 384, 512]
        TOP_K = 2

        def _gelu(v):
            return jax.nn.gelu(v, approximate=False)

        def _forward(x, down_w, down_b, up_w, up_b, router_w, router_b, shared_w1, shared_b1, shared_w2, shared_b2, core_w, core_b, expert_params):
            E = len(expert_params)
            h = x @ down_w + down_b
            cost = jnp.array([w1.shape[0] * w1.shape[1] + w2.shape[0] * w2.shape[1] for w1, _, w2, _ in expert_params], jnp.float32)
            logits = x @ router_w + router_b - COST_LAMBDA * cost
            probs = jax.nn.softmax(logits, axis=-1)
            topv, topi = jax.lax.top_k(probs, TOP_K)
            gate = jax.nn.softmax(topv, axis=-1)
            out = jnp.zeros_like(h)
            for k in range(TOP_K):
                mask = jax.nn.one_hot(topi[..., k], E, dtype=h.dtype)
                acc = jnp.zeros_like(h)
                for e, (w1, b1, w2, b2) in enumerate(expert_params):
                    hm = h * mask[..., e:e + 1]
                    acc = acc + (_gelu(_gelu(hm) @ w1 + b1) @ w2 + b2)
                out = out + acc * gate[..., k:k + 1]
            out = out + 0.1 * (_gelu(_gelu(h) @ shared_w1 + shared_b1) @ shared_w2 + shared_b2)
            out = out @ up_w + up_b
            out = out + (_gelu(x) @ core_w + core_b)
            return out
        ep = [(e0_w1, e0_b1, e0_w2, e0_b2), (e1_w1, e1_b1, e1_w2, e1_b2), (e2_w1, e2_b1, e2_w2, e2_b2), (e3_w1, e3_b1, e3_w2, e3_b2), (e4_w1, e4_b1, e4_w2, e4_b2), (e5_w1, e5_b1, e5_w2, e5_b2), (e6_w1, e6_b1, e6_w2, e6_b2), (e7_w1, e7_b1, e7_w2, e7_b2)]
        return _forward(x, down_w, down_b, up_w, up_b, router_w, router_b, shared_w1, shared_b1, shared_w2, shared_b2, core_w, core_b, ep)
    x = L0_attn_hidden_states
    mod = (_silu(L0_c) @ L0_wmod).reshape(L0_c.shape[0], 6, 1, -1)
    sa, ca, ga, sb, cb, gb = (mod[:, 0], mod[:, 1], mod[:, 2], mod[:, 3], mod[:, 4], mod[:, 5])
    ga = (2 * (ga >= 0) - 1) * jnp.maximum(jnp.abs(ga), 0.25)
    gb = (2 * (gb >= 0) - 1) * jnp.maximum(jnp.abs(gb), 0.25)
    h = _layernorm(x, axis=-1) * (1 + ca) + sa
    x = x + ga * _L0_attn_ref(h, L0_attn_w_qkv, L0_attn_b_qkv, L0_attn_w_out, L0_attn_b_out)
    h = _layernorm(x, axis=-1) * (1 + cb) + sb
    x = x + gb * _L0_ffn_ref(h, L0_ffn_down_w, L0_ffn_down_b, L0_ffn_up_w, L0_ffn_up_b, L0_ffn_router_w, L0_ffn_router_b, L0_ffn_shared_w1, L0_ffn_shared_b1, L0_ffn_shared_w2, L0_ffn_shared_b2, L0_ffn_core_w, L0_ffn_core_b, L0_ffn_e0_w1, L0_ffn_e0_b1, L0_ffn_e0_w2, L0_ffn_e0_b2, L0_ffn_e1_w1, L0_ffn_e1_b1, L0_ffn_e1_w2, L0_ffn_e1_b2, L0_ffn_e2_w1, L0_ffn_e2_b1, L0_ffn_e2_w2, L0_ffn_e2_b2, L0_ffn_e3_w1, L0_ffn_e3_b1, L0_ffn_e3_w2, L0_ffn_e3_b2, L0_ffn_e4_w1, L0_ffn_e4_b1, L0_ffn_e4_w2, L0_ffn_e4_b2, L0_ffn_e5_w1, L0_ffn_e5_b1, L0_ffn_e5_w2, L0_ffn_e5_b2, L0_ffn_e6_w1, L0_ffn_e6_b1, L0_ffn_e6_w2, L0_ffn_e6_b2, L0_ffn_e7_w1, L0_ffn_e7_b1, L0_ffn_e7_w2, L0_ffn_e7_b2)
    return x

_drawn_inputs = setup_inputs


def setup_inputs(seed=0):
    import zlib

    import numpy as np

    out = dict(_drawn_inputs(seed))
    spreads = {'L0_attn_b_qkv': (0.0, 0.333),
     'L0_attn_b_out': (0.0, 0.339),
     'L0_ffn_down_b': (0.0, 0.8),
     'L0_ffn_up_b': (0.0, 0.334),
     'L0_ffn_router_b': (0.0, 0.8),
     'L0_ffn_shared_b1': (0.0, 0.8),
     'L0_ffn_shared_b2': (0.0, 0.8),
     'L0_ffn_core_b': (0.0, 0.308),
     'L0_ffn_e0_b1': (0.0, 0.8),
     'L0_ffn_e0_b2': (0.0, 0.8),
     'L0_ffn_e1_b1': (0.0, 0.8),
     'L0_ffn_e1_b2': (0.0, 0.8),
     'L0_ffn_e2_b1': (0.0, 0.8),
     'L0_ffn_e2_b2': (0.0, 0.8),
     'L0_ffn_e3_b1': (0.0, 0.8),
     'L0_ffn_e3_b2': (0.0, 0.8),
     'L0_ffn_e4_b1': (0.0, 0.8),
     'L0_ffn_e4_b2': (0.0, 0.8),
     'L0_ffn_e5_b1': (0.0, 0.8),
     'L0_ffn_e5_b2': (0.0, 0.8),
     'L0_ffn_e6_b1': (0.0, 0.8),
     'L0_ffn_e6_b2': (0.0, 0.8),
     'L0_ffn_e7_b1': (0.0, 0.8),
     'L0_ffn_e7_b2': (0.0, 0.8)}
    factors = {'L0_attn_w_qkv': 2.668,
     'L0_ffn_down_w': 8.0,
     'L0_ffn_up_w': 3.468,
     'L0_ffn_router_w': 8.0,
     'L0_ffn_shared_w1': 8.0,
     'L0_ffn_shared_w2': 8.0,
     'L0_ffn_e0_w1': 8.0,
     'L0_ffn_e0_w2': 8.0,
     'L0_ffn_e1_w1': 8.0,
     'L0_ffn_e1_w2': 8.0,
     'L0_ffn_e2_w1': 8.0,
     'L0_ffn_e2_w2': 8.0,
     'L0_ffn_e3_w1': 8.0,
     'L0_ffn_e3_w2': 8.0,
     'L0_ffn_e4_w1': 8.0,
     'L0_ffn_e4_w2': 8.0,
     'L0_ffn_e5_w1': 8.0,
     'L0_ffn_e5_w2': 8.0,
     'L0_ffn_e6_w1': 8.0,
     'L0_ffn_e6_w2': 8.0,
     'L0_ffn_e7_w1': 8.0,
     'L0_ffn_e7_w2': 8.0}
    for name, (base, spread) in spreads.items():
        noise = np.random.default_rng([zlib.crc32(name.encode()), seed]).standard_normal(out[name].shape)
        drawn = base * np.exp(spread * noise) if base else spread * noise
        out[name] = jnp.asarray(drawn.astype(out[name].dtype))
    for name, factor in factors.items():
        out[name] = (out[name] * factor).astype(out[name].dtype)
    return out
```

```python
import concourse.bass as bass
from concourse import mybir
from contextlib import ExitStack

B, S, D, L = 4, 1024, 256, 128
P = 128
DC = D // P
TB = S // P
CH = 512
HB = S // CH
NCH = B * HB
TC = CH // P
HID = [128, 256, 384, 512, 128, 256, 384, 512]
E = len(HID)
LN_EPS = 1e-5
COST_LAMBDA = 1e-7
SCORE_SCALE = 1.0 / 16.0
assert SCORE_SCALE * SCORE_SCALE * D == 1.0

UNITS = [(0, 0)] + [(e + 1, j) for e, h in enumerate(HID) for j in range(h // P)]
NU = len(UNITS)
LAST_UNIT = {g: max(u for u, (gg, _) in enumerate(UNITS) if gg == g) for g in range(E + 1)}
FIRST_UNIT = {g: min(u for u, (gg, _) in enumerate(UNITS) if gg == g) for g in range(E + 1)}
GROUPS = E + 1

fp32 = mybir.dt.float32
fp32r = mybir.dt.float32r
u32 = mybir.dt.uint32
ALU = mybir.AluOpType
ACT = mybir.ActivationFunctionType
AX = mybir.AxisListType.X


class Chain:

    def __init__(self, eng, sem, base=0):
        self.eng, self.sem, self.base, self.n = eng, sem, base, 0

    def mark(self, ins):
        self.n += 1
        ins.then_inc(self.sem, 1)
        return self.base + self.n

    def link(self, ins):
        self.eng.wait_ge(self.sem, self.mark(ins))

    def hold(self, ins, idle):
        hold(self.eng, self.sem, self.mark(ins), idle)


def hold(eng, sem, value, idle):
    eng.wait_ge(sem, value)
    eng.sem_inc(idle, 1)


def matmul3(nc, out, stat, mov, start, stop):
    (sh, sl), (mh, ml) = stat, mov
    nc.tensor.matmul(out, sh, mh, start=start, stop=False)
    nc.tensor.matmul(out, sh, ml, start=False, stop=False)
    return nc.tensor.matmul(out, sl, mh, start=False, stop=stop)


def adaln_block(nc, a, out):
    hf_dram = nc.dram_tensor("hf_dram", (NCH, P, DC, CH), fp32, kind="Internal").ap()
    gates_dram = nc.dram_tensor("gates_dram", (NCH, E, CH), fp32, kind="Internal").ap()
    ctx = ExitStack()
    with ctx:
        def sbt(c, name, shape, dt=fp32):
            return c.enter_context(nc.sbuf_tensor(name, shape, dt))

        def pst(c, name, shape):
            return c.enter_context(nc.psum_tensor(name, shape, fp32))

        def sems(*names):
            return [ctx.enter_context(nc.semaphore(n)) for n in names]

        x_all = sbt(ctx, "x_all", [P, B * TB, D])
        w1h = sbt(ctx, "w1h", [P, NU, P], fp32r)
        w1l = sbt(ctx, "w1l", [P, NU, P], fp32r)
        w2h = sbt(ctx, "w2h", [P, NU, L], fp32r)
        w2l = sbt(ctx, "w2l", [P, NU, L], fp32r)
        downh = sbt(ctx, "downh", [P, DC, L], fp32r)
        downl = sbt(ctx, "downl", [P, DC, L], fp32r)
        coreh = sbt(ctx, "coreh", [P, DC, D], fp32r)
        corel = sbt(ctx, "corel", [P, DC, D], fp32r)
        uph = sbt(ctx, "uph", [P, D], fp32r)
        upl = sbt(ctx, "upl", [P, D], fp32r)
        gb_bc = sbt(ctx, "gb_bc", [P, B, D])
        gbias_bc = sbt(ctx, "gbias_bc", [P, B, D])
        b1c = sbt(ctx, "b1c", [P, NU])
        a0c = sbt(ctx, "a0c", [P, NU])
        b2c = sbt(ctx, "b2c", [P, GROUPS])
        u0 = sbt(ctx, "u0", [P, E, L])
        downbc = sbt(ctx, "downbc", [P, 1])
        ident = sbt(ctx, "ident", [P, P])
        ones2 = sbt(ctx, "ones2", [P, 2])
        attn = ExitStack()
        setup = ExitStack()
        Ah = sbt(attn, "Ah", [P, DC, D], fp32r)
        Al = sbt(attn, "Al", [P, DC, D], fp32r)
        Mh = sbt(attn, "Mh", [P, DC, D], fp32r)
        Ml = sbt(attn, "Ml", [P, DC, D], fp32r)
        bqk = sbt(attn, "bqk", [P, DC])
        ga_bc = sbt(attn, "ga_bc", [P, B, D])
        gab_bc = sbt(attn, "gab_bc", [P, B, D])
        modc = sbt(attn, "modc", [P, B, 4, DC])
        rwp = sbt(attn, "rwp", [P, DC, P], fp32r)
        rwh = sbt(attn, "rwh", [P, DC, P], fp32r)
        rb_bc = sbt(attn, "rb_bc", [P, E])
        iota8 = sbt(attn, "iota8", [P, E])

        wqkv = sbt(setup, "wqkv", [P, 3 * DC, D])
        wout = sbt(setup, "wout", [P, DC, D])
        woT = sbt(setup, "woT", [P, DC, D])
        wmod = sbt(setup, "wmod", [P, DC, 6 * D])
        cT = sbt(setup, "cT", [P, DC, B])
        sig = sbt(setup, "sig", [P, DC, B])
        scT = sbt(setup, "scT", [P, DC, B])
        scb = sbt(setup, "scb", [P, DC, B, P])
        bqc = sbt(setup, "bqc", [P, 2 * DC, 1])
        bvc = sbt(setup, "bvc", [P, DC, 1])
        bvb = sbt(setup, "bvb", [P, DC, P])
        bo_bc = sbt(setup, "bo_bc", [P, D])
        upb_bc = sbt(setup, "upb_bc", [P, D])
        coreb_bc = sbt(setup, "coreb_bc", [P, D])
        afull = sbt(setup, "afull", [P, DC, D])
        mfull = sbt(setup, "mfull", [P, DC, D])
        rwraw = sbt(setup, "rwraw", [P, DC, E])
        rbraw = sbt(setup, "rbraw", [P, E])
        t1 = sbt(setup, "t1", [P, D])
        t2 = sbt(setup, "t2", [P, D])
        sps = ExitStack()
        bank = [pst(sps, f"bank{k}", [P, 512]) for k in range(8)]

        (wq_in, c_in, wmod_in, x_in, rows_in, cols_in, rw_in, b1_in, id_made, wo_turned, woT_made,
         fold_ps, fold_made, scT_made, scb_made, bias_ps, mod_ps, brow_ps, g_ps, g_used, sig_made,
         dve_s, a0_made, pool_s, pool_idle) = sems(
            "wq_in", "c_in", "wmod_in", "x_in", "rows_in", "cols_in", "rw_in", "b1_in", "id_made",
            "wo_turned", "woT_made", "fold_ps", "fold_made", "scT_made", "scb_made", "bias_ps", "mod_ps",
            "brow_ps", "g_ps", "g_used", "sig_made", "dve_s", "a0_made", "pool_s", "pool_idle")

        with nc.Block() as block:
            @block.sync
            def _(sp):
                sp.dma_start(wqkv[:], a["w_qkv"].rearrange("(c p) i -> p c i", p=P)).then_inc(wq_in, 16)
                sp.dma_start(wout[:], a["w_out"].rearrange("(c p) o -> p c o", p=P)).then_inc(wq_in, 16)
                for b in range(B):
                    sp.dma_start(x_all[:, b * TB:(b + 1) * TB, :],
                                 a["x"][b].rearrange("(p t) d -> p t d", t=TB)).then_inc(x_in, 16)
                    if b == 0:
                        sp.dma_start(wmod[:], a["wmod"].rearrange("(c p) n -> p c n", p=P)).then_inc(wmod_in, 16)
                sp.wait_ge(x_in, 16 * B)

            @block.gpsimd
            def _(pool):
                pc = Chain(pool, pool_s)
                pc.link(nc.gpsimd.memset(ident[:], 0.0))
                nc.gpsimd.affine_select(out=ident[:], in_=ident[:], compare_op=ALU.not_equal, fill=1.0,
                                        base=0, pattern=[[-1, P]], channel_multiplier=1).then_inc(id_made, 1)
                for e in range(E):
                    nc.gpsimd.memset(iota8[:, e:e + 1], float(e))
                nc.gpsimd.memset(ones2[:], 1.0)
                pc.link(nc.gpsimd.memset(u0[:], 0.0))
                pool.dma_start(rwraw[:], a["router_w"].rearrange("(c p) e -> p c e", p=P)).then_inc(rw_in, 16)
                pool.dma_start(rbraw[:], a["router_b"].partition_broadcast(P)).then_inc(rw_in, 16)
                pool.dma_start(upb_bc[:], a["up_b"].partition_broadcast(P)).then_inc(rows_in, 16)
                pool.dma_start(coreb_bc[:], a["core_b"].partition_broadcast(P)).then_inc(rows_in, 16)

            @block.scalar
            def _(act):
                act.dma_start(cT[:, 0, :], a["c"][:, 0:P].rearrange("b p -> p b"),
                              allow_slow_non_contiguous=True).then_inc(c_in, 16)
                act.dma_start(cT[:, 1, :], a["c"][:, P:D].rearrange("b p -> p b"),
                              allow_slow_non_contiguous=True).then_inc(c_in, 16)
                act.dma_start(bqc[:, 0:DC, :], a["b_qkv"][0:D].rearrange("(c p o) -> p c o", p=P, o=1),
                              allow_slow_non_contiguous=True).then_inc(cols_in, 16)
                act.dma_start(bvc[:], a["b_qkv"][2 * D:3 * D].rearrange("(c p o) -> p c o", p=P, o=1),
                              allow_slow_non_contiguous=True).then_inc(cols_in, 16)
                act.dma_start(bo_bc[:], a["b_out"].partition_broadcast(P)).then_inc(cols_in, 16)
                act.dma_start(b1c[:, 0:1], a["shared_b1"].rearrange("(p n) -> p n", n=1)).then_inc(b1_in, 16)
                act.dma_start(b2c[:, 0:1], a["shared_b2"].rearrange("(p n) -> p n", n=1)).then_inc(b1_in, 16)
                act.dma_start(downbc[:], a["down_b"].rearrange("(p n) -> p n", n=1)).then_inc(b1_in, 16)
                for e in range(E):
                    n, u = HID[e] // P, FIRST_UNIT[e + 1]
                    act.dma_start(b1c[:, u:u + n], a[f"e{e}_b1"].rearrange("(p n) -> p n", n=n)).then_inc(b1_in, 16)
                    act.dma_start(b2c[:, e + 1:e + 2], a[f"e{e}_b2"].rearrange("(p n) -> p n", n=1)).then_inc(b1_in, 16)
                act.wait_ge(c_in, 32)
                nc.scalar.activation(sig[:], cT[:], ACT.Exp, scale=-1.0).then_inc(sig_made, 1)
                act.wait_ge(b1_in, 16 * (3 + 2 * E))
                nc.scalar.activation(a0c[:], b1c[:], ACT.Gelu).then_inc(a0_made, 1)

            @block.vector
            def _(dve):
                dc = Chain(dve, dve_s)
                v = nc.vector
                dve.wait_ge(sig_made, 1)
                dc.link(v.tensor_scalar(sig[:], sig[:], 1.0, None, ALU.add))
                dc.link(v.reciprocal(sig[:], sig[:]))
                v.tensor_tensor(scT[:], cT[:], sig[:], ALU.mult).then_inc(scT_made, 1)
                dve.wait_ge(scT_made, 1)
                for k in range(DC):
                    v.tensor_copy(scb[:, k, :, :], scT[:, k, :].unsqueeze(2).to_broadcast([P, B, P])).then_inc(scb_made, 1)
                dve.wait_ge(cols_in, 48)
                v.tensor_copy(bvb[:], bvc[:].to_broadcast([P, DC, P])).then_inc(scb_made, 1)
                dve.wait_ge(rw_in, 32)
                dc.link(v.memset(rwp[:].bitcast(fp32), 0.0))
                dc.link(v.memset(rwh[:].bitcast(fp32), 0.0))
                v.tensor_copy(rwh[:, :, 0:E], rwraw[:])
                dc.link(v.tensor_copy(rwp[:, :, 0:E], rwraw[:]))
                dc.link(v.tensor_tensor(rwp[:, :, E:2 * E], rwraw[:], rwh[:, :, 0:E].bitcast(fp32), ALU.subtract))
                for e, h in enumerate(HID):
                    v.tensor_scalar(rb_bc[:, e:e + 1], rbraw[:, e:e + 1], -COST_LAMBDA * (2 * L * h), None, ALU.add)
                for k in range(DC):
                    dve.wait_ge(wo_turned, k + 1)
                    v.tensor_copy(woT[:, k, :], bank[k][:, 0:D]).then_inc(woT_made, 1)
                for n, (full, hi, lo) in enumerate(((afull, Ah, Al), (mfull, Mh, Ml))):
                    for k in range(DC):
                        dve.wait_ge(fold_ps, n * DC + k + 1)
                        dc.link(v.tensor_copy(full[:, k, :], bank[2 + n * DC + k][:, 0:D]))
                        dc.link(v.tensor_copy(hi[:, k, :], full[:, k, :]))
                        v.tensor_tensor(lo[:, k, :], full[:, k, :], hi[:, k, :].bitcast(fp32), ALU.subtract).then_inc(fold_made, 1)
                dve.wait_ge(bias_ps, 1)
                v.tensor_copy(bqk[:], bank[6][:, 0:2 * DC:2])
                dve.wait_ge(brow_ps, 1)
                dc.link(v.tensor_tensor(t2[:], bank[7][:, 0:D], bo_bc[:], ALU.add))
                dve.wait_ge(mod_ps, 1)
                for w in range(4):
                    for k in range(DC):
                        src = bank[0][:, (w * DC + k) * B:(w * DC + k + 1) * B]
                        v.tensor_scalar(modc[:, :, w, k], src, 1.0 if w % 2 else 0.0, None, ALU.add)
                for b in range(B):
                    for n, (g, gx, bias) in enumerate(((ga_bc, gab_bc, t2), (gb_bc, gbias_bc, t1))):
                        dve.wait_ge(g_ps, b * 2 + n + 1)
                        src = bank[1 + (b * 2 + n) % 2][:, 0:D]
                        if b == 0 and n == 1:
                            dve.wait_ge(rows_in, 32)
                            dc.link(v.tensor_tensor(t1[:], upb_bc[:], coreb_bc[:], ALU.add))
                        dc.link(v.tensor_scalar(g[:, b, :], src, -1.0, 0.25, ALU.mult, ALU.max))
                        dc.link(v.tensor_tensor(g[:, b, :], src, g[:, b, :], ALU.max))
                        dc.link(v.tensor_scalar(gx[:, b, :], src, 0.0, 2.0, ALU.is_ge, ALU.mult))
                        dc.link(v.tensor_scalar(gx[:, b, :], gx[:, b, :], -1.0, None, ALU.add))
                        dc.link(v.tensor_tensor(g[:, b, :], g[:, b, :], gx[:, b, :], ALU.mult))
                        v.tensor_tensor(gx[:, b, :], g[:, b, :], bias[:], ALU.mult).then_inc(g_used, 1)
                dve.wait_ge(g_used, 2 * B)

            @block.tensor
            def _(pe):
                pe.wait_ge(id_made, 1)
                pe.wait_ge(wq_in, 32)
                for oc in range(DC):
                    for jc in range(DC):
                        last = nc.tensor.transpose(bank[oc][:, jc * P:(jc + 1) * P],
                                                   wout[:, jc, oc * P:(oc + 1) * P], ident[:])
                    last.then_inc(wo_turned, 1)
                for k in range(DC):
                    for o in range(DC):
                        last = nc.tensor.matmul(bank[2 + k][:, 0:D], wqkv[:, o, k * P:(k + 1) * P],
                                                wqkv[:, DC + o, :], start=(o == 0), stop=(o == DC - 1))
                    last.then_inc(fold_ps, 1)
                pe.wait_ge(woT_made, DC)
                for k in range(DC):
                    for o in range(DC):
                        last = nc.tensor.matmul(bank[4 + k][:, 0:D], wqkv[:, 2 * DC + o, k * P:(k + 1) * P],
                                                woT[:, o, :], start=(o == 0), stop=(o == DC - 1))
                    last.then_inc(fold_ps, 1)
                pe.wait_ge(cols_in, 48)
                for k in range(DC):
                    for o in range(DC):
                        last = nc.tensor.matmul(bank[6][:, 2 * k:2 * k + 1], wqkv[:, DC + o, k * P:(k + 1) * P],
                                                bqc[:, o, :], start=(o == 0), stop=(o == DC - 1))
                last.then_inc(bias_ps, 1)
                pe.wait_ge(scb_made, DC + 1)
                for o in range(DC):
                    last = nc.tensor.matmul(bank[7][:, 0:D], bvb[:, o, :], woT[:, o, :], start=(o == 0), stop=(o == DC - 1))
                last.then_inc(brow_ps, 1)
                pe.wait_ge(wmod_in, 16)
                for w, seg in enumerate((0, 1, 3, 4)):
                    for k in range(DC):
                        for o in range(DC):
                            last = nc.tensor.matmul(bank[0][:, (w * DC + k) * B:(w * DC + k + 1) * B],
                                                    wmod[:, o, seg * D + k * P:seg * D + (k + 1) * P],
                                                    scT[:, o, :], start=(o == 0), stop=(o == DC - 1))
                last.then_inc(mod_ps, 1)
                pe.wait_ge(fold_made, 2)
                for b in range(B):
                    for n, seg in enumerate((2, 5)):
                        if b:
                            pe.wait_ge(g_used, (b - 1) * 2 + n + 1)
                        for o in range(DC):
                            last = nc.tensor.matmul(bank[1 + n][:, 0:D], scb[:, o, b, :],
                                                    wmod[:, o, seg * D:(seg + 1) * D], start=(o == 0), stop=(o == DC - 1))
                        last.then_inc(g_ps, 1)
        sps.close()
        setup.close()

        attention(nc, a, ctx, attn, locals())
        attn.close()
        experts(nc, a, out, ctx, locals())


def attention(nc, a, ctx, attn, T):
    def sbt(name, shape, dt=fp32):
        return attn.enter_context(nc.sbuf_tensor(name, shape, dt))

    def sems(*names):
        return [ctx.enter_context(nc.semaphore(n)) for n in names]

    x_all, ident = T["x_all"], T["ident"]
    hf_dram, gates_dram = T["hf_dram"], T["gates_dram"]
    w1h, w1l, w2h, w2l = T["w1h"], T["w1l"], T["w2h"], T["w2l"]
    modc, a0c, u0 = T["modc"], T["a0c"], T["u0"]

    hfull = sbt("hfull", [P, DC, S])
    hTh = sbt("hTh", [P, DC, S], fp32r)
    hTl = sbt("hTl", [P, DC, S], fp32r)
    qh = sbt("qh", [P, DC, S], fp32r)
    ql = sbt("ql", [P, DC, S], fp32r)
    vh = sbt("vh", [P, TB, D], fp32r)
    vl = sbt("vl", [P, TB, D], fp32r)
    prob = sbt("prob", [P, 2, S])
    xhat = prob[:].rearrange("p a (t d) -> p (a t) d", d=D)
    pTh = sbt("pTh", [P, TB, P], fp32r)
    pTl = sbt("pTl", [P, TB, P], fp32r)
    stat = sbt("stat", [P, TB, 6])
    mv = sbt("mv", [P, TB, 2])
    ve = sbt("ve", [P, TB])
    lnv = sbt("lnv", [P, TB])
    y0 = sbt("y0", [P, TB])
    nt = sbt("nt", [P, TB])
    rstd = sbt("rstd", [P, TB])
    nmr = sbt("nmr", [P, TB])
    cur = sbt("cur", [P, 4, DC])
    mx = sbt("mx", [P, TB])
    negm = sbt("negm", [P, TB])
    rsum = sbt("rsum", [P, TB])
    rinv = sbt("rinv", [P, TB])
    ot = sbt("ot", [P, D])
    lg = sbt("lg", [2 * E, S])
    lt = sbt("lt", [P, TB, 2 * E])
    lo8 = sbt("lo8", [P, TB, E])
    m8 = sbt("m8", [P, TB, E])
    ix = sbt("ix", [P, TB, E], u32)
    ixf = sbt("ixf", [P, TB, 2])
    e8 = sbt("e8", [P, TB, E])
    ssum = sbt("ssum", [P, TB])
    dp = sbt("dp", [P, TB])
    g0 = sbt("g0", [P, TB])
    g1 = sbt("g1", [P, TB])
    k0 = sbt("k0", [P, TB, E])
    k1 = sbt("k1", [P, TB, E])
    gt = sbt("gt", [E, S])
    stage = sbt("stage", [P, 2, 512])
    wtmp = sbt("wtmp", [P, P])

    psc = ExitStack()
    sc = psc.enter_context(nc.psum_tensor("sc", [P, 2, S], fp32))
    ptp = psc.enter_context(nc.psum_tensor("ptp", [P, S], fp32))
    ob = psc.enter_context(nc.psum_tensor("ob", [P, 512], fp32))
    xb = psc.enter_context(nc.psum_tensor("xb", [P, 512], fp32))
    quad = [sc[:, n // 2, (n % 2) * CH:(n % 2 + 1) * CH] for n in range(4)]
    vbank = [ptp[:, 0:512], ptp[:, 512:1024], ob[:], xb[:]]

    w_in = sems("w_in0", "w_in1")
    (w_split, d_s, a_s, var_ready, y0_ready, xhat_ready, turned, hfull_ready, ht_ready,
     q_ps, qh_ready, ql_ready, v_ps, vh_ready, vl_ready, sc_ready, negm_ready, p_ready, pt_ready,
     pth_ready, ptl_ready, pv_ready, x1_ready, lg_ps, lg_ready, lt_ready, d_ready, e_ready, gates_ready,
     gt_ps, gt_ready, stored, p_s, w_taken, idle) = sems(
        "w_split", "d_s", "a_s", "var_ready", "y0_ready", "xhat_ready", "turned", "hfull_ready",
        "ht_ready", "q_ps", "qh_ready", "ql_ready", "v_ps", "vh_ready", "vl_ready", "sc_ready", "negm_ready",
        "p_ready", "pt_ready", "pth_ready", "ptl_ready", "pv_ready", "x1_ready", "lg_ps", "lg_ready",
        "lt_ready", "d_ready", "e_ready", "gates_ready", "gt_ps", "gt_ready", "stored", "p_s", "w_taken", "idle")

    pieces = []
    for e in range(E):
        n, u = HID[e] // P, FIRST_UNIT[e + 1]
        pieces.append((a[f"e{e}_w1"].rearrange("l (q n) -> l q n", n=n), (P, n), "q n -> n q",
                       w1h[:, u:u + n, :], w1l[:, u:u + n, :], 1.0, None))
        pieces.append((a[f"e{e}_w2"].rearrange("(p n) l -> p n l", n=n), (n, L), None,
                       w2h[:, u:u + n, :], w2l[:, u:u + n, :], 1.0, e))
    pieces.append((a["shared_w1"].rearrange("l (n q) -> l n q", n=1), (1, P), None, w1h[:, 0:1, :], w1l[:, 0:1, :], 1.0, None))
    pieces.append((a["shared_w2"].rearrange("(p n) l -> p n l", n=1), (1, L), None, w2h[:, 0:1, :], w2l[:, 0:1, :], 0.1, None))
    pieces.append((a["down_w"].rearrange("(c p) l -> p c l", p=P), (DC, L), None, T["downh"][:], T["downl"][:], 1.0, None))
    pieces.append((a["up_w"].rearrange("p (n l) -> p n l", n=1), (1, D), None, T["uph"][:].unsqueeze(1), T["upl"][:].unsqueeze(1), 1.0, None))
    pieces.append((a["core_w"].rearrange("(c p) n -> p c n", p=P), (DC, D), None, T["coreh"][:], T["corel"][:], 1.0, None))

    def staged(k):
        s0, s1 = pieces[k][1]
        return stage[:, k % 2, 0:s0 * s1].rearrange("p (x y) -> p x y", x=s0)

    with nc.Block() as block:
        @block.sync
        def _(sp):
            for k, piece in enumerate(pieces):
                if k >= 2:
                    sp.wait_ge(w_taken, k - 1)
                sp.dma_start(staged(k), piece[0]).then_inc(w_in[k % 2], 16)

        @block.gpsimd
        def _(pool):
            g = nc.gpsimd
            pc = Chain(pool, p_s)
            for k, (src, shape, turn, hi, lo, scale, expert) in enumerate(pieces):
                pool.wait_ge(w_in[k % 2], 16 * (k // 2 + 1))
                raw = staged(k)
                if turn:
                    raw = raw.rearrange("p q n -> p n q")
                if scale != 1.0:
                    pc.link(g.tensor_scalar(wtmp[:].unsqueeze(1), raw, scale, 0.0, ALU.mult, ALU.add))
                    raw = wtmp[:].unsqueeze(1)
                pc.link(g.tensor_scalar(hi, raw, 1.0, 0.0, ALU.mult, ALU.add))
                pc.link(g.tensor_tensor(lo, raw, hi.bitcast(fp32), ALU.subtract))
                if expert is not None:
                    for j in range(shape[0]):
                        u = FIRST_UNIT[expert + 1] + j
                        pc.link(g.tensor_scalar(wtmp[:], raw[:, j, :], a0c[:, u:u + 1], 0.0, ALU.mult, ALU.add))
                        pc.link(g.tensor_tensor(u0[:, expert, :], u0[:, expert, :], wtmp[:], ALU.add))
                pool.sem_inc(w_taken, 1)

        @block.vector
        def _(dve):
            v = nc.vector
            LINKS = DVE_LINKS
            with dve.Fori(0, B) as b:
                dc = Chain(dve, d_s, b * LINKS)

                def normalise(s, last):
                    dc.hold(last, idle)
                    for t in range(TB):
                        last = v.bn_aggr(mv[:, t, :], stat[:, t, :])
                    dc.link(last)
                    v.tensor_scalar(ve[:], mv[:, :, 1], LN_EPS, None, ALU.add).then_inc(var_ready, 1)
                    dve.wait_ge(y0_ready, b * 2 + s + 1)
                    dc.link(v.tensor_tensor(nt[:], y0[:], y0[:], ALU.mult))
                    dc.link(v.tensor_tensor(nt[:], nt[:], ve[:], ALU.mult))
                    dc.link(v.tensor_scalar(nt[:], nt[:], -0.5, 1.5, ALU.mult, ALU.add))
                    dc.link(v.tensor_tensor(rstd[:], y0[:], nt[:], ALU.mult))
                    dc.link(v.scalar_tensor_tensor(nmr[:], mv[:, :, 0], -1.0, rstd[:], ALU.mult, ALU.mult))
                    for t in range(TB):
                        v.tensor_scalar(xhat[:, t, :], x_all[:, bass.ds(b * TB + t, 1), :].rearrange("p a d -> p (a d)"),
                                        rstd[:, t:t + 1], nmr[:, t:t + 1], ALU.mult, ALU.add).then_inc(xhat_ready, 1)

                def split_ht(s):
                    for n in range(4):
                        half, c = n // 2, n % 2
                        cols = slice(half * CH, (half + 1) * CH)
                        dve.wait_ge(hfull_ready, (b * 2 + s) * 4 + n + 1)
                        dc.link(v.tensor_copy(hTh[:, c, cols], hfull[:, c, cols]))
                        v.tensor_tensor(hTl[:, c, cols], hfull[:, c, cols], hTh[:, c, cols].bitcast(fp32),
                                        ALU.subtract).then_inc(ht_ready, 1)

                dc.link(v.tensor_copy(cur[:].unsqueeze(1), modc[:, bass.ds(b, 1), :, :]))
                for t in range(TB):
                    last = v.bn_stats(stat[:, t, :], x_all[:, bass.ds(b * TB + t, 1), :].rearrange("p a d -> p (a d)"))
                normalise(0, last)
                dve.wait_ge(xhat_ready, b * 2 * TB + TB)
                dc.link(v.tensor_tensor(x_all[:, bass.ds(b * TB, TB), :], x_all[:, bass.ds(b * TB, TB), :],
                                        T["gab_bc"][:, bass.ds(b, 1), :].to_broadcast([P, TB, D]), ALU.add))
                split_ht(0)
                for n in range(4):
                    half, c = n // 2, n % 2
                    cols = slice(half * CH, (half + 1) * CH)
                    dve.wait_ge(qh_ready, b * 4 + n + 1)
                    v.scalar_tensor_tensor(ql[:, c, cols], quad[n], T["bqk"][:, c:c + 1], qh[:, c, cols].bitcast(fp32),
                                           ALU.add, ALU.subtract).then_inc(ql_ready, 1)
                for n in range(4):
                    dve.wait_ge(vh_ready, b * 4 + n + 1)
                    pair = slice(2 * n, 2 * n + 2)
                    v.tensor_tensor(vl[:, pair, :].rearrange("p t d -> p (t d)"), vbank[n],
                                    vh[:, pair, :].rearrange("p t d -> p (t d)").bitcast(fp32),
                                    ALU.subtract).then_inc(vl_ready, 1)

                def row_max(t):
                    dve.wait_ge(sc_ready, b * TB + t + 1)
                    dc.link(v.reduce_max(mx[:, t:t + 1], sc[:, t % 2, :], AX))
                    v.tensor_scalar(negm[:, t:t + 1], mx[:, t:t + 1], -SCORE_SCALE, None, ALU.mult).then_inc(negm_ready, 1)

                def residual(t):
                    dve.wait_ge(pv_ready, b * TB + t + 1)
                    dc.link(v.reciprocal(rinv[:, t:t + 1], rsum[:, t:t + 1]))
                    dc.link(v.scalar_tensor_tensor(ot[:], (ob, xb)[t % 2][:, 0:D], rinv[:, t:t + 1],
                                                   T["ga_bc"][:, bass.ds(b, 1), :].rearrange("p a d -> p (a d)"),
                                                   ALU.mult, ALU.mult))
                    row = x_all[:, bass.ds(b * TB + t, 1), :].rearrange("p a d -> p (a d)")
                    v.tensor_tensor(row, ot[:], row, ALU.add).then_inc(x1_ready, 1)
                    hold(dve, x1_ready, b * TB + t + 1, idle)
                    return v.bn_stats(stat[:, t, :], row)

                row_max(0)
                row_max(1)
                for t in range(TB):
                    dve.wait_ge(pth_ready, b * TB + t + 1)
                    v.tensor_tensor(pTl[:].rearrange("p t q -> p (t q)"), ptp[:],
                                    pTh[:].rearrange("p t q -> p (t q)").bitcast(fp32), ALU.subtract).then_inc(ptl_ready, 1)
                    if t + 2 < TB:
                        row_max(t + 2)
                    if t:
                        residual(t - 1)
                normalise(1, residual(TB - 1))
                split_ht(1)

                dve.wait_ge(lt_ready, b + 1)
                dc.link(v.tensor_copy(lt[:].rearrange("p t e -> p (t e)"), ptp[:, 0:TB * 2 * E]))
                dc.link(v.tensor_tensor(lo8[:], lt[:, :, 0:E], lt[:, :, E:2 * E], ALU.add))
                dc.hold(v.tensor_tensor(lo8[:], lo8[:], T["rb_bc"][:].unsqueeze(1).to_broadcast([P, TB, E]), ALU.add), idle)
                for t in range(TB):
                    last = v.max(m8[:, t, :], lo8[:, t, :])
                dc.link(last)
                v.tensor_tensor(k0[:], m8[:], m8[:, :, 0:1].to_broadcast([P, TB, E]), ALU.subtract).then_inc(d_ready, 1)
                for t in range(TB):
                    last = v.max_index(ix[:, t, :], m8[:, t, :], lo8[:, t, :])
                dc.link(last)
                dc.link(v.tensor_copy(ixf[:], ix[:, :, 0:2]))
                dve.wait_ge(e_ready, b * 2 + 1)
                dc.link(v.reduce_sum(ssum[:], e8[:], AX))
                dc.link(v.reciprocal(ssum[:], ssum[:]))
                dc.link(v.tensor_tensor(dp[:], e8[:, :, 1], e8[:, :, 0], ALU.subtract))
                v.tensor_tensor(dp[:], dp[:], ssum[:], ALU.mult).then_inc(d_ready, 1)
                iota = T["iota8"][:].unsqueeze(1).to_broadcast([P, TB, E])
                v.tensor_tensor(k0[:], iota, ixf[:, :, 0:1].to_broadcast([P, TB, E]), ALU.is_equal)
                dc.link(v.tensor_tensor(k1[:], iota, ixf[:, :, 1:2].to_broadcast([P, TB, E]), ALU.is_equal))
                dve.wait_ge(e_ready, b * 2 + 2)
                dc.link(v.tensor_scalar(g0[:], g1[:], 1.0, None, ALU.add))
                dc.link(v.reciprocal(g0[:], g0[:]))
                dc.link(v.tensor_tensor(g1[:], g1[:], g0[:], ALU.mult))
                v.tensor_tensor(k0[:], k0[:], g0[:].unsqueeze(2).to_broadcast([P, TB, E]), ALU.mult)
                dc.link(v.tensor_tensor(k1[:], k1[:], g1[:].unsqueeze(2).to_broadcast([P, TB, E]), ALU.mult))
                v.tensor_tensor(k0[:], k0[:], k1[:], ALU.add).then_inc(gates_ready, 1)
                dve.wait_ge(gates_ready, b + 1)
                assert dc.n == LINKS, dc.n

        @block.scalar
        def _(act):
            sa = nc.scalar.activation
            with act.Fori(0, B) as b:
                def normalise(s):
                    act.wait_ge(var_ready, b * 2 + s + 1)
                    sa(lnv[:], ve[:], ACT.Ln).then_inc(a_s, 1)
                    act.wait_ge(a_s, b * 2 + s + 1)
                    sa(y0[:], lnv[:], ACT.Exp, scale=-0.5).then_inc(y0_ready, 1)

                def modulate(s):
                    for n in range(4):
                        half, c = n // 2, n % 2
                        act.wait_ge(turned, (b * 2 + s) * 4 + n + 1)
                        sa(hfull[:, c, half * CH:(half + 1) * CH], quad[n], ACT.Identity,
                           scale=cur[:, 2 * s + 1, c:c + 1], bias=cur[:, 2 * s, c:c + 1]).then_inc(hfull_ready, 1)

                normalise(0)
                modulate(0)
                for n in range(4):
                    half, c = n // 2, n % 2
                    act.wait_ge(q_ps, b * 4 + n + 1)
                    sa(qh[:, c, half * CH:(half + 1) * CH], quad[n], ACT.Identity,
                       bias=T["bqk"][:, c:c + 1]).then_inc(qh_ready, 1)
                for n in range(4):
                    act.wait_ge(v_ps, b * 4 + n + 1)
                    sa(vh[:, 2 * n:2 * n + 2, :].rearrange("p t d -> p (t d)"), vbank[n], ACT.Copy).then_inc(vh_ready, 1)

                def softmax(t):
                    act.wait_ge(negm_ready, b * TB + t + 1)
                    if t >= 2:
                        act.wait_ge(pt_ready, b * TB + t - 1)
                    sa(prob[:, t % 2, :], sc[:, t % 2, :], ACT.Exp, bias=negm[:, t:t + 1], scale=SCORE_SCALE,
                       accum_out=rsum[:, t:t + 1]).then_inc(p_ready, 1)

                softmax(0)
                for t in range(TB):
                    act.wait_ge(pt_ready, b * TB + t + 1)
                    sa(pTh[:].rearrange("p t q -> p (t q)"), ptp[:], ACT.Copy).then_inc(pth_ready, 1)
                    if t + 1 < TB:
                        softmax(t + 1)

                normalise(1)
                modulate(1)
                act.wait_ge(hfull_ready, b * 8 + 8)
                for half in range(HB):
                    act.dma_start(hf_dram[bass.ds(b * HB + half, 1)].rearrange("a p c t -> p (a c) t"),
                                  hfull[:, :, half * CH:(half + 1) * CH]).then_inc(stored, 16)
                for half in range(HB):
                    act.wait_ge(lg_ps, b * HB + half + 1)
                    sa(lg[:, half * CH:(half + 1) * CH], (xb, ob)[half][0:2 * E, :], ACT.Copy).then_inc(lg_ready, 1)
                act.wait_ge(d_ready, b * 2 + 1)
                sa(e8[:], k0[:], ACT.Exp).then_inc(e_ready, 1)
                act.wait_ge(d_ready, b * 2 + 2)
                sa(g1[:], dp[:], ACT.Exp).then_inc(e_ready, 1)
                act.wait_ge(gt_ps, b + 1)
                sa(gt[:], ptp[0:E, :], ACT.Copy).then_inc(gt_ready, 1)
                act.wait_ge(gt_ready, b + 1)
                act.dma_start(gates_dram[bass.ds(b * HB, HB)].rearrange("h e t -> e h t"),
                              gt[:].rearrange("e (h t) -> e h t", h=HB)).then_inc(stored, 16)
                act.wait_ge(stored, (b + 1) * 16 * (HB + 1))

        @block.tensor
        def _(pe):
            with pe.Fori(0, B) as b:
                def turn(s):
                    for n in range(4):
                        half, c = n // 2, n % 2
                        if c == 0:
                            pe.wait_ge(xhat_ready, (b * 2 + s) * TB + (half + 1) * TC)
                        for t in range(TC):
                            last = nc.tensor.transpose(quad[n][:, t * P:(t + 1) * P],
                                                       xhat[:, half * TC + t, c * P:(c + 1) * P], ident[:])
                        last.then_inc(turned, 1)

                def ht(c, cols):
                    return hTh[:, c, cols], hTl[:, c, cols]

                turn(0)
                for n in range(4):
                    half, c = n // 2, n % 2
                    pe.wait_ge(ht_ready, b * 8 + 2 * half + 2)
                    for k in range(DC):
                        last = matmul3(nc, quad[n], (T["Ah"][:, k, c * P:(c + 1) * P], T["Al"][:, k, c * P:(c + 1) * P]),
                                       ht(k, slice(half * CH, (half + 1) * CH)), k == 0, k == DC - 1)
                    last.then_inc(q_ps, 1)
                for n in range(4):
                    for j in range(2):
                        t = 2 * n + j
                        for k in range(DC):
                            last = matmul3(nc, vbank[n][:, j * D:(j + 1) * D], ht(k, slice(t * P, (t + 1) * P)),
                                           (T["Mh"][:, k, :], T["Ml"][:, k, :]), k == 0, k == DC - 1)
                    last.then_inc(v_ps, 1)

                def scores(t):
                    if t >= 2:
                        pe.wait_ge(p_ready, b * TB + t - 1)
                    for half in range(HB):
                        for k in range(DC):
                            cols = slice(t * P, (t + 1) * P)
                            last = matmul3(nc, sc[:, t % 2, half * CH:(half + 1) * CH], (qh[:, k, cols], ql[:, k, cols]),
                                           ht(k, slice(half * CH, (half + 1) * CH)), k == 0, k == DC - 1)
                    last.then_inc(sc_ready, 1)

                pe.wait_ge(ql_ready, b * 4 + 4)
                scores(0)
                scores(1)
                for t in range(TB):
                    pe.wait_ge(p_ready, b * TB + t + 1)
                    if t == 0:
                        pe.wait_ge(vl_ready, b * 4 + 4)
                    else:
                        pe.wait_ge(ptl_ready, b * TB + t)
                    for k in range(TB):
                        last = nc.tensor.transpose(ptp[:, k * P:(k + 1) * P], prob[:, t % 2, k * P:(k + 1) * P], ident[:])
                    last.then_inc(pt_ready, 1)
                    if t + 2 < TB:
                        scores(t + 2)
                    pe.wait_ge(ptl_ready, b * TB + t + 1)
                    if t >= 2:
                        pe.wait_ge(x1_ready, b * TB + t - 1)
                    for k in range(TB):
                        last = matmul3(nc, (ob, xb)[t % 2][:, 0:D], (pTh[:, k, :], pTl[:, k, :]),
                                       (vh[:, k, :], vl[:, k, :]), k == 0, k == TB - 1)
                    last.then_inc(pv_ready, 1)

                turn(1)
                for half in range(HB):
                    pe.wait_ge(ht_ready, b * 8 + 4 + 2 * half + 2)
                    dst = (xb, ob)[half]
                    for k in range(DC):
                        h, l = ht(k, slice(half * CH, (half + 1) * CH))
                        nc.tensor.matmul(dst[:], T["rwp"][:, k, :], h, start=(k == 0), stop=False)
                        last = nc.tensor.matmul(dst[:], T["rwh"][:, k, :], l, start=False, stop=(k == DC - 1))
                    last.then_inc(lg_ps, 1)
                for t in range(TB):
                    if t % TC == 0:
                        hold(pe, lg_ready, b * HB + t // TC + 1, idle)
                    last = nc.tensor.transpose(ptp[:, t * 2 * E:(t + 1) * 2 * E], lg[:, t * P:(t + 1) * P],
                                               ident[0:2 * E, 0:2 * E])
                last.then_inc(lt_ready, 1)
                pe.wait_ge(gates_ready, b + 1)
                for t in range(TB):
                    last = nc.tensor.transpose(ptp[0:E, t * P:(t + 1) * P], k0[:, t, :], ident[:])
                last.then_inc(gt_ps, 1)
    psc.close()


def experts(nc, a, out, ctx, T):
    def sbt(name, shape, dt=fp32):
        return ctx.enter_context(nc.sbuf_tensor(name, shape, dt))

    def sems(*names):
        return [ctx.enter_context(nc.semaphore(n)) for n in names]

    x_all, b1c, b2c = T["x_all"], T["b1c"], T["b2c"]
    w1h, w1l, w2h, w2l = T["w1h"], T["w1l"], T["w2h"], T["w2l"]
    NA = 4
    hin = sbt("hin", [P, 2, DC, CH])
    hh = sbt("hh", [P, DC, CH], fp32r)
    hl = sbt("hl", [P, DC, CH], fp32r)
    gf = sbt("gf", [P, CH])
    gh = sbt("gh", [P, 2, CH], fp32r)
    gl = sbt("gl", [P, 2, CH], fp32r)
    gxf = sbt("gxf", [P, DC, CH])
    gxh = sbt("gxh", [P, DC, CH], fp32r)
    gxl = sbt("gxl", [P, DC, CH], fp32r)
    af = sbt("af", [P, NA, CH])
    ah = sbt("ah", [P, NA, CH], fp32r)
    al = sbt("al", [P, NA, CH], fp32r)
    gbc = sbt("gbc", [P, E, CH])
    y = sbt("y", [P, CH])
    yh = sbt("yh", [P, CH], fp32r)
    yl = sbt("yl", [P, CH], fp32r)
    te = sbt("te", [P, 2, CH])
    od = sbt("od", [P, TC, D])
    negc = sbt("negc", [P, E])
    csum = sbt("csum", [P, 1])
    cb = sbt("cb", [P, GROUPS])
    call = sbt("call", [P, 1])

    psc = ExitStack()
    pre = psc.enter_context(nc.psum_tensor("pre", [P, 4, CH], fp32))
    acc = psc.enter_context(nc.psum_tensor("acc", [P, 2, CH], fp32))
    dn = psc.enter_context(nc.psum_tensor("dn", [P, CH], fp32))

    (h_in, h_split, dn_ps, gf_ready, g_ready, gxf_ready, gx_ready, pre_ps, af_ready, al_ready, a_used,
     te_ready, y_ready, yl_ready, gates_in, out_ps, od_ready, xr_ready, of_ready, sent, d2_s, c_ps,
     c_made, gx_used) = sems(
        "h_in", "h_split", "dn_ps", "gf_ready", "g_ready", "gxf_ready", "gx_ready", "pre_ps", "af_ready",
        "al_ready", "a_used", "te_ready", "y_ready", "yl_ready", "gates_in", "out_ps", "od_ready",
        "xr_ready", "of_ready", "sent", "d2_s", "c_ps", "c_made", "gx_used")

    LATE = 3

    with nc.Block() as block:
        def chunks(eng, body):
            with eng.Fori(0, B - 1) as b:
                for half in range(HB):
                    body(b, half, True)
            for half in range(HB):
                body(B - 1, half, half < HB - 1)

        def nth(b, half):
            return b * HB + half

        @block.sync
        def _(sp):
            sp.dma_start(hin[:, 0], hf_dram_at(T, 0, 0)).then_inc(h_in, 16)
            for e in range(E):
                sp.dma_start(gbc[:, e, :], gates_at(T, 0, 0, e)).then_inc(gates_in, 16)

            def body(b, half, more):
                i = nth(b, half)
                if more:
                    nb, nhalf = (b, half + 1) if half + 1 < HB else (b + 1, 0)
                    sp.wait_ge(gxf_ready, i * DC + 1)
                    sp.dma_start(hin[:, nhalf], hf_dram_at(T, nb, nhalf)).then_inc(h_in, 16)
                    for e in range(E):
                        sp.wait_ge(te_ready, i * E + e + 1)
                        sp.dma_start(gbc[:, e, :], gates_at(T, nb, nhalf, e)).then_inc(gates_in, 16)
                sp.wait_ge(of_ready, i + 1)
                sp.dma_start(out_at(out, b, half), od[:]).then_inc(sent, 16)

            chunks(sp, body)
            sp.wait_ge(sent, 16 * NCH)

        @block.scalar
        def _(act):
            sa = nc.scalar.activation

            def down_gelu(i, slot):
                act.wait_ge(dn_ps, i + 1)
                sa(gf[:], dn[:], ACT.Gelu, bias=T["downbc"][:]).then_inc(gf_ready, 1)

            act.wait_ge(dn_ps, 1)
            sa(gf[:], dn[:], ACT.Gelu, bias=T["downbc"][:]).then_inc(gf_ready, 1)

            def body(b, half, more):
                i = nth(b, half)
                for u in range(NU):
                    s = u % NA
                    act.wait_ge(pre_ps, i * NU + u + 1)
                    if u >= NA:
                        act.wait_ge(a_used, i * NU + u - NA + 1)
                    sa(af[:, s, :], pre[:, s, :], ACT.Gelu, bias=b1c[:, u:u + 1])
                    sa(ah[:, s, :], pre[:, s, :], ACT.Gelu, bias=b1c[:, u:u + 1]).then_inc(af_ready, 1)
                    if u in (1, 2):
                        if u == 1:
                            act.wait_ge(h_in, i * 16 + 16)
                        sa(gxf[:, u - 1, :], hin[:, half, u - 1, :], ACT.Gelu).then_inc(gxf_ready, 1)
                    if u == NU - 1 and more:
                        act.wait_ge(dn_ps, i + 2)
                        act.wait_ge(g_ready, i + 1)
                        sa(gf[:], dn[:], ACT.Gelu, bias=T["downbc"][:]).then_inc(gf_ready, 1)

            chunks(act, body)

        @block.vector
        def _(dve):
            v = nc.vector

            def split(hi, lo, full, n, sem, dc):
                dc.link(v.tensor_copy(hi, full))
                v.tensor_tensor(lo, full, hi.bitcast(fp32), ALU.subtract).then_inc(sem, n)

            dc = Chain(dve, d2_s)
            dve.wait_ge(h_in, 16)
            split(hh[:], hl[:], hin[:, 0], 1, h_split, dc)
            dve.wait_ge(c_ps, 1)
            cps = acc[:, 0, 0:2 * E].rearrange("p (e two) -> p e two", two=2)[:, :, 0]
            v.tensor_scalar(negc[:], cps, -1.0, None, ALU.mult)
            v.tensor_scalar(cb[:, 0:1], b2c[:, 0:1], 0.1, None, ALU.mult)
            dc.link(v.tensor_tensor(cb[:, 1:], cps, b2c[:, 1:], ALU.add))
            v.reduce_sum(call[:], cb[:], AX).then_inc(c_made, 1)
            dve.wait_ge(c_made, 1)
            dve.wait_ge(gf_ready, 1)
            split(gh[:, 0, :], gl[:, 0, :], gf[:], 1, g_ready, dc)
            n0 = dc.n

            def body(b, half, more):
                i = nth(b, half)
                PER = DVE_LINKS_B
                dc = Chain(dve, d2_s, i * PER + n0)

                def group(g):
                    dve.wait_ge(a_used, i * NU + LAST_UNIT[g] + 1)
                    if g == 0:
                        v.tensor_scalar(y[:], acc[:, (g % 2), :], call[:], None, ALU.add).then_inc(y_ready, 1)
                    else:
                        e = g - 1
                        if g == 1:
                            dve.wait_ge(gates_in, (i + 1) * 16 * E)
                        if g >= 3:
                            dve.wait_ge(y_ready, i * GROUPS + g - 1)
                        v.scalar_tensor_tensor(te[:, g % 2, :], acc[:, g % 2, :], negc[:, e:e + 1], gbc[:, e, :],
                                               ALU.add, ALU.mult).then_inc(te_ready, 1)

                for u in range(NU):
                    s = u % NA
                    dve.wait_ge(af_ready, i * NU + u + 1)
                    v.tensor_tensor(al[:, s, :], af[:, s, :], ah[:, s, :].bitcast(fp32), ALU.subtract).then_inc(al_ready, 1)
                    for g in range(GROUPS):
                        if LAST_UNIT[g] + LATE == u:
                            group(g)
                    if u in (4, 5):
                        c = u - 4
                        dve.wait_ge(gxf_ready, i * DC + c + 1)
                        split(gxh[:, c, :], gxl[:, c, :], gxf[:, c, :], 1, gx_ready, dc)
                    if u in (8, 9) and more:
                        c = u - 8
                        if c == 0:
                            dve.wait_ge(h_in, (i + 2) * 16)
                        dc.link(v.tensor_copy(hh[:, c, :], hin[:, 1 - half, c, :]))
                        ins = v.tensor_tensor(hl[:, c, :], hin[:, 1 - half, c, :], hh[:, c, :].bitcast(fp32), ALU.subtract)
                        if c == DC - 1:
                            ins.then_inc(h_split, 1)
                for g in range(GROUPS):
                    if LAST_UNIT[g] + LATE >= NU:
                        group(g)
                if more:
                    dve.wait_ge(gf_ready, i + 2)
                    split(gh[:, 1 - half, :], gl[:, 1 - half, :], gf[:], 1, g_ready, dc)
                dve.wait_ge(y_ready, (i + 1) * GROUPS)
                split(yh[:], yl[:], y[:], 1, yl_ready, dc)
                dve.wait_ge(out_ps, i + 1)
                dve.wait_ge(xr_ready, i + 1)
                v.tensor_tensor(od[:], pre[:, :, 0:D], T["gb_bc"][:, bass.ds(b, 1), :].to_broadcast([P, TC, D]),
                                ALU.mult).then_inc(od_ready, 1)
                assert dc.n == PER or not more, dc.n

            chunks(dve, body)

        @block.gpsimd
        def _(pool):
            g = nc.gpsimd

            def body(b, half, more):
                i = nth(b, half)
                rows = x_all[:, bass.ds(i * TC, TC), :]
                g.tensor_tensor(rows, rows, T["gbias_bc"][:, bass.ds(b, 1), :].to_broadcast([P, TC, D]), ALU.add).then_inc(xr_ready, 1)
                for e in range(E):
                    pool.wait_ge(y_ready, i * GROUPS + e + 1)
                    pool.wait_ge(te_ready, i * E + e + 1)
                    g.tensor_tensor(y[:], y[:], te[:, (e + 1) % 2, :], ALU.add).then_inc(y_ready, 1)
                hold(pool, od_ready, i + 1, T["pool_idle"])
                g.tensor_tensor(od[:], od[:], rows, ALU.add).then_inc(of_ready, 1)
                hold(pool, sent, 16 * (i + 1), T["pool_idle"])

            chunks(pool, body)

        @block.tensor
        def _(pe):
            mm = nc.tensor.matmul

            def down():
                for k in range(DC):
                    last = matmul3(nc, dn[:], (T["downh"][:, k, :], T["downl"][:, k, :]), (hh[:, k, :], hl[:, k, :]),
                                   k == 0, k == DC - 1)
                last.then_inc(dn_ps, 1)

            for e in range(E):
                last = mm(acc[:, 0, 2 * e:2 * e + 2], T["u0"][:, e, :], T["ones2"][:], start=True, stop=True)
            last.then_inc(c_ps, 1)
            pe.wait_ge(h_split, 1)
            down()
            pe.wait_ge(c_made, 1)

            def body(b, half, more):
                i = nth(b, half)

                def second(u):
                    g, s = UNITS[u][0], u % NA
                    pe.wait_ge(al_ready, i * NU + u + 1)
                    if u == FIRST_UNIT[g] and g >= 2:
                        if g == 2:
                            pe.wait_ge(y_ready, i * GROUPS + 1)
                        else:
                            pe.wait_ge(te_ready, i * E + g - 2)
                    last = matmul3(nc, acc[:, g % 2, :], (w2h[:, u, :], w2l[:, u, :]), (ah[:, s, :], al[:, s, :]),
                                   u == FIRST_UNIT[g], u == LAST_UNIT[g])
                    last.then_inc(a_used, 1)

                pe.wait_ge(g_ready, i + 1)
                for u in range(NU):
                    if u >= 4:
                        pe.wait_ge(af_ready, i * NU + u - 3)
                    matmul3(nc, pre[:, u % 4, :], (w1h[:, u, :], w1l[:, u, :]), (gh[:, half, :], gl[:, half, :]),
                            True, True).then_inc(pre_ps, 1)
                    if u >= 2:
                        second(u - 2)
                    if u == 16 and more:
                        pe.wait_ge(h_split, i + 2)
                        down()
                second(NU - 2)
                second(NU - 1)
                pe.wait_ge(af_ready, (i + 1) * NU)
                pe.wait_ge(gx_ready, (i + 1) * DC)
                for t in range(TC):
                    cols = slice(t * P, (t + 1) * P)
                    for k in range(DC):
                        matmul3(nc, pre[:, t, 0:D], (gxh[:, k, cols], gxl[:, k, cols]),
                                (T["coreh"][:, k, :], T["corel"][:, k, :]), k == 0, False)
                pe.wait_ge(yl_ready, i + 1)
                for t in range(TC):
                    cols = slice(t * P, (t + 1) * P)
                    last = matmul3(nc, pre[:, t, 0:D], (yh[:, cols], yl[:, cols]), (T["uph"][:], T["upl"][:]), False, True)
                last.then_inc(out_ps, 1)
                if more:
                    pe.wait_ge(od_ready, i + 1)

            chunks(pe, body)
    psc.close()


def hf_dram_at(T, b, half):
    return T["hf_dram"][bass.ds(b * HB + half, 1)].rearrange("a p c t -> p (a c) t")


def gates_at(T, b, half, e):
    row = T["gates_dram"][bass.ds(b * HB + half, 1), e, :]
    return row.rearrange("a t -> (a t)").partition_broadcast(P)


def out_at(out, b, half):
    o = out.rearrange("b (p h t) d -> b h p t d", h=HB, t=TC)
    return o[bass.ds(b, 1), half].rearrange("a p t d -> p (a t) d")


DVE_LINKS = 62
DVE_LINKS_B = 6


_ARGS = {'x': 'L0_attn_hidden_states', 'w_qkv': 'L0_attn_w_qkv', 'b_qkv': 'L0_attn_b_qkv', 'w_out': 'L0_attn_w_out',
         'b_out': 'L0_attn_b_out', 'c': 'L0_c', 'wmod': 'L0_wmod'}
for _n in ('down_w', 'down_b', 'up_w', 'up_b', 'router_w', 'router_b', 'shared_w1', 'shared_b1', 'shared_w2',
           'shared_b2', 'core_w', 'core_b'):
    _ARGS[_n] = 'L0_ffn_' + _n
for _e in range(E):
    for _n in ('w1', 'b1', 'w2', 'b2'):
        _ARGS[f'e{_e}_{_n}'] = f'L0_ffn_e{_e}_{_n}'


def kernel(**inputs):
    import numpy as _np
    import concourse.bacc as _bacc
    from concourse import mybir as _mybir
    from concourse.bass_utils import run_bass_kernel_spmd as _run

    nc = _bacc.Bacc("TRN2", target_bir_lowering=False, num_devices=1)
    arrays, args = {}, {}
    for short, name in _ARGS.items():
        v = _np.ascontiguousarray(inputs[name])
        arrays[f"in_{short}_dram"] = v
        args[short] = nc.dram_tensor(f"in_{short}_dram", v.shape, _mybir.dt.from_np(v.dtype), kind="ExternalInput").ap()
    o = nc.dram_tensor("out_0_dram", (B, S, D), _mybir.dt.float32, kind="ExternalOutput").ap()
    adaln_block(nc, args, o)
    r = _run(nc, [arrays], core_ids=[0])
    return r.results[0]["out_0_dram"]
```

```python
import concourse.bass as bass
from concourse import mybir
from contextlib import ExitStack

B, S, D, L = 4, 1024, 256, 128
P = 128
DC = D // P
TB = S // P
CH = 512
HB = S // CH
NCH = B * HB
TC = CH // P
HID = [128, 256, 384, 512, 128, 256, 384, 512]
E = len(HID)
LN_EPS = 1e-5
COST_LAMBDA = 1e-7
SCORE_SCALE = 1.0 / 16.0
assert SCORE_SCALE * SCORE_SCALE * D == 1.0

UNITS = [(0, 0)] + [(e + 1, j) for e, h in enumerate(HID) for j in range(h // P)]
NU = len(UNITS)
LAST_UNIT = {g: max(u for u, (gg, _) in enumerate(UNITS) if gg == g) for g in range(E + 1)}
FIRST_UNIT = {g: min(u for u, (gg, _) in enumerate(UNITS) if gg == g) for g in range(E + 1)}
GROUPS = E + 1

fp32 = mybir.dt.float32
fp32r = mybir.dt.float32r
u32 = mybir.dt.uint32
ALU = mybir.AluOpType
ACT = mybir.ActivationFunctionType
AX = mybir.AxisListType.X


class Chain:

    def __init__(self, eng, sem, base=0):
        self.eng, self.sem, self.base, self.n = eng, sem, base, 0

    def mark(self, ins):
        self.n += 1
        ins.then_inc(self.sem, 1)
        return self.base + self.n

    def link(self, ins):
        self.eng.wait_ge(self.sem, self.mark(ins))

    def hold(self, ins, idle):
        hold(self.eng, self.sem, self.mark(ins), idle)


def hold(eng, sem, value, idle):
    eng.wait_ge(sem, value)
    eng.sem_inc(idle, 1)


def matmul3(nc, out, stat, mov, start, stop):
    (sh, sl), (mh, ml) = stat, mov
    nc.tensor.matmul(out, sh, mh, start=start, stop=False)
    nc.tensor.matmul(out, sh, ml, start=False, stop=False)
    return nc.tensor.matmul(out, sl, mh, start=False, stop=stop)


class Kept:
    pass


class Norm:

    def __init__(self, stat, mv, ve, rstd, nmr):
        self.stat, self.mv, self.ve, self.rstd, self.nmr = stat, mv, ve, rstd, nmr


def adaln_block(nc, a, out):
    ctx = ExitStack()
    attn = ExitStack()
    K = Kept()
    K.hf_dram = nc.dram_tensor("hf_dram", (NCH, P, DC, CH), fp32, kind="Internal").ap()
    K.gates_dram = nc.dram_tensor("gates_dram", (NCH, E, CH), fp32, kind="Internal").ap()
    K.rows_dram = nc.dram_tensor("rows_dram", (B, 3, D), fp32, kind="Internal").ap()
    with ctx, attn:
        def keep(name, shape, dt=fp32, c=ctx):
            return c.enter_context(nc.sbuf_tensor(name, shape, dt))

        K.sems = lambda *names: [ctx.enter_context(nc.semaphore(n)) for n in names]
        K.idle = {}
        for e in ("dve", "pool", "pe", "sp"):
            K.idle[e], = K.sems("idle_" + e)

        K.x_all = keep("x_all", [P, B * TB, D])
        K.w1h = keep("w1h", [P, NU, P], fp32r)
        K.w1l = keep("w1l", [P, NU, P], fp32r)
        K.w2h = keep("w2h", [P, NU, L], fp32r)
        K.w2l = keep("w2l", [P, NU, L], fp32r)
        K.downh = keep("downh", [P, DC, L], fp32r)
        K.downl = keep("downl", [P, DC, L], fp32r)
        K.coreh = keep("coreh", [P, DC, D], fp32r)
        K.corel = keep("corel", [P, DC, D], fp32r)
        K.uph = keep("uph", [P, D], fp32r)
        K.upl = keep("upl", [P, D], fp32r)
        K.b1c = keep("b1c", [P, NU])
        K.a0c = keep("a0c", [P, NU])
        K.b2c = keep("b2c", [P, GROUPS])
        K.u0 = keep("u0", [P, E, L])
        K.downbc = keep("downbc", [P, 1])
        K.ident = keep("ident", [P, P])
        K.ones2 = keep("ones2", [P, 2])
        K.Ah = keep("Ah", [P, DC, D], fp32r, attn)
        K.Al = keep("Al", [P, DC, D], fp32r, attn)
        K.Mh = keep("Mh", [P, DC, D], fp32r, attn)
        K.Ml = keep("Ml", [P, DC, D], fp32r, attn)
        K.bqk = keep("bqk", [P, DC], fp32, attn)
        K.bvo_bc = keep("bvo_bc", [P, D], fp32, attn)
        K.modc = keep("modc", [P, B, 4, DC], fp32, attn)
        K.rwp = keep("rwp", [P, DC, P], fp32r, attn)
        K.rwh = keep("rwh", [P, DC, P], fp32r, attn)
        K.rb_bc = keep("rb_bc", [P, E], fp32, attn)
        K.iota8 = keep("iota8", [P, E], fp32, attn)
        (K.b1_in, K.x0_in, K.x_in, K.rows_stored) = K.sems("b1_in", "x0_in", "x_in", "rows_stored")
        prepare(nc, a, K)
        attention(nc, a, K, attn)
        attn.close()
        experts(nc, out, K, ctx)


def prepare(nc, a, K):
    setup = ExitStack()
    with setup:
        def sbt(name, shape, dt=fp32):
            return setup.enter_context(nc.sbuf_tensor(name, shape, dt))

        wqkv = sbt("wqkv", [P, 3 * DC, D])
        wout = sbt("wout", [P, DC, D])
        woT = sbt("woT", [P, DC, D])
        wmod = sbt("wmod", [P, DC, 6 * D])
        crow = sbt("crow", [B, D])
        sig = sbt("sig", [B, D])
        sc = sbt("sc_rows", [B, D])
        scT = sbt("scT", [P, DC, B])
        bqc = sbt("bqc", [P, DC, 1])
        bvc = sbt("bvc", [P, DC, 1])
        bvb = sbt("bvb", [P, DC, P])
        bo_bc = sbt("bo_bc", [P, D])
        upb = sbt("upb", [B, D])
        coreb = sbt("coreb", [B, D])
        rwraw = sbt("rwraw", [P, DC, E])
        rbraw = sbt("rbraw", [P, E])
        grow = sbt("grow", [B, 3, D])
        sgn = sbt("sgn", [B, 2, D])
        bank = [setup.enter_context(nc.psum_tensor(f"bank{k}", [P, 512], fp32)) for k in range(8)]

        (wq_in, wo_in, c_in, wmodA_in, wmodB_in, rows_in, cols_in, rw_in, id_made, wo_turned, woT_made,
         fold_ps, fold_made, sc_made, sc_turned, scT_made, bvb_made, bias_ps, brow_ps, modA_ps, modB_ps, modc_read,
         g_ps, grow_made, sig_made, dve_s, pool_s) = K.sems(
            "wq_in", "wo_in", "c_in", "wmodA_in", "wmodB_in", "rows_in", "cols_in", "rw_in", "id_made",
            "wo_turned", "woT_made", "fold_ps", "fold_made", "sc_made", "sc_turned", "scT_made", "bvb_made",
            "bias_ps", "brow_ps", "modA_ps", "modB_ps", "modc_read", "g_ps", "grow_made", "sig_made", "dve_s", "pool_s")

        with nc.Block() as block:
            @block.sync
            def _(sp):
                wm = a["wmod"].rearrange("(c p) n -> p c n", p=P)
                sp.dma_start(K.x_all[:, 0:TB, :], a["x"][0].rearrange("(p t) d -> p t d", t=TB)).then_inc(K.x0_in, 16)
                sp.dma_start(wqkv[:], a["w_qkv"].rearrange("(c p) i -> p c i", p=P)).then_inc(wq_in, 16)
                sp.dma_start(wmod[:, :, 0:3 * D], wm[:, :, 0:3 * D]).then_inc(wmodA_in, 16)
                sp.dma_start(wmod[:, :, 3 * D:6 * D], wm[:, :, 3 * D:6 * D]).then_inc(wmodB_in, 16)
                for b in range(1, B):
                    sp.dma_start(K.x_all[:, b * TB:(b + 1) * TB, :],
                                 a["x"][b].rearrange("(p t) d -> p t d", t=TB)).then_inc(K.x_in, 16)
                sp.wait_ge(grow_made, 1)
                sp.dma_start(K.rows_dram, grow[:]).then_inc(K.rows_stored, 16)
                sp.wait_ge(K.rows_stored, 16)

            @block.gpsimd
            def _(pool):
                g = nc.gpsimd
                pc = Chain(pool, pool_s)
                pc.link(g.memset(K.ident[:], 0.0))
                g.affine_select(out=K.ident[:], in_=K.ident[:], compare_op=ALU.not_equal, fill=1.0,
                                base=0, pattern=[[-1, P]], channel_multiplier=1).then_inc(id_made, 1)
                pool.dma_start(rwraw[:], a["router_w"].rearrange("(c p) e -> p c e", p=P)).then_inc(rw_in, 16)
                pool.dma_start(rbraw[:], a["router_b"].partition_broadcast(P)).then_inc(rw_in, 16)
                pool.dma_start(upb[:], a["up_b"].partition_broadcast(B)).then_inc(rows_in, 16)
                pool.dma_start(coreb[:], a["core_b"].partition_broadcast(B)).then_inc(rows_in, 16)
                for e in range(E):
                    g.memset(K.iota8[:, e:e + 1], float(e))
                g.memset(K.ones2[:], 1.0)
                pc.link(g.memset(K.u0[:], 0.0))

            @block.scalar
            def _(act):
                act.dma_start(crow[:], a["c"]).then_inc(c_in, 16)
                act.dma_start(wout[:], a["w_out"].rearrange("(c p) o -> p c o", p=P)).then_inc(wo_in, 16)
                act.dma_start(bqc[:], a["b_qkv"][0:D].rearrange("(c p o) -> p c o", p=P, o=1),
                              allow_slow_non_contiguous=True).then_inc(cols_in, 16)
                act.dma_start(bvc[:], a["b_qkv"][2 * D:3 * D].rearrange("(c p o) -> p c o", p=P, o=1),
                              allow_slow_non_contiguous=True).then_inc(cols_in, 16)
                act.dma_start(bo_bc[:], a["b_out"].partition_broadcast(P)).then_inc(cols_in, 16)
                act.wait_ge(c_in, 16)
                nc.scalar.activation(sig[:], crow[:], ACT.Exp, scale=-1.0).then_inc(sig_made, 1)
                act.dma_start(K.b1c[:, 0:1], a["shared_b1"].rearrange("(p n) -> p n", n=1)).then_inc(K.b1_in, 16)
                act.dma_start(K.b2c[:, 0:1], a["shared_b2"].rearrange("(p n) -> p n", n=1)).then_inc(K.b1_in, 16)
                act.dma_start(K.downbc[:], a["down_b"].rearrange("(p n) -> p n", n=1)).then_inc(K.b1_in, 16)
                for e in range(E):
                    n, u = HID[e] // P, FIRST_UNIT[e + 1]
                    act.dma_start(K.b1c[:, u:u + n], a[f"e{e}_b1"].rearrange("(p n) -> p n", n=n)).then_inc(K.b1_in, 16)
                    act.dma_start(K.b2c[:, e + 1:e + 2], a[f"e{e}_b2"].rearrange("(p n) -> p n", n=1)).then_inc(K.b1_in, 16)

            @block.vector
            def _(dve):
                dc = Chain(dve, dve_s)
                v = nc.vector
                dc.link(v.memset(K.rwp[:].bitcast(fp32), 0.0))
                dc.link(v.memset(K.rwh[:].bitcast(fp32), 0.0))
                dve.wait_ge(sig_made, 1)
                dc.link(v.tensor_scalar(sig[:], sig[:], 1.0, None, ALU.add))
                dc.link(v.reciprocal(sig[:], sig[:]))
                v.tensor_tensor(sc[:], crow[:], sig[:], ALU.mult).then_inc(sc_made, 1)
                dve.wait_ge(sc_turned, 1)
                v.tensor_copy(scT[:].rearrange("p k b -> p (k b)"), bank[6][:, 0:DC * B]).then_inc(scT_made, 1)
                for k in range(DC):
                    dve.wait_ge(wo_turned, k + 1)
                    v.tensor_copy(woT[:, k, :], bank[k][:, 0:D]).then_inc(woT_made, 1)
                dve.wait_ge(cols_in, 48)
                v.tensor_copy(bvb[:], bvc[:].to_broadcast([P, DC, P])).then_inc(bvb_made, 1)
                for n, (hi, lo) in enumerate(((K.Ah, K.Al), (K.Mh, K.Ml))):
                    for k in range(DC):
                        dve.wait_ge(fold_ps, n * DC + k + 1)
                        dc.link(v.tensor_copy(hi[:, k, :], bank[2 + n * DC + k][:, 0:D]))
                        v.tensor_tensor(lo[:, k, :], bank[2 + n * DC + k][:, 0:D], hi[:, k, :].bitcast(fp32), ALU.subtract).then_inc(fold_made, 1)
                dve.wait_ge(bias_ps, 1)
                v.tensor_copy(K.bqk[:], bank[6][:, 16:16 + 2 * DC:2])
                for n, sem in enumerate((modA_ps, modB_ps)):
                    dve.wait_ge(sem, 1)
                    for w in (0, 1):
                        for k in range(DC):
                            src = bank[n][:, (w * DC + k) * B:(w * DC + k + 1) * B]
                            v.tensor_scalar(K.modc[:, :, 2 * n + w, k], src, float(w), None, ALU.add).then_inc(modc_read, 1)
                dve.wait_ge(brow_ps, 1)
                v.tensor_tensor(K.bvo_bc[:], bank[7][:, 0:D], bo_bc[:], ALU.add)
                dve.wait_ge(rw_in, 32)
                v.tensor_copy(K.rwp[:, :, 0:E], rwraw[:])
                dc.link(v.tensor_copy(K.rwh[:, :, 0:E], rwraw[:]))
                v.tensor_tensor(K.rwp[:, :, E:2 * E], rwraw[:], K.rwh[:, :, 0:E].bitcast(fp32), ALU.subtract)
                for e, h in enumerate(HID):
                    v.tensor_scalar(K.rb_bc[:, e:e + 1], rbraw[:, e:e + 1], -COST_LAMBDA * (2 * L * h), None, ALU.add)
                dve.wait_ge(g_ps, 1)
                g, src = grow[:, 0:2, :].rearrange("b n d -> b (n d)"), bank[2][0:B, :]
                s = sgn[:].rearrange("b n d -> b (n d)")
                v.tensor_scalar(s, src, 0.0, 2.0, ALU.is_ge, ALU.mult)
                dc.link(v.tensor_scalar(g, src, -1.0, 0.25, ALU.mult, ALU.max))
                dc.link(v.tensor_tensor(g, src, g, ALU.max))
                dc.link(v.tensor_scalar(s, s, -1.0, None, ALU.add))
                dc.link(v.tensor_tensor(g, g, s, ALU.mult))
                dve.wait_ge(rows_in, 32)
                dc.link(v.tensor_tensor(grow[:, 2, :], upb[:], coreb[:], ALU.add))
                v.tensor_tensor(grow[:, 2, :], grow[:, 2, :], grow[:, 1, :], ALU.mult).then_inc(grow_made, 1)
                dve.wait_ge(grow_made, 1)

            @block.tensor
            def _(pe):
                mm = nc.tensor.matmul

                def pair(dst, lhs, rhs):
                    for o in range(DC):
                        last = mm(dst, lhs(o), rhs(o), start=(o == 0), stop=(o == DC - 1))
                    return last

                pe.wait_ge(id_made, 1)
                pe.wait_ge(wo_in, 16)
                for oc in range(DC):
                    for jc in range(DC):
                        last = nc.tensor.transpose(bank[oc][:, jc * P:(jc + 1) * P],
                                                   wout[:, jc, oc * P:(oc + 1) * P], K.ident[:])
                    last.then_inc(wo_turned, 1)
                pe.wait_ge(sc_made, 1)
                for k in range(DC):
                    last = nc.tensor.transpose(bank[6][:, k * B:(k + 1) * B], sc[:, k * P:(k + 1) * P], K.ident[0:B, 0:B])
                last.then_inc(sc_turned, 1)
                pe.wait_ge(wq_in, 16)
                for k in range(DC):
                    pair(bank[2 + k][:, 0:D], lambda o: wqkv[:, o, k * P:(k + 1) * P],
                         lambda o: wqkv[:, DC + o, :]).then_inc(fold_ps, 1)
                pe.wait_ge(woT_made, DC)
                for k in range(DC):
                    pair(bank[4 + k][:, 0:D], lambda o: wqkv[:, 2 * DC + o, k * P:(k + 1) * P],
                         lambda o: woT[:, o, :]).then_inc(fold_ps, 1)
                pe.wait_ge(scT_made, 1)
                pe.wait_ge(cols_in, 48)
                for k in range(DC):
                    last = pair(bank[6][:, 16 + 2 * k:17 + 2 * k], lambda o: wqkv[:, DC + o, k * P:(k + 1) * P],
                                lambda o: bqc[:, o, :])
                last.then_inc(bias_ps, 1)
                pe.wait_ge(bvb_made, 1)
                pair(bank[7][:, 0:D], lambda o: bvb[:, o, :], lambda o: woT[:, o, :]).then_inc(brow_ps, 1)

                def columns(dst, segs, sem):
                    for w, seg in enumerate(segs):
                        for k in range(DC):
                            last = pair(dst[:, (w * DC + k) * B:(w * DC + k + 1) * B],
                                        lambda o: wmod[:, o, seg * D + k * P:seg * D + (k + 1) * P],
                                        lambda o: scT[:, o, :])
                    last.then_inc(sem, 1)

                pe.wait_ge(wmodA_in, 16)
                columns(bank[0], (0, 1), modA_ps)
                pe.wait_ge(wmodB_in, 16)
                columns(bank[1], (3, 4), modB_ps)
                pe.wait_ge(fold_made, 1)
                for n, seg in enumerate((2, 5)):
                    last = pair(bank[2][0:B, n * D:(n + 1) * D], lambda o: scT[:, o, :],
                                lambda o: wmod[:, o, seg * D:(seg + 1) * D])
                last.then_inc(g_ps, 1)


def attention(nc, a, K, attn):
    def sbt(name, shape, dt=fp32):
        return attn.enter_context(nc.sbuf_tensor(name, shape, dt))

    x_all, ident, bqk, modc = K.x_all, K.ident, K.bqk, K.modc
    ga_bc = sbt("ga_bc", [P, B, D])
    hfull = sbt("hfull", [P, 2, CH])
    hTh = sbt("hTh", [P, DC, S], fp32r)
    hTl = sbt("hTl", [P, DC, S], fp32r)
    qh = sbt("qh", [P, DC, S], fp32r)
    ql = sbt("ql", [P, DC, S], fp32r)
    vh = sbt("vh", [P, TB, D], fp32r)
    vl = sbt("vl", [P, TB, D], fp32r)
    prob = sbt("prob", [P, 2, S])
    pTh = sbt("pTh", [P, TB, P], fp32r)
    pTl = sbt("pTl", [P, TB, P], fp32r)
    xhat = sbt("xhat", [P, TB, D])
    xhatF = sbt("xhatF", [P, TC, D])
    hff = sbt("hff", [P, DC, CH])
    fh = sbt("fh", [P, DC, CH], fp32r)
    fl = sbt("fl", [P, DC, CH], fp32r)
    halfneg = sbt("halfneg", [P, TB])
    norm = {}
    for k in ("P", "F"):
        norm[k] = Norm(stat=sbt("stat" + k, [P, TB, 6]), mv=sbt("mv" + k, [P, TB, 2]), ve=sbt("ve" + k, [P, TB]),
                                  rstd=sbt("rstd" + k, [P, TB]), nmr=sbt("nmr" + k, [P, TB]))
    cur = sbt("cur", [P, 2, 2, DC])
    mx = sbt("mx", [P, TB])
    negm = sbt("negm", [P, TB])
    rsum = sbt("rsum", [P, TB])
    rinv = sbt("rinv", [P, TB])
    ot = sbt("ot", [P, D])
    lg = sbt("lg", [2 * E, CH])
    lt = sbt("lt", [P, TB, 2 * E])
    lo8 = sbt("lo8", [P, TB, E])
    m8 = sbt("m8", [P, TB, E])
    ix = sbt("ix", [P, TB, E], u32)
    ixf = sbt("ixf", [P, TB, 2])
    d8 = sbt("d8", [P, TB, E])
    e8 = sbt("e8", [P, TB, E])
    ssum = sbt("ssum", [P, TB])
    dp = sbt("dp", [P, TB])
    g0 = sbt("g0", [P, TB])
    g1 = sbt("g1", [P, TB])
    k0 = sbt("k0", [P, TB, E])
    k1 = sbt("k1", [P, TB, E])
    gates = sbt("gates", [P, B * TB, E])
    stage = sbt("stage", [P, 2, 512])
    wtmp = sbt("wtmp", [P, P])

    psc = ExitStack()
    sc = psc.enter_context(nc.psum_tensor("sc", [P, 2, S], fp32))
    ptp = psc.enter_context(nc.psum_tensor("ptp", [P, S], fp32))
    ob = [psc.enter_context(nc.psum_tensor(f"ob{k}", [P, 512], fp32)) for k in range(2)]
    quad = [sc[:, n // 2, (n % 2) * CH:(n % 2 + 1) * CH] for n in range(4)]
    vbank = [ptp[:, 0:512], ptp[:, 512:1024], ob[0][:], ob[1][:]]

    w_in = K.sems("w_in0", "w_in1")
    gt_stored = K.sems("gt_stored0", "gt_stored1")
    (ga_in, a0_made, half_made, d_s, p_s, w_taken, xvar_ready, xrstd_ready, fvar_ready, frstd_ready, xhat_ready, xhatF_ready,
     turned, fturned, hfull_ready, hff_ready, ht_ready, f_ready, q_ps, qh_ready, ql_ready, v_ps, vh_ready,
     vl_ready, sc_ready, negm_ready, p_ready, pt_ready, pth_ready, ptl_ready, pv_ready, ot_ready, x1_ready, lg_ps,
     lg_ready, lt_ready, lt_read, d_ready, e_ready, gates_ready, gt_ps, gt_ready, stored, cur_ready) = K.sems(
        "ga_in", "a0_made", "half_made", "d_s", "p_s", "w_taken", "xvar_ready", "xrstd_ready", "fvar_ready", "frstd_ready",
        "xhat_ready", "xhatF_ready", "turned", "fturned", "hfull_ready", "hff_ready", "ht_ready", "f_ready",
        "q_ps", "qh_ready", "ql_ready", "v_ps", "vh_ready", "vl_ready", "sc_ready", "negm_ready", "p_ready",
        "pt_ready", "pth_ready", "ptl_ready", "pv_ready", "ot_ready", "x1_ready", "lg_ps", "lg_ready", "lt_ready",
        "lt_read", "d_ready", "e_ready", "gates_ready", "gt_ps", "gt_ready", "stored", "cur_ready")

    pieces = []
    for e in range(E):
        n, u = HID[e] // P, FIRST_UNIT[e + 1]
        pieces.append((a[f"e{e}_w1"].rearrange("l (q n) -> l q n", n=n), (P, n), True,
                       K.w1h[:, u:u + n, :], K.w1l[:, u:u + n, :], 1.0, None))
        pieces.append((a[f"e{e}_w2"].rearrange("(p n) l -> p n l", n=n), (n, L), False,
                       K.w2h[:, u:u + n, :], K.w2l[:, u:u + n, :], 1.0, e))
    one = lambda w: w.rearrange("p (n l) -> p n l", n=1)
    pieces.append((one(a["shared_w1"]), (1, P), False, K.w1h[:, 0:1, :], K.w1l[:, 0:1, :], 1.0, None))
    pieces.append((one(a["shared_w2"]), (1, L), False, K.w2h[:, 0:1, :], K.w2l[:, 0:1, :], 0.1, None))
    pieces.append((a["down_w"].rearrange("(c p) l -> p c l", p=P), (DC, L), False, K.downh[:], K.downl[:], 1.0, None))
    pieces.append((one(a["up_w"]), (1, D), False, K.uph[:].unsqueeze(1), K.upl[:].unsqueeze(1), 1.0, None))
    pieces.append((a["core_w"].rearrange("(c p) n -> p c n", p=P), (DC, D), False, K.coreh[:], K.corel[:], 1.0, None))
    PER_BATCH = -(-len(pieces) // B)

    def staged(k):
        s0, s1 = pieces[k][1]
        return stage[:, k % 2, 0:s0 * s1].rearrange("p (x y) -> p x y", x=s0)

    def sequences(eng, boundary, tiles):
        boundary(-1, False, True)
        with eng.Fori(0, B - 1) as b:
            tiles(b, True)
            boundary(b, True, True)
        tiles(B - 1, False)
        boundary(B - 1, True, False)

    def row(t):
        return x_all[:, bass.ds(t, 1), :].rearrange("p a d -> p (a d)")

    with nc.Block() as block:
        @block.sync
        def _(sp):
            sp.dma_start(ga_bc[:], K.rows_dram[:, 0, :].partition_broadcast(P)).then_inc(ga_in, 16)
            for k, piece in enumerate(pieces):
                if k >= 2:
                    sp.wait_ge(w_taken, k - 1)
                sp.dma_start(staged(k), piece[0]).then_inc(w_in[k % 2], 16)

        @block.gpsimd
        def _(pool):
            g = nc.gpsimd
            pc = Chain(pool, p_s)

            def split_piece(k):
                src, shape, turn, hi, lo, scale, expert = pieces[k]
                pool.wait_ge(w_in[k % 2], 16 * (k // 2 + 1))
                raw = staged(k)
                if turn:
                    raw = raw.rearrange("p q n -> p n q")
                if scale != 1.0:
                    pc.link(g.tensor_scalar(wtmp[:].unsqueeze(1), raw, scale, 0.0, ALU.mult, ALU.add))
                    raw = wtmp[:].unsqueeze(1)
                pc.link(g.tensor_scalar(hi, raw, 1.0, 0.0, ALU.mult, ALU.add))
                pc.link(g.tensor_tensor(lo, raw, hi.bitcast(fp32), ALU.subtract))
                if expert is not None:
                    for j in range(shape[0]):
                        u = FIRST_UNIT[expert + 1] + j
                        pc.link(g.tensor_scalar(wtmp[:], raw[:, j, :], K.a0c[:, u:u + 1], 0.0, ALU.mult, ALU.add))
                        pc.link(g.tensor_tensor(K.u0[:, expert, :], K.u0[:, expert, :], wtmp[:], ALU.add))
                pool.sem_inc(w_taken, 1)

            def inverse_root(n, cols, seen, count, made):
                pool.wait_ge(seen, count)
                g.tensor_tensor(n.rstd[:, cols], n.ve[:, cols], halfneg[:, cols], ALU.pow).then_inc(made, 1)

            every, first, second = slice(0, TB), slice(0, TC), slice(TC, TB)
            pc.link(g.memset(halfneg[:], -0.5))
            inverse_root(norm["P"], every, xvar_ready, 1, xrstd_ready)
            pool.wait_ge(a0_made, 1)
            for b in range(B):
                for k in range(b * PER_BATCH, min(len(pieces), (b + 1) * PER_BATCH)):
                    split_piece(k)
                if b + 1 < B:
                    inverse_root(norm["P"], every, xvar_ready, b + 2, xrstd_ready)
                inverse_root(norm["F"], first, fvar_ready, 2 * b + 1, frstd_ready)
                inverse_root(norm["F"], second, fvar_ready, 2 * b + 2, frstd_ready)

        @block.vector
        def _(dve):
            v = nc.vector
            idle = K.idle["dve"]
            per_loop = DVE_LINKS_A
            dc = Chain(dve, d_s)

            def aggregate(n, lo, hi, sem):
                for t in range(lo, hi):
                    last = v.bn_aggr(n.mv[:, t, :], n.stat[:, t, :])
                dc.link(last)
                v.tensor_scalar(n.ve[:, lo:hi], n.mv[:, lo:hi, 1], LN_EPS, None, ALU.add).then_inc(sem, 1)

            def shift(n, lo, hi, sem, count):
                dve.wait_ge(sem, count)
                dc.link(v.scalar_tensor_tensor(n.nmr[:, lo:hi], n.mv[:, lo:hi, 0], -1.0, n.rstd[:, lo:hi], ALU.mult, ALU.mult))

            def normalise(n, dst, t, src, sem):
                v.tensor_scalar(dst, src, n.rstd[:, t:t + 1], n.nmr[:, t:t + 1], ALU.mult, ALU.add).then_inc(sem, 1)

            def split_keys(p, half):
                for c in range(DC):
                    n = 2 * half + c
                    cols = slice(half * CH, (half + 1) * CH)
                    dve.wait_ge(hfull_ready, p * 4 + n + 1)
                    dc.link(v.tensor_copy(hTh[:, c, cols], hfull[:, c, :]))
                    v.tensor_tensor(hTl[:, c, cols], hfull[:, c, :], hTh[:, c, cols].bitcast(fp32),
                                    ALU.subtract).then_inc(ht_ready, 1)

            def split_ffn(f, half):
                for c in range(DC):
                    if half and c == 0:
                        dve.wait_ge(lg_ps, f * HB + half)
                    dve.wait_ge(hff_ready, f * 4 + 2 * half + c + 1)
                    dc.link(v.tensor_copy(fh[:, c, :], hff[:, c, :]))
                    v.tensor_tensor(fl[:, c, :], hff[:, c, :], fh[:, c, :].bitcast(fp32), ALU.subtract).then_inc(f_ready, 1)

            def row_max(b, t):
                dve.wait_ge(sc_ready, b * TB + t + 1)
                dc.link(v.reduce_max(mx[:, t:t + 1], sc[:, t % 2, :], AX))
                v.tensor_scalar(negm[:, t:t + 1], mx[:, t:t + 1], -SCORE_SCALE, None, ALU.mult).then_inc(negm_ready, 1)

            def residual(b, t):
                dve.wait_ge(pv_ready, b * TB + t + 1)
                dc.link(v.reciprocal(rinv[:, t:t + 1], rsum[:, t:t + 1]))
                dc.link(v.scalar_tensor_tensor(ot[:], ob[t % 2][:, 0:D], rinv[:, t:t + 1], K.bvo_bc[:], ALU.mult, ALU.add))
                dc.link(v.tensor_tensor(ot[:], ot[:], ga_bc[:, bass.ds(b, 1), :].rearrange("p a d -> p (a d)"), ALU.mult))
                v.tensor_tensor(row(b * TB + t), ot[:], row(b * TB + t), ALU.add).then_inc(x1_ready, 1)

            def stats1(b, t):
                hold(dve, x1_ready, b * TB + t + 1, idle)
                return v.bn_stats(norm["F"].stat[:, t, :], row(b * TB + t))

            def queries_low(p, n):
                half, c = n // 2, n % 2
                cols = slice(half * CH, (half + 1) * CH)
                dve.wait_ge(qh_ready, p * 4 + n + 1)
                v.scalar_tensor_tensor(ql[:, c, cols], quad[n], bqk[:, c:c + 1], qh[:, c, cols].bitcast(fp32),
                                       ALU.add, ALU.subtract).then_inc(ql_ready, 1)

            def values_low(p, n):
                dve.wait_ge(vh_ready, p * 4 + n + 1)
                pair = slice(2 * n, 2 * n + 2)
                v.tensor_tensor(vl[:, pair, :].rearrange("p t d -> p (t d)"), vbank[n],
                                vh[:, pair, :].rearrange("p t d -> p (t d)").bitcast(fp32), ALU.subtract).then_inc(vl_ready, 1)

            def route(f):
                every = [P, TB, E]
                dve.wait_ge(lt_ready, (f + 1) * HB)
                v.tensor_copy(lt[:].rearrange("p t e -> p (t e)"), ob[0][:, 0:TB * 2 * E]).then_inc(lt_read, 1)
                dve.wait_ge(lt_read, f + 2)
                dc.link(v.tensor_tensor(lo8[:], lt[:, :, 0:E], lt[:, :, E:2 * E], ALU.add))
                dc.hold(v.tensor_tensor(lo8[:], lo8[:], K.rb_bc[:].unsqueeze(1).to_broadcast(every), ALU.add), idle)
                for t in range(TB):
                    last = v.max(m8[:, t, :], lo8[:, t, :])
                dc.link(last)
                v.tensor_tensor(d8[:], m8[:], m8[:, :, 0:1].to_broadcast(every), ALU.subtract).then_inc(d_ready, 1)
                for t in range(TB):
                    last = v.max_index(ix[:, t, :], m8[:, t, :], lo8[:, t, :])
                dc.link(last)
                dc.link(v.tensor_copy(ixf[:], ix[:, :, 0:2]))
                dve.wait_ge(e_ready, f * 2 + 1)
                dc.link(v.reduce_sum(ssum[:], e8[:], AX))
                dc.link(v.reciprocal(ssum[:], ssum[:]))
                dc.link(v.tensor_tensor(dp[:], e8[:, :, 1], e8[:, :, 0], ALU.subtract))
                v.tensor_tensor(dp[:], dp[:], ssum[:], ALU.mult).then_inc(d_ready, 1)
                iota = K.iota8[:].unsqueeze(1).to_broadcast(every)
                v.tensor_tensor(k0[:], iota, ixf[:, :, 0:1].to_broadcast(every), ALU.is_equal)
                dc.link(v.tensor_tensor(k1[:], iota, ixf[:, :, 1:2].to_broadcast(every), ALU.is_equal))
                dve.wait_ge(e_ready, f * 2 + 2)
                dc.link(v.tensor_scalar(g0[:], g1[:], 1.0, None, ALU.add))
                dc.link(v.reciprocal(g0[:], g0[:]))
                dc.link(v.tensor_tensor(g1[:], g1[:], g0[:], ALU.mult))
                v.tensor_tensor(k0[:], k0[:], g0[:].unsqueeze(2).to_broadcast(every), ALU.mult)
                dc.link(v.tensor_tensor(k1[:], k1[:], g1[:].unsqueeze(2).to_broadcast(every), ALU.mult))
                v.tensor_tensor(gates[:, bass.ds(f * TB, TB), :], k0[:], k1[:], ALU.add).then_inc(gates_ready, 1)

            def tiles(b, more):
                nP, nF = norm["P"], norm["F"]
                for t in range(TB):
                    dve.wait_ge(pth_ready, b * TB + t + 1)
                    v.tensor_tensor(pTl[:].rearrange("p t q -> p (t q)"), ptp[:],
                                    pTh[:].rearrange("p t q -> p (t q)").bitcast(fp32), ALU.subtract).then_inc(ptl_ready, 1)
                    if t + 2 < TB:
                        row_max(b, t + 2)
                    if t >= 2:
                        stats1(b, t - 2)
                    if t:
                        residual(b, t - 1)
                    if more and t < 4:
                        for k in (2 * t, 2 * t + 1):
                            last = v.bn_stats(nP.stat[:, k, :], row((b + 1) * TB + k))
                        if t == 3:
                            dc.hold(last, idle)
                            aggregate(nP, 0, TB, xvar_ready)
                    if t == 4:
                        dc.link(v.tensor_copy(cur[:, 1].unsqueeze(1), modc[:, bass.ds(b, 1), 2:4, :]))
                        if more:
                            dc.link(v.tensor_copy(cur[:, 0].unsqueeze(1), modc[:, bass.ds(b + 1, 1), 0:2, :]))
                    if t == 5:
                        hold(dve, x1_ready, b * TB + 5, idle)
                        aggregate(nF, 0, TC, fvar_ready)
                    if more and t == 5:
                        shift(nP, 0, TB, xrstd_ready, b + 2)
                    if more and t in (5, 6):
                        for k in range((t - 5) * TC, (t - 4) * TC):
                            normalise(nP, xhat[:, k, :], k, row((b + 1) * TB + k), xhat_ready)
                    if t == 6:
                        shift(nF, 0, TC, frstd_ready, 2 * b + 1)
                        for k in range(TC):
                            normalise(nF, xhatF[:, k, :], k, row(b * TB + k), xhatF_ready)
                    if more and t == TB - 1:
                        split_keys(b + 1, 0)
                stats1(b, TB - 2)
                residual(b, TB - 1)

            def boundary(f, has_last, has_next):
                p, nP, nF = f + 1, norm["P"], norm["F"]
                if has_last:
                    dc.hold(stats1(f, TB - 1), idle)
                    aggregate(nF, TC, TB, fvar_ready)
                if has_next:
                    if not has_last:
                        dve.wait_ge(K.x0_in, 16)
                        for t in range(TB):
                            last = v.bn_stats(nP.stat[:, t, :], x_all[:, t, :])
                        dc.link(last)
                        aggregate(nP, 0, TB, xvar_ready)
                        v.tensor_copy(cur[:, 0], modc[:, 0, 0:2, :]).then_inc(cur_ready, 1)
                        shift(nP, 0, TB, xrstd_ready, 1)
                        for t in range(TB):
                            normalise(nP, xhat[:, t, :], t, x_all[:, t, :], xhat_ready)
                        split_keys(p, 0)
                    split_keys(p, 1)
                    queries_low(p, 0)
                    queries_low(p, 1)
                if has_last:
                    shift(nF, TC, TB, frstd_ready, 2 * f + 2)
                    for t in range(TC, TB):
                        normalise(nF, xhat[:, t, :], t, row(f * TB + t), xhatF_ready)
                if has_next:
                    queries_low(p, 2)
                    queries_low(p, 3)
                if has_last:
                    split_ffn(f, 0)
                if has_next:
                    values_low(p, 0)
                    values_low(p, 1)
                if has_last:
                    split_ffn(f, 1)
                if has_next:
                    values_low(p, 2)
                    values_low(p, 3)
                    row_max(p, 0)
                    row_max(p, 1)
                if has_last:
                    route(f)
                if not has_last:
                    dve.sem_inc(lt_read, 1)
                    dve.wait_ge(K.x_in, 16 * (B - 1))
                    dve.wait_ge(ga_in, 16)

            boundary(-1, False, True)
            n0 = dc.n
            with dve.Fori(0, B - 1) as b:
                dc.base, dc.n = b * per_loop + n0, 0
                tiles(b, True)
                boundary(b, True, True)
                assert dc.n == per_loop, dc.n
            dc.base, dc.n = (B - 1) * per_loop + n0, 0
            tiles(B - 1, False)
            boundary(B - 1, True, False)
            dve.wait_ge(gates_ready, B)

        @block.scalar
        def _(act):
            sa = nc.scalar.activation

            def softmax(b, t):
                act.wait_ge(negm_ready, b * TB + t + 1)
                if t >= 2:
                    act.wait_ge(pt_ready, b * TB + t - 1)
                sa(prob[:, t % 2, :], sc[:, t % 2, :], ACT.Exp, bias=negm[:, t:t + 1], scale=SCORE_SCALE,
                   accum_out=rsum[:, t:t + 1]).then_inc(p_ready, 1)

            def modulate_keys(p, half):
                for c in range(DC):
                    n = 2 * half + c
                    act.wait_ge(turned, p * 4 + n + 1)
                    if half:
                        act.wait_ge(ht_ready, p * 4 + c + 1)
                    sa(hfull[:, c, :], quad[n], ACT.Identity, scale=cur[:, 0, 1, c:c + 1],
                       bias=cur[:, 0, 0, c:c + 1]).then_inc(hfull_ready, 1)

            def modulate_ffn(f, half):
                for c in range(DC):
                    n = 2 * half + c
                    act.wait_ge(fturned, f * 4 + n + 1)
                    if half:
                        act.wait_ge(f_ready, f * 4 + c + 1)
                        if c == 0:
                            act.wait_ge(stored, (f * HB + 1) * 16)
                    sa(hff[:, c, :], quad[n], ACT.Identity, scale=cur[:, 1, 1, c:c + 1],
                       bias=cur[:, 1, 0, c:c + 1]).then_inc(hff_ready, 1)
                act.wait_ge(hff_ready, f * 4 + 2 * half + 2)
                act.dma_start(K.hf_dram[bass.ds(f * HB + half, 1)].rearrange("a p c t -> p (a c) t"), hff[:]).then_inc(stored, 16)

            def queries_high(p, n):
                half, c = n // 2, n % 2
                act.wait_ge(q_ps, p * 4 + n + 1)
                sa(qh[:, c, half * CH:(half + 1) * CH], quad[n], ACT.Identity, bias=bqk[:, c:c + 1]).then_inc(qh_ready, 1)

            def values_high(p, n):
                act.wait_ge(v_ps, p * 4 + n + 1)
                sa(vh[:, 2 * n:2 * n + 2, :].rearrange("p t d -> p (t d)"), vbank[n], ACT.Copy).then_inc(vh_ready, 1)

            def logits(f, half):
                act.wait_ge(lg_ps, f * HB + half + 1)
                if half:
                    act.wait_ge(lt_ready, f * HB + half)
                sa(lg[:], quad[2 * half][0:2 * E, :], ACT.Copy).then_inc(lg_ready, 1)

            def tiles(b, more):
                softmax(b, 0)
                for t in range(TB):
                    act.wait_ge(pt_ready, b * TB + t + 1)
                    sa(pTh[:].rearrange("p t q -> p (t q)"), ptp[:], ACT.Copy).then_inc(pth_ready, 1)
                    if t + 1 < TB:
                        softmax(b, t + 1)
                    if more and t == 6:
                        modulate_keys(b + 1, 0)

            def boundary(f, has_last, has_next):
                p = f + 1
                if not has_last:
                    act.wait_ge(cur_ready, 1)
                    modulate_keys(p, 0)
                if has_next:
                    modulate_keys(p, 1)
                    for n in range(4):
                        queries_high(p, n)
                if has_last:
                    modulate_ffn(f, 0)
                if has_next:
                    values_high(p, 0)
                    values_high(p, 1)
                if has_last:
                    modulate_ffn(f, 1)
                if has_next:
                    values_high(p, 2)
                    values_high(p, 3)
                if has_last:
                    logits(f, 0)
                    logits(f, 1)
                    act.wait_ge(d_ready, f * 2 + 1)
                    sa(e8[:], d8[:], ACT.Exp).then_inc(e_ready, 1)
                    act.wait_ge(d_ready, f * 2 + 2)
                    sa(g1[:], dp[:], ACT.Exp).then_inc(e_ready, 1)
                    act.wait_ge(stored, (f * HB + 2) * 16)

            act.wait_ge(K.b1_in, 16 * (3 + 2 * E))
            sa(K.a0c[:], K.b1c[:], ACT.Gelu).then_inc(a0_made, 1)
            sequences(act, boundary, tiles)
            for b in range(B):
                act.wait_ge(gt_ps, b + 1)
                if b >= 2:
                    act.wait_ge(gt_stored[b % 2], 16 * (b // 2))
                sa(prob[0:E, b % 2, :], gt_bank(sc, ptp, b), ACT.Copy).then_inc(gt_ready, 1)
                act.wait_ge(gt_ready, b + 1)
                act.dma_start(K.gates_dram[b * HB:(b + 1) * HB].rearrange("h e t -> e h t"),
                              prob[0:E, b % 2, :].rearrange("e (h t) -> e h t", h=HB)).then_inc(gt_stored[b % 2], 16)
            for k in range(2):
                act.wait_ge(gt_stored[k], 16 * B // 2)

        @block.tensor
        def _(pe):
            mm = nc.tensor.matmul
            idle = K.idle["pe"]

            def ht(c, cols):
                return hTh[:, c, cols], hTl[:, c, cols]

            def turn(src, half, wait_sem, count, sem):
                pe.wait_ge(wait_sem, count)
                for c in range(DC):
                    for t in range(TC):
                        last = nc.tensor.transpose(quad[2 * half + c][:, t * P:(t + 1) * P],
                                                   src[:, t, c * P:(c + 1) * P], ident[:])
                    last.then_inc(sem, 1)

            def turn_keys(p, half):
                turn(xhat[:, half * TC:(half + 1) * TC, :], half, xhat_ready, p * TB + (half + 1) * TC, turned)

            def turn_ffn(f, half):
                turn((xhatF[:], xhat[:, TC:TB, :])[half], half, xhatF_ready, f * TB + (half + 1) * TC, fturned)

            def queries(p, half):
                pe.wait_ge(ht_ready, p * 4 + 2 * half + 2)
                for c in range(DC):
                    for k in range(DC):
                        last = matmul3(nc, quad[2 * half + c], (K.Ah[:, k, c * P:(c + 1) * P], K.Al[:, k, c * P:(c + 1) * P]),
                                       ht(k, slice(half * CH, (half + 1) * CH)), k == 0, k == DC - 1)
                    last.then_inc(q_ps, 1)

            def values(p, n):
                for j in range(2):
                    t = 2 * n + j
                    for k in range(DC):
                        last = matmul3(nc, vbank[n][:, j * D:(j + 1) * D], ht(k, slice(t * P, (t + 1) * P)),
                                       (K.Mh[:, k, :], K.Ml[:, k, :]), k == 0, k == DC - 1)
                last.then_inc(v_ps, 1)

            def scores(b, t):
                for half in range(HB):
                    for k in range(DC):
                        cols = slice(t * P, (t + 1) * P)
                        last = matmul3(nc, sc[:, t % 2, half * CH:(half + 1) * CH], (qh[:, k, cols], ql[:, k, cols]),
                                       ht(k, slice(half * CH, (half + 1) * CH)), k == 0, k == DC - 1)
                last.then_inc(sc_ready, 1)

            def router(f, half):
                pe.wait_ge(f_ready, f * 4 + 2 * half + 2)
                for k in range(DC):
                    mm(quad[2 * half], K.rwp[:, k, :], fh[:, k, :], start=(k == 0), stop=False)
                    last = mm(quad[2 * half], K.rwh[:, k, :], fl[:, k, :], start=False, stop=(k == DC - 1))
                last.then_inc(lg_ps, 1)

            def turn_logits(f, half):
                hold(pe, lg_ready, f * HB + half + 1, idle)
                for t in range(TC):
                    n = half * TC + t
                    last = nc.tensor.transpose(ob[0][:, n * 2 * E:(n + 1) * 2 * E], lg[:, t * P:(t + 1) * P],
                                               ident[0:2 * E, 0:2 * E])
                last.then_inc(lt_ready, 1)

            def tiles(b, more):
                for t in range(TB):
                    pe.wait_ge(p_ready, b * TB + t + 1)
                    if t == 0:
                        pe.wait_ge(vl_ready, b * 4 + 4)
                    else:
                        pe.wait_ge(ptl_ready, b * TB + t)
                    for k in range(TB):
                        last = nc.tensor.transpose(ptp[:, k * P:(k + 1) * P], prob[:, t % 2, k * P:(k + 1) * P], ident[:])
                    last.then_inc(pt_ready, 1)
                    if t + 2 < TB:
                        scores(b, t + 2)
                    elif more:
                        turn_keys(b + 1, t + 2 - TB)
                    pe.wait_ge(ptl_ready, b * TB + t + 1)
                    if t >= 2:
                        pe.wait_ge(x1_ready, b * TB + t - 1)
                    if t == 0:
                        pe.wait_ge(lt_read, b + 1)
                    for k in range(TB):
                        last = matmul3(nc, ob[t % 2][:, 0:D], (pTh[:, k, :], pTl[:, k, :]),
                                       (vh[:, k, :], vl[:, k, :]), k == 0, k == TB - 1)
                    last.then_inc(pv_ready, 1)

            def boundary(f, has_last, has_next):
                p = f + 1
                if not has_last:
                    turn_keys(p, 0)
                    turn_keys(p, 1)
                if has_next:
                    queries(p, 0)
                    queries(p, 1)
                    pe.wait_ge(ql_ready, p * 4 + 2)
                if has_last:
                    turn_ffn(f, 0)
                if has_next:
                    values(p, 0)
                    values(p, 1)
                    pe.wait_ge(ql_ready, p * 4 + 4)
                if has_last:
                    pe.wait_ge(x1_ready, f * TB + TB)
                    turn_ffn(f, 1)
                if has_next:
                    values(p, 2)
                    values(p, 3)
                if has_last:
                    router(f, 0)
                    router(f, 1)
                    if has_next:
                        pe.wait_ge(vl_ready, p * 4 + 3)
                    turn_logits(f, 0)
                if has_next:
                    scores(p, 0)
                if has_last:
                    turn_logits(f, 1)
                if has_next:
                    scores(p, 1)

            sequences(pe, boundary, tiles)
            for b in range(B):
                pe.wait_ge(gates_ready, B)
                if b == 3:
                    pe.wait_ge(gt_ready, 1)
                for t in range(TB):
                    last = nc.tensor.transpose(gt_bank(sc, ptp, b)[:, t * P:(t + 1) * P], gates[:, b * TB + t, :], ident[:])
                last.then_inc(gt_ps, 1)
    psc.close()


def gt_bank(sc, ptp, b):
    return (sc[0:E, 0, :], sc[0:E, 1, :], ptp[0:E, :], sc[0:E, 0, :])[b]


def experts(nc, out, K, ctx):
    def sbt(name, shape, dt=fp32):
        return ctx.enter_context(nc.sbuf_tensor(name, shape, dt))

    x_all, b1c, b2c = K.x_all, K.b1c, K.b2c
    w1h, w1l, w2h, w2l = K.w1h, K.w1l, K.w2h, K.w2l
    NA, NPRE, NG, LAG = 6, 3, 3, 4
    assert NU % NPRE == 0 and GROUPS % NG == 0 and (HB * NU) % NA == 0
    GX_AT, H_AT, DOWN_AT, GF_AT = 11, 13, 16, 18
    Y_AT, OUT_AT, OD_AT = LAG + 2, LAG + 4, LAG + 5

    hin = sbt("hin", [P, HB, DC, CH])
    hh = sbt("hh", [P, DC, CH], fp32r)
    hl = sbt("hl", [P, DC, CH], fp32r)
    gf = sbt("gf", [P, CH])
    gh = sbt("gh", [P, HB, CH], fp32r)
    gl = sbt("gl", [P, HB, CH], fp32r)
    gxf = sbt("gxf", [P, DC, CH])
    gxh = sbt("gxh", [P, DC, CH], fp32r)
    gxl = sbt("gxl", [P, DC, CH], fp32r)
    af = sbt("af", [P, NA, CH])
    ah = sbt("ah", [P, NA, CH], fp32r)
    al = sbt("al", [P, NA, CH], fp32r)
    gbc = sbt("gbc", [P, E, CH])
    y = sbt("y", [P, HB, CH])
    yh = sbt("yh", [P, CH], fp32r)
    yl = sbt("yl", [P, CH], fp32r)
    te = sbt("te", [P, NG, CH])
    od = sbt("od", [P, TC, D])
    negc = sbt("negc", [P, E])
    cb = sbt("cb", [P, GROUPS])
    call = sbt("call", [P, 1])
    mod_bc = sbt("mod_bc", [P, B, 2, D])

    psc = ExitStack()
    pre = psc.enter_context(nc.psum_tensor("pre", [P, NPRE, CH], fp32))
    acc = psc.enter_context(nc.psum_tensor("acc", [P, NG, CH], fp32))
    op = psc.enter_context(nc.psum_tensor("op", [P, 2, CH], fp32))
    dn = op[:, 0, :]

    gates_in = K.sems(*[f"gates_in{e}" for e in range(E)])
    (mod_in, h_in, h_split, dn_ps, gf_ready, g_ready, gxf_ready, gx_ready, pre_ps, af_ready, al_ready, a_used,
     te_ready, y0_ready, add_ready, yl_ready, out_ps, od_ready, xr_ready, of_ready, sent, d2_s, c_ps, c_made) = K.sems(
        "mod_in", "h_in", "h_split", "dn_ps", "gf_ready", "g_ready", "gxf_ready", "gx_ready", "pre_ps", "af_ready",
        "al_ready", "a_used", "te_ready", "y0_ready", "add_ready", "yl_ready", "out_ps", "od_ready", "xr_ready", "of_ready",
        "sent", "d2_s", "c_ps", "c_made")

    SPILLS = {g: LAST_UNIT[g] + LAG + 1 >= NU for g in range(GROUPS)}

    def slot(half, u):
        return (half * NU + u) % NA

    def chunks(eng, body):
        for half in range(HB):
            body(0, half, half > 0, True)
        with eng.Fori(1, B - 1) as b:
            for half in range(HB):
                body(b, half, True, True)
        for half in range(HB):
            body(B - 1, half, True, half < HB - 1)

    def following(b, half):
        return (b, half + 1) if half + 1 < HB else (b + 1, 0)

    def preceding(b, half):
        return (b, half - 1) if half else (b - 1, HB - 1)

    def hf_at(b, half):
        return K.hf_dram[bass.ds(b * HB + half, 1)].rearrange("a p c t -> p (a c) t")

    def gates_at(b, half, e):
        return K.gates_dram[bass.ds(b * HB + half, 1), e, :].rearrange("a t -> (a t)").partition_broadcast(P)

    def out_at(b, half):
        o = out.rearrange("b (p h t) d -> b h p t d", h=HB, t=TC)
        return o[bass.ds(b, 1), half].rearrange("a p t d -> p (a t) d")

    with nc.Block() as block:
        @block.sync
        def _(sp):
            sp.dma_start(hin[:, 0], hf_at(0, 0)).then_inc(h_in, 16)
            for e in range(E):
                sp.dma_start(gbc[:, e, :], gates_at(0, 0, e)).then_inc(gates_in[e], 16)
            sp.dma_start(mod_bc[:], K.rows_dram[:, 1:3, :].partition_broadcast(P)).then_inc(mod_in, 16)

            def store(b, half):
                hold(sp, of_ready, b * HB + half + 1, K.idle["sp"])
                sp.dma_start(out_at(b, half), od[:]).then_inc(sent, 16)

            def body(b, half, prev, more):
                i = b * HB + half
                if more:
                    hold(sp, g_ready, i + 1, K.idle["sp"])
                    if prev:
                        hold(sp, gxf_ready, i * DC, K.idle["sp"])
                    sp.dma_start(hin[:, 1 - half], hf_at(*following(b, half))).then_inc(h_in, 16)
                if prev:
                    store(*preceding(b, half))
                if more:
                    for e in range(E):
                        hold(sp, te_ready, i * E + e + 1, K.idle["sp"])
                        sp.dma_start(gbc[:, e, :], gates_at(*following(b, half), e)).then_inc(gates_in[e], 16)

            chunks(sp, body)
            store(B - 1, HB - 1)
            sp.wait_ge(sent, 16 * NCH)

        @block.scalar
        def _(act):
            sa = nc.scalar.activation
            act.wait_ge(dn_ps, 1)
            sa(gf[:], dn[:], ACT.Gelu, bias=K.downbc[:]).then_inc(gf_ready, 1)

            def body(b, half, prev, more):
                i = b * HB + half
                for u in range(NU):
                    s = slot(half, u)
                    act.wait_ge(pre_ps, i * NU + u + 1)
                    if prev or u >= NA:
                        act.wait_ge(a_used, i * NU + u - NA + 1)
                    sa(af[:, s, :], pre[:, u % NPRE, :], ACT.Gelu, bias=b1c[:, u:u + 1])
                    sa(ah[:, s, :], pre[:, u % NPRE, :], ACT.Gelu, bias=b1c[:, u:u + 1]).then_inc(af_ready, 1)
                    if u in (GX_AT, GX_AT + 1):
                        c = u - GX_AT
                        if c == 0 and prev:
                            act.wait_ge(gx_ready, i * DC)
                        sa(gxf[:, c, :], hin[:, half, c, :], ACT.Gelu).then_inc(gxf_ready, 1)
                    if u == GF_AT and more:
                        act.wait_ge(dn_ps, i + 2)
                        act.wait_ge(g_ready, i + 1)
                        sa(gf[:], dn[:], ACT.Gelu, bias=K.downbc[:]).then_inc(gf_ready, 1)

            chunks(act, body)

        @block.vector
        def _(dve):
            v = nc.vector
            dc = Chain(dve, d2_s)

            def split(hi, lo, full, sem):
                dc.link(v.tensor_copy(hi, full))
                v.tensor_tensor(lo, full, hi.bitcast(fp32), ALU.subtract).then_inc(sem, 1)

            dve.wait_ge(h_in, 16)
            split(hh[:], hl[:], hin[:, 0], h_split)
            dve.wait_ge(c_ps, 1)
            cps = acc[:, 0, 0:2 * E].rearrange("p (e two) -> p e two", two=2)[:, :, 0]
            v.tensor_scalar(negc[:], cps, -1.0, None, ALU.mult)
            v.tensor_scalar(cb[:, 0:1], b2c[:, 0:1], 0.1, None, ALU.mult)
            dc.link(v.tensor_tensor(cb[:, 1:], cps, b2c[:, 1:], ALU.add))
            v.reduce_sum(call[:], cb[:], AX).then_inc(c_made, 1)
            dve.wait_ge(c_made, 1)
            dve.wait_ge(gf_ready, 1)
            split(gh[:, 0, :], gl[:, 0, :], gf[:], g_ready)
            dve.wait_ge(mod_in, 16)
            links = [dc.n]

            def group(b, half, g, prev=True):
                i = b * HB + half
                dve.wait_ge(a_used, i * NU + LAST_UNIT[g] + 1)
                if g == 0:
                    v.tensor_scalar(y[:, half, :], acc[:, 0, :], call[:], None, ALU.add).then_inc(y0_ready, 1)
                else:
                    e = g - 1
                    dve.wait_ge(gates_in[e], (i + 1) * 16)
                    if g > NG:
                        dve.wait_ge(add_ready, i * E + g - NG)
                    elif prev:
                        dve.wait_ge(add_ready, i * E + min(g - (NG - 1), 0))
                    v.scalar_tensor_tensor(te[:, g % NG, :], acc[:, g % NG, :], negc[:, e:e + 1], gbc[:, e, :],
                                           ALU.add, ALU.mult).then_inc(te_ready, 1)

            def sum_parts(b, half):
                dve.wait_ge(add_ready, (b * HB + half + 1) * E)
                split(yh[:], yl[:], y[:, half, :], yl_ready)

            def outputs(b, half, n):
                i = b * HB + half
                dve.wait_ge(out_ps, i * 2 + n + 1)
                v.tensor_tensor(od[:, 2 * n:2 * n + 2, :].rearrange("p t d -> p t d"),
                                op[:, n, :].rearrange("p (t d) -> p t d", t=2),
                                mod_bc[:, bass.ds(b, 1), 0, :].to_broadcast([P, 2, D]), ALU.mult).then_inc(od_ready, 1)

            def body(b, half, prev, more):
                i = b * HB + half
                first = links[0] if not prev else links[0] + FIRST_LINKS + (i - 1) * DVE_LINKS_B
                dc.base, dc.n = first, 0
                for u in range(NU):
                    s = slot(half, u)
                    for g in range(GROUPS):
                        due = LAST_UNIT[g] + LAG + 1
                        if due == u:
                            group(b, half, g, prev)
                        if due - NU == u and prev:
                            group(*preceding(b, half), g)
                    dve.wait_ge(af_ready, i * NU + u + 1)
                    v.tensor_tensor(al[:, s, :], af[:, s, :], ah[:, s, :].bitcast(fp32), ALU.subtract).then_inc(al_ready, 1)
                    if prev and u == Y_AT:
                        sum_parts(*preceding(b, half))
                    if prev and u == OD_AT:
                        if not (isinstance(i, int) and i == 1):
                            dve.wait_ge(sent, 16 * (i - 1))
                        outputs(*preceding(b, half), 0)
                    if prev and u == OD_AT + 1:
                        outputs(*preceding(b, half), 1)
                    if u in (GX_AT + 1, GX_AT + 2):
                        c = u - GX_AT - 1
                        dve.wait_ge(gxf_ready, i * DC + c + 1)
                        split(gxh[:, c, :], gxl[:, c, :], gxf[:, c, :], gx_ready)
                    if u in (H_AT, H_AT + 1) and more:
                        c = u - H_AT
                        if c == 0:
                            dve.wait_ge(h_in, (i + 2) * 16)
                        dc.link(v.tensor_copy(hh[:, c, :], hin[:, 1 - half, c, :]))
                        ins = v.tensor_tensor(hl[:, c, :], hin[:, 1 - half, c, :], hh[:, c, :].bitcast(fp32), ALU.subtract)
                        if c == DC - 1:
                            ins.then_inc(h_split, 1)
                    if u == GF_AT + 1 and more:
                        dve.wait_ge(gf_ready, i + 2)
                        split(gh[:, 1 - half, :], gl[:, 1 - half, :], gf[:], g_ready)
                assert dc.n == (DVE_LINKS_B if prev and more else FIRST_LINKS if more else dc.n), (dc.n, prev, more)
                dc.base = dc.base + dc.n
                dc.n = 0

            chunks(dve, body)
            for g in range(GROUPS):
                if SPILLS[g]:
                    group(B - 1, HB - 1, g)
            sum_parts(B - 1, HB - 1)
            dve.wait_ge(sent, 16 * (NCH - 1))
            outputs(B - 1, HB - 1, 0)
            outputs(B - 1, HB - 1, 1)

        @block.gpsimd
        def _(pool):
            g = nc.gpsimd
            pool.wait_ge(mod_in, 16)

            def add(b, half, e):
                i = b * HB + half
                if e:
                    pool.wait_ge(add_ready, i * E + e)
                else:
                    pool.wait_ge(y0_ready, i + 1)
                pool.wait_ge(te_ready, i * E + e + 1)
                g.tensor_tensor(y[:, half, :], y[:, half, :], te[:, (e + 1) % NG, :], ALU.add).then_inc(add_ready, 1)

            def rows(b, half):
                return x_all[:, bass.ds((b * HB + half) * TC, TC), :]

            def finish(b, half):
                i = b * HB + half
                hold(pool, xr_ready, i + 1, K.idle["pool"])
                hold(pool, od_ready, 2 * (i + 1), K.idle["pool"])
                g.tensor_tensor(od[:], od[:], rows(b, half), ALU.add).then_inc(of_ready, 1)

            def residual(b, half):
                g.tensor_tensor(rows(b, half), rows(b, half),
                                mod_bc[:, bass.ds(b, 1), 1, :].to_broadcast([P, TC, D]), ALU.add).then_inc(xr_ready, 1)

            def body(b, half, prev, more):
                if prev:
                    for e in range(E):
                        if SPILLS[e + 1]:
                            add(*preceding(b, half), e)
                own = [e for e in range(E) if not SPILLS[e + 1]]
                for e in own[:2]:
                    add(b, half, e)
                if prev:
                    finish(*preceding(b, half))
                residual(b, half)
                for e in own[2:]:
                    add(b, half, e)

            chunks(pool, body)
            for e in range(E):
                if SPILLS[e + 1]:
                    add(B - 1, HB - 1, e)
            finish(B - 1, HB - 1)

        @block.tensor
        def _(pe):
            mm = nc.tensor.matmul

            def down():
                for k in range(DC):
                    last = matmul3(nc, dn[:], (K.downh[:, k, :], K.downl[:, k, :]), (hh[:, k, :], hl[:, k, :]),
                                   k == 0, k == DC - 1)
                last.then_inc(dn_ps, 1)

            def second(b, half, u):
                i, g, s = b * HB + half, UNITS[u][0], slot(half, u)
                pe.wait_ge(al_ready, i * NU + u + 1)
                if u == FIRST_UNIT[g]:
                    if g > NG:
                        pe.wait_ge(te_ready, i * E + g - NG)
                    elif g == NG:
                        pe.wait_ge(y0_ready, i + 1)
                    elif prev_any(i):
                        pe.wait_ge(te_ready, i * E + g - (NG - 1))
                last = matmul3(nc, acc[:, g % NG, :], (w2h[:, u, :], w2l[:, u, :]), (ah[:, s, :], al[:, s, :]),
                               u == FIRST_UNIT[g], u == LAST_UNIT[g])
                last.then_inc(a_used, 1)

            def prev_any(i):
                return not (isinstance(i, int) and i == 0)

            def outputs(b, half, more=True):
                i = b * HB + half
                pe.wait_ge(gx_ready, (i + 1) * DC)
                pe.wait_ge(yl_ready, i + 1)
                pe.wait_ge(gf_ready, i + 2 if more else NCH)
                for t in range(TC):
                    cols, dst = slice(t * P, (t + 1) * P), op[:, t // 2, (t % 2) * D:(t % 2 + 1) * D]
                    for k in range(DC):
                        matmul3(nc, dst, (gxh[:, k, cols], gxl[:, k, cols]), (K.coreh[:, k, :], K.corel[:, k, :]), k == 0, False)
                    last = matmul3(nc, dst, (yh[:, cols], yl[:, cols]), (K.uph[:], K.upl[:]), False, True)
                    if t % 2:
                        last.then_inc(out_ps, 1)

            pe.wait_ge(h_split, 1)
            down()
            for e in range(E):
                last = mm(acc[:, 0, 2 * e:2 * e + 2], K.u0[:, e, :], K.ones2[:], start=True, stop=True)
            last.then_inc(c_ps, 1)
            pe.wait_ge(c_made, 1)

            def body(b, half, prev, more):
                i = b * HB + half
                for u in range(NU):
                    if u == 0:
                        pe.wait_ge(g_ready, i + 1)
                    if prev or u >= NPRE:
                        pe.wait_ge(af_ready, i * NU + u - NPRE + 1)
                    matmul3(nc, pre[:, u % NPRE, :], (w1h[:, u, :], w1l[:, u, :]), (gh[:, half, :], gl[:, half, :]),
                            True, True).then_inc(pre_ps, 1)
                    if u >= LAG:
                        second(b, half, u - LAG)
                    elif prev:
                        second(*preceding(b, half), u - LAG + NU)
                    if u == OUT_AT and prev:
                        outputs(*preceding(b, half))
                    if u == DOWN_AT and more:
                        pe.wait_ge(h_split, i + 2)
                        if prev:
                            pe.wait_ge(od_ready, 2 * i)
                        down()

            chunks(pe, body)
            for u in range(NU - LAG, NU):
                second(B - 1, HB - 1, u)
            outputs(B - 1, HB - 1, False)
    psc.close()


DVE_LINKS_A = 63
DVE_LINKS_B = 6
FIRST_LINKS = 5


_ARGS = {'x': 'L0_attn_hidden_states', 'w_qkv': 'L0_attn_w_qkv', 'b_qkv': 'L0_attn_b_qkv', 'w_out': 'L0_attn_w_out',
         'b_out': 'L0_attn_b_out', 'c': 'L0_c', 'wmod': 'L0_wmod'}
for _n in ('down_w', 'down_b', 'up_w', 'up_b', 'router_w', 'router_b', 'shared_w1', 'shared_b1', 'shared_w2',
           'shared_b2', 'core_w', 'core_b'):
    _ARGS[_n] = 'L0_ffn_' + _n
for _e in range(E):
    for _n in ('w1', 'b1', 'w2', 'b2'):
        _ARGS[f'e{_e}_{_n}'] = f'L0_ffn_e{_e}_{_n}'


def kernel(**inputs):
    import numpy as _np
    import concourse.bacc as _bacc
    from concourse import mybir as _mybir
    from concourse.bass_utils import run_bass_kernel_spmd as _run

    nc = _bacc.Bacc("TRN2", target_bir_lowering=False, num_devices=1)
    arrays, args = {}, {}
    for short, name in _ARGS.items():
        v = _np.ascontiguousarray(inputs[name])
        arrays[f"in_{short}_dram"] = v
        args[short] = nc.dram_tensor(f"in_{short}_dram", v.shape, _mybir.dt.from_np(v.dtype), kind="ExternalInput").ap()
    o = nc.dram_tensor("out_0_dram", (B, S, D), _mybir.dt.float32, kind="ExternalOutput").ap()
    adaln_block(nc, args, o)
    r = _run(nc, [arrays], core_ids=[0])
    return r.results[0]["out_0_dram"]
```

```python
import concourse.bass as bass
from concourse import mybir
from contextlib import ExitStack

B, S, D, L = 4, 1024, 256, 128
P = 128
DC = D // P
TB = S // P
CH = 512
HB = S // CH
NCH = B * HB
TC = CH // P
HID = [128, 256, 384, 512, 128, 256, 384, 512]
E = len(HID)
LN_EPS = 1e-5
COST_LAMBDA = 1e-7
SCORE_SCALE = 1.0 / 16.0
assert SCORE_SCALE * SCORE_SCALE * D == 1.0

UNITS = [(0, 0)] + [(e + 1, j) for e, h in enumerate(HID) for j in range(h // P)]
NU = len(UNITS)
LAST_UNIT = {g: max(u for u, (gg, _) in enumerate(UNITS) if gg == g) for g in range(E + 1)}
FIRST_UNIT = {g: min(u for u, (gg, _) in enumerate(UNITS) if gg == g) for g in range(E + 1)}
GROUPS = E + 1

fp32 = mybir.dt.float32
fp32r = mybir.dt.float32r
u32 = mybir.dt.uint32
ALU = mybir.AluOpType
ACT = mybir.ActivationFunctionType
AX = mybir.AxisListType.X


class Chain:

    def __init__(self, eng, sem, base=0):
        self.eng, self.sem, self.base, self.n = eng, sem, base, 0

    def mark(self, ins):
        self.n += 1
        ins.then_inc(self.sem, 1)
        return self.base + self.n

    def link(self, ins):
        self.eng.wait_ge(self.sem, self.mark(ins))

    def hold(self, ins, idle):
        hold(self.eng, self.sem, self.mark(ins), idle)


def hold(eng, sem, value, idle):
    eng.wait_ge(sem, value)
    eng.sem_inc(idle, 1)


def matmul3(nc, out, stat, mov, start, stop):
    (sh, sl), (mh, ml) = stat, mov
    nc.tensor.matmul(out, sh, mh, start=start, stop=False)
    nc.tensor.matmul(out, sh, ml, start=False, stop=False)
    return nc.tensor.matmul(out, sl, mh, start=False, stop=stop)


class Kept:
    pass


class Norm:

    def __init__(self, stat, mv, ve, rstd, nmr):
        self.stat, self.mv, self.ve, self.rstd, self.nmr = stat, mv, ve, rstd, nmr


def adaln_block(nc, a, out):
    ctx = ExitStack()
    attn = ExitStack()
    K = Kept()
    K.hf_dram = nc.dram_tensor("hf_dram", (NCH, P, DC, CH), fp32, kind="Internal").ap()
    K.gates_dram = nc.dram_tensor("gates_dram", (NCH, TC, E, P), fp32, kind="Internal").ap()
    K.rows_dram = nc.dram_tensor("rows_dram", (B, 4, D), fp32, kind="Internal").ap()
    with ctx, attn:
        def keep(name, shape, dt=fp32, c=ctx):
            return c.enter_context(nc.sbuf_tensor(name, shape, dt))

        K.sems = lambda *names: [ctx.enter_context(nc.semaphore(n)) for n in names]
        K.idle = {}
        for e in ("dve", "pool", "pe", "sp"):
            K.idle[e], = K.sems("idle_" + e)

        K.x_all = keep("x_all", [P, B * TB, D])
        K.w1h = keep("w1h", [P, NU, P], fp32r)
        K.w1l = keep("w1l", [P, NU, P], fp32r)
        K.w2h = keep("w2h", [P, NU, L], fp32r)
        K.w2l = keep("w2l", [P, NU, L], fp32r)
        K.downh = keep("downh", [P, DC, L], fp32r)
        K.downl = keep("downl", [P, DC, L], fp32r)
        K.coreh = keep("coreh", [P, DC, D], fp32r)
        K.corel = keep("corel", [P, DC, D], fp32r)
        K.uph = keep("uph", [P, D], fp32r)
        K.upl = keep("upl", [P, D], fp32r)
        K.b1c = keep("b1c", [P, NU])
        K.a0c = keep("a0c", [P, NU])
        K.b2c = keep("b2c", [P, GROUPS])
        K.u0 = keep("u0", [P, E, L])
        K.downbc = keep("downbc", [P, 1])
        K.ident = keep("ident", [P, P])
        K.ones2 = keep("ones2", [P, 2])
        K.g0h = keep("g0h", [P, CH], fp32r)
        K.g0l = keep("g0l", [P, CH], fp32r)
        K.negc = keep("negc", [P, E])
        K.cb = keep("cb", [P, GROUPS])
        K.call = keep("call", [P, 1])
        K.rb_bc = keep("rb_bc", [P, E])
        K.iota8 = keep("iota8", [P, E])
        K.lt = keep("lt", [P, TB, 2 * E])
        K.lo8 = K.lt[:, :, 0:E]
        K.m8 = keep("m8", [P, TB, E])
        K.ix = keep("ix", [P, TB, E], u32)
        K.ixf = keep("ixf", [P, TB, 2])
        K.d8 = keep("d8", [P, TB, E])
        K.e8 = K.d8
        K.ssum = keep("ssum", [P, TB])
        K.dp = keep("dp", [P, TB])
        K.g0 = keep("g0", [P, TB])
        K.g1 = keep("g1", [P, TB])
        K.k0 = keep("k0", [P, TB, E])
        K.k1 = K.m8
        K.gates = K.k0
        K.gt = keep("gt", [TB * E, P])
        K.Ah = keep("Ah", [P, DC, D], fp32r, attn)
        K.Al = keep("Al", [P, DC, D], fp32r, attn)
        K.Mh = keep("Mh", [P, DC, D], fp32r, attn)
        K.Ml = keep("Ml", [P, DC, D], fp32r, attn)
        K.bqk = keep("bqk", [P, DC], fp32, attn)
        K.xhat = keep("xhat", [P, TB, D], fp32, attn)
        K.halfneg = keep("halfneg", [P, TB], fp32, attn)
        K.norm = {}
        for k in ("P", "F"):
            K.norm[k] = Norm(stat=keep("stat" + k, [P, TB, 6], fp32, attn), mv=keep("mv" + k, [P, TB, 2], fp32, attn),
                             ve=keep("ve" + k, [P, TB], fp32, attn), rstd=keep("rstd" + k, [P, TB], fp32, attn),
                             nmr=keep("nmr" + k, [P, TB], fp32, attn))
        K.modc = keep("modc", [P, B, 4, DC], fp32, attn)
        K.rwp = keep("rwp", [P, DC, P], fp32r, attn)
        K.rwh = keep("rwh", [P, DC, P], fp32r, attn)
        (K.b1_in, K.a0_made, K.x0_in, K.x_in, K.rows_stored, K.xvar_ready, K.xrstd_ready, K.xshift_ready, K.xhat_ready,
         K.lt_read, K.d_ready, K.e_ready, K.gates_ready, K.gt_ps, K.gt_made, K.gt_stored,
         K.h_split, K.dn_ps, K.gf_ready, K.g_ready, K.c_ps, K.c_made) = K.sems(
            "b1_in", "a0_made", "x0_in", "x_in", "rows_stored", "xvar_ready", "xrstd_ready", "xshift_ready", "xhat_ready",
            "lt_read", "d_ready", "e_ready", "gates_ready", "gt_ps", "gt_made", "gt_stored",
            "h_split", "dn_ps", "gf_ready", "g_ready", "c_ps", "c_made")
        prepare(nc, a, K)
        attention(nc, a, K, attn)
        attn.close()
        experts(nc, out, K, ctx)


def aggregate(v, dc, n, lo, hi, sem):
    for t in range(lo, hi):
        last = v.bn_aggr(n.mv[:, t, :], n.stat[:, t, :])
    dc.link(last)
    v.tensor_scalar(n.ve[:, lo:hi], n.mv[:, lo:hi, 1], LN_EPS, None, ALU.add).then_inc(sem, 1)


def shift(v, n, lo, hi, sem):
    v.scalar_tensor_tensor(n.nmr[:, lo:hi], n.mv[:, lo:hi, 0], -1.0, n.rstd[:, lo:hi], ALU.mult, ALU.mult).then_inc(sem, 1)


def normalise(nc, n, dst, t, src, sem):
    nc.scalar.activation(dst, src, ACT.Identity, scale=n.rstd[:, t:t + 1], bias=n.nmr[:, t:t + 1]).then_inc(sem, 1)


def route(v, dve, dc, K, f, part):
    every = [P, TB, E]
    if part == 0:
        dve.wait_ge(K.lt_read, f + 2)
        dc.link(v.tensor_tensor(K.lo8, K.lt[:, :, 0:E], K.lt[:, :, E:2 * E], ALU.add))
        dc.hold(v.tensor_tensor(K.lo8, K.lo8, K.rb_bc[:].unsqueeze(1).to_broadcast(every), ALU.add), K.idle["dve"])
        for t in range(TB):
            last = v.max(K.m8[:, t, :], K.lo8[:, t, :])
        dc.link(last)
        v.tensor_tensor(K.d8[:], K.m8[:], K.m8[:, :, 0:1].to_broadcast(every), ALU.subtract).then_inc(K.d_ready, 1)
        for t in range(TB):
            last = v.max_index(K.ix[:, t, :], K.m8[:, t, :], K.lo8[:, t, :])
        dc.link(last)
        dc.link(v.tensor_copy(K.ixf[:], K.ix[:, :, 0:2]))
    elif part == 1:
        dve.wait_ge(K.e_ready, f * 2 + 1)
        dc.link(v.reduce_sum(K.ssum[:], K.e8[:], AX))
        dc.link(v.reciprocal(K.ssum[:], K.ssum[:]))
        dc.link(v.tensor_tensor(K.dp[:], K.e8[:, :, 1], K.e8[:, :, 0], ALU.subtract))
        v.tensor_tensor(K.dp[:], K.dp[:], K.ssum[:], ALU.mult).then_inc(K.d_ready, 1)
        iota = K.iota8[:].unsqueeze(1).to_broadcast(every)
        v.tensor_tensor(K.k0[:], iota, K.ixf[:, :, 0:1].to_broadcast(every), ALU.is_equal)
        dc.link(v.tensor_tensor(K.k1[:], iota, K.ixf[:, :, 1:2].to_broadcast(every), ALU.is_equal))
    else:
        dve.wait_ge(K.e_ready, f * 2 + 2)
        dc.link(v.tensor_scalar(K.g0[:], K.g1[:], 1.0, None, ALU.add))
        dc.link(v.reciprocal(K.g0[:], K.g0[:]))
        dc.link(v.tensor_tensor(K.g1[:], K.g1[:], K.g0[:], ALU.mult))
        v.tensor_tensor(K.k0[:], K.k0[:], K.g0[:].unsqueeze(2).to_broadcast(every), ALU.mult)
        dc.link(v.tensor_tensor(K.k1[:], K.k1[:], K.g1[:].unsqueeze(2).to_broadcast(every), ALU.mult))
        v.tensor_tensor(K.gates[:], K.k0[:], K.k1[:], ALU.add).then_inc(K.gates_ready, 1)


def route_exp(nc, act, K, f, part):
    dst, src = ((K.e8, K.d8), (K.g1, K.dp))[part]
    act.wait_ge(K.d_ready, f * 2 + part + 1)
    nc.scalar.activation(dst[:], src[:], ACT.Exp).then_inc(K.e_ready, 1)


def turn_gates(nc, pe, K, f, dst):
    hold(pe, K.gates_ready, f + 1, K.idle["pe"])
    nc.tensor.transpose(dst, K.gates[:].rearrange("p t e -> p (t e)"), K.ident[:]).then_inc(K.gt_ps, 1)


def store_gates(act, K, f):
    act.wait_ge(K.gt_made, f + 1)
    act.dma_start(K.gates_dram[bass.ds(f * HB, HB)].rearrange("h t e p -> (h t e) p"),
                  K.gt[:]).then_inc(K.gt_stored, 16)


def down(nc, K, dst, high, low):
    for k in range(DC):
        last = matmul3(nc, dst, (K.downh[:, k, :], K.downl[:, k, :]), (high(k), low(k)), k == 0, k == DC - 1)
    last.then_inc(K.dn_ps, 1)


def prepare(nc, a, K):
    setup = ExitStack()
    with setup:
        def sbt(name, shape, dt=fp32):
            return setup.enter_context(nc.sbuf_tensor(name, shape, dt))

        wqkv = sbt("wqkv", [P, 3 * DC, D])
        wout = sbt("wout", [P, DC, D])
        woT = sbt("woT", [P, DC, D])
        wmod = sbt("wmod", [P, DC, 6 * D])
        crow = sbt("crow", [B, D])
        sig = sbt("sig", [B, D])
        sc = sbt("sc_rows", [B, D])
        scT = sbt("scT", [P, DC, B])
        bqc = sbt("bqc", [P, DC, 1])
        bvc = sbt("bvc", [P, DC, 1])
        bvb = sbt("bvb", [P, DC, P])
        bo_bc = sbt("bo_bc", [P, D])
        bvo_bc = sbt("bvo_bc", [P, D])
        upb = sbt("upb", [B, D])
        coreb = sbt("coreb", [B, D])
        rwraw = sbt("rwraw", [P, DC, E])
        rbraw = sbt("rbraw", [P, E])
        grow = sbt("grow", [B, 4, D])
        sgn = sbt("sgn", [B, 2, D])
        bank = [setup.enter_context(nc.psum_tensor(f"bank{k}", [P, 512], fp32)) for k in range(8)]

        (wq_in, wo_in, c_in, wmodA_in, wmodB_in, rows_in, cols_in, rw_in, id_made, wo_turned, woT_made,
         fold_ps, fold_made, sc_made, sc_turned, scT_made, bvb_made, bias_ps, brow_ps, modA_ps, modB_ps, 
         g_ps, grow_made, sig_made, dve_s, pool_s) = K.sems(
            "wq_in", "wo_in", "c_in", "wmodA_in", "wmodB_in", "rows_in", "cols_in", "rw_in", "id_made",
            "wo_turned", "woT_made", "fold_ps", "fold_made", "sc_made", "sc_turned", "scT_made", "bvb_made",
            "bias_ps", "brow_ps", "modA_ps", "modB_ps", "g_ps", "grow_made", "sig_made", "dve_s", "pool_s")

        with nc.Block() as block:
            @block.sync
            def _(sp):
                wm = a["wmod"].rearrange("(c p) n -> p c n", p=P)
                sp.dma_start(wqkv[:], a["w_qkv"].rearrange("(c p) i -> p c i", p=P)).then_inc(wq_in, 16)
                sp.dma_start(wmod[:, :, 0:3 * D], wm[:, :, 0:3 * D]).then_inc(wmodA_in, 16)
                sp.dma_start(K.x_all[:, 0:TB, :], a["x"][0].rearrange("(p t) d -> p t d", t=TB)).then_inc(K.x0_in, 16)
                sp.dma_start(wmod[:, :, 3 * D:6 * D], wm[:, :, 3 * D:6 * D]).then_inc(wmodB_in, 16)
                for b in range(1, B):
                    sp.dma_start(K.x_all[:, b * TB:(b + 1) * TB, :],
                                 a["x"][b].rearrange("(p t) d -> p t d", t=TB)).then_inc(K.x_in, 16)
                sp.wait_ge(grow_made, 1)
                sp.dma_start(K.rows_dram, grow[:]).then_inc(K.rows_stored, 16)

            @block.gpsimd
            def _(pool):
                g = nc.gpsimd
                pc = Chain(pool, pool_s)
                pc.link(g.memset(K.ident[:], 0.0))
                g.affine_select(out=K.ident[:], in_=K.ident[:], compare_op=ALU.not_equal, fill=1.0,
                                base=0, pattern=[[-1, P]], channel_multiplier=1).then_inc(id_made, 1)
                pool.dma_start(rwraw[:], a["router_w"].rearrange("(c p) e -> p c e", p=P)).then_inc(rw_in, 16)
                pool.dma_start(rbraw[:], a["router_b"].partition_broadcast(P)).then_inc(rw_in, 16)
                pool.dma_start(upb[:], a["up_b"].partition_broadcast(B)).then_inc(rows_in, 16)
                pool.dma_start(coreb[:], a["core_b"].partition_broadcast(B)).then_inc(rows_in, 16)
                for e in range(E):
                    g.memset(K.iota8[:, e:e + 1], float(e))
                g.memset(K.ones2[:], 1.0)
                pc.link(g.memset(K.u0[:], 0.0))
                pc.link(g.memset(K.halfneg[:], -0.5))
                pc.link(g.memset(K.rwp[:].bitcast(fp32), 0.0))
                pc.link(g.memset(K.rwh[:].bitcast(fp32), 0.0))
                pool.wait_ge(rw_in, 32)
                g.tensor_scalar(K.rwp[:, :, 0:E], rwraw[:], 1.0, 0.0, ALU.mult, ALU.add)
                pc.link(g.tensor_scalar(K.rwh[:, :, 0:E], rwraw[:], 1.0, 0.0, ALU.mult, ALU.add))
                g.tensor_tensor(K.rwp[:, :, E:2 * E], rwraw[:], K.rwh[:, :, 0:E].bitcast(fp32), ALU.subtract)
                for e, h in enumerate(HID):
                    g.tensor_scalar(K.rb_bc[:, e:e + 1], rbraw[:, e:e + 1], 1.0, -COST_LAMBDA * (2 * L * h), ALU.mult, ALU.add)
                n = K.norm["P"]
                pool.wait_ge(K.xvar_ready, 1)
                g.tensor_tensor(n.rstd[:], n.ve[:], K.halfneg[:], ALU.pow).then_inc(K.xrstd_ready, 1)

            @block.scalar
            def _(act):
                act.dma_start(crow[:], a["c"]).then_inc(c_in, 16)
                act.dma_start(wout[:], a["w_out"].rearrange("(c p) o -> p c o", p=P)).then_inc(wo_in, 16)
                act.dma_start(bqc[:], a["b_qkv"][0:D].rearrange("(c p o) -> p c o", p=P, o=1),
                              allow_slow_non_contiguous=True).then_inc(cols_in, 16)
                act.dma_start(bvc[:], a["b_qkv"][2 * D:3 * D].rearrange("(c p o) -> p c o", p=P, o=1),
                              allow_slow_non_contiguous=True).then_inc(cols_in, 16)
                act.dma_start(bo_bc[:], a["b_out"].partition_broadcast(P)).then_inc(cols_in, 16)
                act.wait_ge(c_in, 16)
                nc.scalar.activation(sig[:], crow[:], ACT.Exp, scale=-1.0).then_inc(sig_made, 1)
                act.dma_start(K.b1c[:, 0:1], a["shared_b1"].rearrange("(p n) -> p n", n=1)).then_inc(K.b1_in, 16)
                act.dma_start(K.b2c[:, 0:1], a["shared_b2"].rearrange("(p n) -> p n", n=1)).then_inc(K.b1_in, 16)
                act.dma_start(K.downbc[:], a["down_b"].rearrange("(p n) -> p n", n=1)).then_inc(K.b1_in, 16)
                for e in range(E):
                    n, u = HID[e] // P, FIRST_UNIT[e + 1]
                    act.dma_start(K.b1c[:, u:u + n], a[f"e{e}_b1"].rearrange("(p n) -> p n", n=n)).then_inc(K.b1_in, 16)
                    act.dma_start(K.b2c[:, e + 1:e + 2], a[f"e{e}_b2"].rearrange("(p n) -> p n", n=1)).then_inc(K.b1_in, 16)
                act.wait_ge(K.xshift_ready, 1)
                for t in range(TB):
                    normalise(nc, K.norm["P"], K.xhat[:, t, :], t, K.x_all[:, t, :], K.xhat_ready)
                act.wait_ge(K.b1_in, 16 * (3 + 2 * E))
                nc.scalar.activation(K.a0c[:], K.b1c[:], ACT.Gelu).then_inc(K.a0_made, 1)

            @block.vector
            def _(dve):
                dc = Chain(dve, dve_s)
                v = nc.vector
                dve.wait_ge(sig_made, 1)
                dc.link(v.tensor_scalar(sig[:], sig[:], 1.0, None, ALU.add))
                dc.link(v.reciprocal(sig[:], sig[:]))
                v.tensor_tensor(sc[:], crow[:], sig[:], ALU.mult).then_inc(sc_made, 1)
                dve.wait_ge(sc_turned, 1)
                v.tensor_copy(scT[:].rearrange("p k b -> p (k b)"), bank[6][:, 0:DC * B]).then_inc(scT_made, 1)
                for k in range(DC):
                    dve.wait_ge(wo_turned, k + 1)
                    v.tensor_copy(woT[:, k, :], bank[k][:, 0:D]).then_inc(woT_made, 1)
                dve.wait_ge(K.x0_in, 16)
                for t in range(TB):
                    last = v.bn_stats(K.norm["P"].stat[:, t, :], K.x_all[:, t, :])
                dc.link(last)
                aggregate(v, dc, K.norm["P"], 0, TB, K.xvar_ready)
                for n, (hi, lo) in enumerate(((K.Ah, K.Al), (K.Mh, K.Ml))):
                    for k in range(DC):
                        dve.wait_ge(fold_ps, n * DC + k + 1)
                        dc.link(v.tensor_copy(hi[:, k, :], bank[2 + n * DC + k][:, 0:D]))
                        v.tensor_tensor(lo[:, k, :], bank[2 + n * DC + k][:, 0:D], hi[:, k, :].bitcast(fp32), ALU.subtract).then_inc(fold_made, 1)
                    if n == 0:
                        dve.wait_ge(K.xrstd_ready, 1)
                        shift(v, K.norm["P"], 0, TB, K.xshift_ready)
                dve.wait_ge(cols_in, 48)
                v.tensor_copy(bvb[:], bvc[:].to_broadcast([P, DC, P])).then_inc(bvb_made, 1)
                def columns_read(n, sem):
                    dve.wait_ge(sem, 1)
                    for w in (0, 1):
                        for k in range(DC):
                            src = bank[n][:, (w * DC + k) * B:(w * DC + k + 1) * B]
                            v.tensor_scalar(K.modc[:, :, 2 * n + w, k], src, float(w), None, ALU.add)

                dve.wait_ge(g_ps, 1)
                g, src = grow[:, 0:2, :].rearrange("b n d -> b (n d)"), bank[2][0:B, :]
                s = sgn[:].rearrange("b n d -> b (n d)")
                v.tensor_scalar(s, src, 0.0, 2.0, ALU.is_ge, ALU.mult)
                dc.link(v.tensor_scalar(g, src, -1.0, 0.25, ALU.mult, ALU.max))
                dc.link(v.tensor_tensor(g, src, g, ALU.max))
                dc.link(v.tensor_scalar(s, s, -1.0, None, ALU.add))
                dc.link(v.tensor_tensor(g, g, s, ALU.mult))
                dve.wait_ge(rows_in, 32)
                dc.link(v.tensor_tensor(grow[:, 2, :], upb[:], coreb[:], ALU.add))
                v.tensor_tensor(grow[:, 2, :], grow[:, 2, :], grow[:, 1, :], ALU.mult)
                columns_read(0, modA_ps)
                columns_read(1, modB_ps)
                dve.wait_ge(bias_ps, 1)
                v.tensor_copy(K.bqk[:], bank[6][:, 16:16 + 2 * DC:2])
                dve.wait_ge(brow_ps, 1)
                dc.link(v.tensor_tensor(bvo_bc[:], bank[7][:, 0:D], bo_bc[:], ALU.add))
                v.tensor_tensor(grow[:, 3, :], grow[:, 0, :], bvo_bc[0:B, :], ALU.mult).then_inc(grow_made, 1)

            @block.tensor
            def _(pe):
                mm = nc.tensor.matmul

                def pair(dst, lhs, rhs):
                    for o in range(DC):
                        last = mm(dst, lhs(o), rhs(o), start=(o == 0), stop=(o == DC - 1))
                    return last

                pe.wait_ge(id_made, 1)
                pe.wait_ge(wo_in, 16)
                for oc in range(DC):
                    for jc in range(DC):
                        last = nc.tensor.transpose(bank[oc][:, jc * P:(jc + 1) * P],
                                                   wout[:, jc, oc * P:(oc + 1) * P], K.ident[:])
                    last.then_inc(wo_turned, 1)
                pe.wait_ge(sc_made, 1)
                for k in range(DC):
                    last = nc.tensor.transpose(bank[6][:, k * B:(k + 1) * B], sc[:, k * P:(k + 1) * P], K.ident[0:B, 0:B])
                last.then_inc(sc_turned, 1)
                pe.wait_ge(wq_in, 16)
                for k in range(DC):
                    pair(bank[2 + k][:, 0:D], lambda o: wqkv[:, o, k * P:(k + 1) * P],
                         lambda o: wqkv[:, DC + o, :]).then_inc(fold_ps, 1)
                pe.wait_ge(woT_made, DC)
                for k in range(DC):
                    pair(bank[4 + k][:, 0:D], lambda o: wqkv[:, 2 * DC + o, k * P:(k + 1) * P],
                         lambda o: woT[:, o, :]).then_inc(fold_ps, 1)
                def columns(dst, segs, sem):
                    for w, seg in enumerate(segs):
                        for k in range(DC):
                            last = pair(dst[:, (w * DC + k) * B:(w * DC + k + 1) * B],
                                        lambda o: wmod[:, o, seg * D + k * P:seg * D + (k + 1) * P],
                                        lambda o: scT[:, o, :])
                    last.then_inc(sem, 1)

                pe.wait_ge(scT_made, 1)
                pe.wait_ge(wmodA_in, 16)
                pe.wait_ge(wmodB_in, 16)
                pe.wait_ge(fold_made, 1)
                for n, seg in enumerate((2, 5)):
                    last = pair(bank[2][0:B, n * D:(n + 1) * D], lambda o: scT[:, o, :],
                                lambda o: wmod[:, o, seg * D:(seg + 1) * D])
                last.then_inc(g_ps, 1)
                columns(bank[0], (0, 1), modA_ps)
                columns(bank[1], (3, 4), modB_ps)
                pe.wait_ge(cols_in, 48)
                for k in range(DC):
                    last = pair(bank[6][:, 16 + 2 * k:17 + 2 * k], lambda o: wqkv[:, DC + o, k * P:(k + 1) * P],
                                lambda o: bqc[:, o, :])
                last.then_inc(bias_ps, 1)
                pe.wait_ge(bvb_made, 1)
                pair(bank[7][:, 0:D], lambda o: bvb[:, o, :], lambda o: woT[:, o, :]).then_inc(brow_ps, 1)


def attention(nc, a, K, attn):
    def sbt(name, shape, dt=fp32):
        return attn.enter_context(nc.sbuf_tensor(name, shape, dt))

    x_all, ident, bqk, modc = K.x_all, K.ident, K.bqk, K.modc
    xhat, norm = K.xhat, K.norm
    ga_bc = sbt("ga_bc", [P, B, D])
    gv_bc = sbt("gv_bc", [P, B, D])
    hfull = sbt("hfull", [P, 2, CH])
    hTh = sbt("hTh", [P, DC, S], fp32r)
    hTl = sbt("hTl", [P, DC, S], fp32r)
    qh = sbt("qh", [P, DC, S], fp32r)
    ql = sbt("ql", [P, DC, S], fp32r)
    vh = sbt("vh", [P, TB, D], fp32r)
    vl = sbt("vl", [P, TB, D], fp32r)
    prob = sbt("prob", [P, 2, S])
    pTh = sbt("pTh", [P, TB, P], fp32r)
    pTl = sbt("pTl", [P, TB, P], fp32r)
    hff = (hfull, sbt("hff", [P, DC, CH]))
    fh = sbt("fh", [P, DC, CH], fp32r)
    fl = sbt("fl", [P, DC, CH], fp32r)
    cur = sbt("cur", [P, 2, 2, DC])
    mx = sbt("mx", [P, TB])
    negm = sbt("negm", [P, TB])
    rsum = sbt("rsum", [P, TB])
    rinv = sbt("rinv", [P, TB])
    ot = sbt("ot", [P, D])
    lg = sbt("lg", [2 * E, CH])
    stage = sbt("stage", [P, 2, 512])
    wtmp = sbt("wtmp", [P, P])

    psc = ExitStack()
    sc = psc.enter_context(nc.psum_tensor("sc", [P, 2, S], fp32))
    ptp = psc.enter_context(nc.psum_tensor("ptp", [P, S], fp32))
    ob = [psc.enter_context(nc.psum_tensor(f"ob{k}", [P, 512], fp32)) for k in range(2)]
    quad = [sc[:, n // 2, (n % 2) * CH:(n % 2 + 1) * CH] for n in range(4)]
    GATES_TILE = 3
    gt_bank = ob[GATES_TILE % 2][0:TB * E, D:D + P]
    lg_bank = (quad[0], ptp[:, 0:512])
    c_cols = ptp[:, CH:CH + 2 * E]
    c_once = c_cols.rearrange("p (e two) -> p e two", two=2)[:, :, 0]
    vbank = [ptp[:, 0:512], ptp[:, 512:1024], ob[0][:], ob[1][:]]

    w_in = K.sems("w_in0", "w_in1")
    turned_halves = [(pTh[:, n * TC:(n + 1) * TC, :].rearrange("p t q -> p (t q)"),
                      pTl[:, n * TC:(n + 1) * TC, :].rearrange("p t q -> p (t q)"),
                      ptp[:, n * CH:(n + 1) * CH]) for n in range(2)]
    first_h_in, = K.sems("first_h_in")
    first_h = prob[:, 0, :].rearrange("p (c t) -> p c t", c=DC)
    first_high, first_low = qh[:, :, 0:CH], ql[:, :, 0:CH]
    first_g = prob[:, 1, 0:CH]
    stored = K.sems("stored0", "stored1")
    (ga_in, gv_in, d_s, p_s, w_taken, fvar_ready, frstd_ready, fshift_ready, xhatF_ready, turned,
     fturned, hfull_ready, hff_ready, ht_ready, f_ready, q_ps, qh_ready, ql_ready, v_ps, vh_ready, vl_ready,
     sc_ready, negm_ready, p_ready, pt_ready, pth_ready, ptl_ready, pv_ready, xp_ready, x1_ready,
     lg_ps, lg_ready, lt_ready, cur_ready) = K.sems(
        "ga_in", "gv_in", "d_s", "p_s", "w_taken", "fvar_ready", "frstd_ready", "fshift_ready",
        "xhatF_ready", "turned", "fturned", "hfull_ready", "hff_ready", "ht_ready", "f_ready", "q_ps",
        "qh_ready", "ql_ready", "v_ps", "vh_ready", "vl_ready", "sc_ready", "negm_ready", "p_ready",
        "pt_ready", "pth_ready", "ptl_ready", "pv_ready", "xp_ready", "x1_ready", "lg_ps",
        "lg_ready", "lt_ready", "cur_ready")
    xvar_ready, xrstd_ready, xshift_ready, xhat_ready, lt_read = (
        K.xvar_ready, K.xrstd_ready, K.xshift_ready, K.xhat_ready, K.lt_read)

    pieces = []
    for e in range(E):
        n, u = HID[e] // P, FIRST_UNIT[e + 1]
        pieces.append((a[f"e{e}_w1"].rearrange("l (q n) -> l q n", n=n), (P, n), True,
                       K.w1h[:, u:u + n, :], K.w1l[:, u:u + n, :], 1.0, None))
        pieces.append((a[f"e{e}_w2"].rearrange("(p n) l -> p n l", n=n), (n, L), False,
                       K.w2h[:, u:u + n, :], K.w2l[:, u:u + n, :], 1.0, e))
    one = lambda w: w.rearrange("p (n l) -> p n l", n=1)
    pieces.append((one(a["shared_w1"]), (1, P), False, K.w1h[:, 0:1, :], K.w1l[:, 0:1, :], 1.0, None))
    pieces.append((one(a["shared_w2"]), (1, L), False, K.w2h[:, 0:1, :], K.w2l[:, 0:1, :], 0.1, None))
    pieces.append((a["down_w"].rearrange("(c p) l -> p c l", p=P), (DC, L), False, K.downh[:], K.downl[:], 1.0, None))
    pieces.append((one(a["up_w"]), (1, D), False, K.uph[:].unsqueeze(1), K.upl[:].unsqueeze(1), 1.0, None))
    pieces.append((a["core_w"].rearrange("(c p) n -> p c n", p=P), (DC, D), False, K.coreh[:], K.corel[:], 1.0, None))
    PER_BATCH = -(-len(pieces) // B)

    def staged(k):
        s0, s1 = pieces[k][1]
        return stage[:, k % 2, 0:s0 * s1].rearrange("p (x y) -> p x y", x=s0)

    def sequences(eng, boundary, tiles):
        boundary(-1, False, True)
        tiles(0, False, True)
        with eng.Fori(0, B - 2) as f:
            boundary(f, True, True)
            tiles(f + 1, True, True)
        boundary(B - 2, True, True)
        tiles(B - 1, True, False)
        boundary(B - 1, True, False)

    def row(t):
        return x_all[:, bass.ds(t, 1), :].rearrange("p a d -> p (a d)")

    with nc.Block() as block:
        @block.sync
        def _(sp):
            sp.wait_ge(K.rows_stored, 16)
            sp.dma_start(gv_bc[:], K.rows_dram[:, 3, :].partition_broadcast(P)).then_inc(gv_in, 16)
            sp.dma_start(ga_bc[:], K.rows_dram[:, 0, :].partition_broadcast(P)).then_inc(ga_in, 16)
            for k, piece in enumerate(pieces):
                if k >= 2:
                    sp.wait_ge(w_taken, k - 1)
                sp.dma_start(staged(k), piece[0]).then_inc(w_in[k % 2], 16)
            sp.wait_ge(stored[0], (B - 1) * 16)
            sp.wait_ge(pt_ready, 2 * (B * TB - 1))
            sp.dma_start(first_h, K.hf_dram[0]).then_inc(first_h_in, 16)

        @block.gpsimd
        def _(pool):
            g = nc.gpsimd
            pc = Chain(pool, p_s)

            def split_piece(k):
                src, shape, turn, hi, lo, scale, expert = pieces[k]
                pool.wait_ge(w_in[k % 2], 16 * (k // 2 + 1))
                raw = staged(k)
                if turn:
                    raw = raw.rearrange("p q n -> p n q")
                if scale != 1.0:
                    pc.link(g.tensor_scalar(wtmp[:].unsqueeze(1), raw, scale, 0.0, ALU.mult, ALU.add))
                    raw = wtmp[:].unsqueeze(1)
                pc.link(g.tensor_scalar(hi, raw, 1.0, 0.0, ALU.mult, ALU.add))
                pc.link(g.tensor_tensor(lo, raw, hi.bitcast(fp32), ALU.subtract))
                if expert is not None:
                    for j in range(shape[0]):
                        u = FIRST_UNIT[expert + 1] + j
                        pc.link(g.tensor_scalar(wtmp[:], raw[:, j, :], K.a0c[:, u:u + 1], 0.0, ALU.mult, ALU.add))
                        pc.link(g.tensor_tensor(K.u0[:, expert, :], K.u0[:, expert, :], wtmp[:], ALU.add))
                pool.sem_inc(w_taken, 1)

            def inverse_root(n, cols, seen, count, made):
                pool.wait_ge(seen, count)
                g.tensor_tensor(n.rstd[:, cols], n.ve[:, cols], K.halfneg[:, cols], ALU.pow).then_inc(made, 1)

            every, first, second = slice(0, TB), slice(0, TC), slice(TC, TB)
            pool.wait_ge(K.a0_made, 1)
            pool.wait_ge(gv_in, 16)
            for b in range(B):
                pool.wait_ge(xhat_ready, (b + 1) * TB)
                rows = x_all[:, b * TB:(b + 1) * TB, :]
                g.tensor_tensor(rows, rows, gv_bc[:, b:b + 1, :].to_broadcast([P, TB, D]), ALU.add).then_inc(xp_ready, 1)
                for k in range(b * PER_BATCH, min(len(pieces), (b + 1) * PER_BATCH)):
                    split_piece(k)
                if b + 1 < B:
                    inverse_root(norm["P"], every, xvar_ready, b + 2, xrstd_ready)
                inverse_root(norm["F"], first, fvar_ready, 2 * b + 1, frstd_ready)
                inverse_root(norm["F"], second, fvar_ready, 2 * b + 2, frstd_ready)

        @block.vector
        def _(dve):
            v = nc.vector
            idle = K.idle["dve"]
            dc = Chain(dve, d_s)

            def split_keys(p, half):
                for c in range(DC):
                    n = 2 * half + c
                    cols = slice(half * CH, (half + 1) * CH)
                    dve.wait_ge(hfull_ready, p * 4 + n + 1)
                    dc.link(v.tensor_copy(hTh[:, c, cols], hfull[:, c, :]))
                    v.tensor_tensor(hTl[:, c, cols], hfull[:, c, :], hTh[:, c, cols].bitcast(fp32),
                                    ALU.subtract).then_inc(ht_ready, 1)

            def split_ffn(f, half):
                for c in range(DC):
                    if half and c == 0:
                        dve.wait_ge(lg_ps, f * HB + half)
                    dve.wait_ge(hff_ready, f * 4 + 2 * half + c + 1)
                    dc.link(v.tensor_copy(fh[:, c, :], hff[half][:, c, :]))
                    v.tensor_tensor(fl[:, c, :], hff[half][:, c, :], fh[:, c, :].bitcast(fp32), ALU.subtract).then_inc(f_ready, 1)

            def row_max(b, t):
                dve.wait_ge(sc_ready, b * TB + t + 1)
                dc.link(v.reduce_max(mx[:, t:t + 1], sc[:, t % 2, :], AX))
                v.tensor_scalar(negm[:, t:t + 1], mx[:, t:t + 1], -SCORE_SCALE, None, ALU.mult).then_inc(negm_ready, 1)

            def residual(b, t, gates_too):
                dve.wait_ge(pv_ready, b * TB + t + 1)
                dc.link(v.reciprocal(rinv[:, t:t + 1], rsum[:, t:t + 1]))
                if gates_too:
                    v.tensor_copy(K.gt[:], gt_bank).then_inc(K.gt_made, 1)
                dc.link(v.scalar_tensor_tensor(ot[:], ob[t % 2][:, 0:D], rinv[:, t:t + 1],
                                               ga_bc[:, bass.ds(b, 1), :].rearrange("p a d -> p (a d)"), ALU.mult, ALU.mult))
                v.tensor_tensor(row(b * TB + t), ot[:], row(b * TB + t), ALU.add).then_inc(x1_ready, 1)

            def stats1(b, t):
                hold(dve, x1_ready, b * TB + t + 1, idle)
                return v.bn_stats(norm["F"].stat[:, t, :], row(b * TB + t))

            def queries_low(p, n):
                half, c = n // 2, n % 2
                cols = slice(half * CH, (half + 1) * CH)
                dve.wait_ge(qh_ready, p * 4 + n + 1)
                v.scalar_tensor_tensor(ql[:, c, cols], quad[n], bqk[:, c:c + 1], qh[:, c, cols].bitcast(fp32),
                                       ALU.add, ALU.subtract).then_inc(ql_ready, 1)

            def values_low(p, n):
                dve.wait_ge(vh_ready, p * 4 + n + 1)
                pair = slice(2 * n, 2 * n + 2)
                v.tensor_tensor(vl[:, pair, :].rearrange("p t d -> p (t d)"), vbank[n],
                                vh[:, pair, :].rearrange("p t d -> p (t d)").bitcast(fp32), ALU.subtract).then_inc(vl_ready, 1)

            def take_logits(f):
                dve.wait_ge(lt_ready, (f + 1) * HB)
                v.tensor_copy(K.lt[:].rearrange("p t e -> p (t e)"), ob[0][:, 0:TB * 2 * E]).then_inc(lt_read, 1)

            def tiles(b, routed, more):
                nP, nF = norm["P"], norm["F"]
                for t in range(TB):
                    for n, (high, low, bank) in enumerate(turned_halves):
                        dve.wait_ge(pth_ready, 2 * (b * TB + t) + n + 1)
                        v.tensor_tensor(low, bank, high.bitcast(fp32), ALU.subtract).then_inc(ptl_ready, 1)
                    if t + 2 < TB:
                        row_max(b, t + 2)
                    if more and t >= TB - 2:
                        split_keys(b + 1, t - TB + 2)
                    if more and t == TB - 1:
                        queries_low(b + 1, 0)
                        queries_low(b + 1, 1)
                    if t >= 2:
                        stats1(b, t - 2)
                    if t == 1:
                        dve.wait_ge(xp_ready, b + 1)
                    if t:
                        residual(b, t - 1, routed and t - 1 == GATES_TILE)
                    if routed and t < 3:
                        route(v, dve, dc, K, b - 1, t)
                    if more and t < 4:
                        for k in (2 * t, 2 * t + 1):
                            last = v.bn_stats(nP.stat[:, k, :], row((b + 1) * TB + k))
                        if t == 3:
                            dc.hold(last, idle)
                            aggregate(v, dc, nP, 0, TB, xvar_ready)
                    if t == 4:
                        v.tensor_copy(cur[:, 1].unsqueeze(1), modc[:, bass.ds(b, 1), 2:4, :]).then_inc(cur_ready, 1)
                        if more:
                            v.tensor_copy(cur[:, 0].unsqueeze(1), modc[:, bass.ds(b + 1, 1), 0:2, :]).then_inc(cur_ready, 1)
                            dve.wait_ge(xrstd_ready, b + 2)
                            shift(v, nP, 0, TB, xshift_ready)
                    if t == 5:
                        hold(dve, x1_ready, b * TB + 5, idle)
                        aggregate(v, dc, nF, 0, TC, fvar_ready)
                    if t == 6:
                        dve.wait_ge(frstd_ready, 2 * b + 1)
                        shift(v, nF, 0, TC, fshift_ready)
                    if not more and t == 6:
                        dve.wait_ge(first_h_in, 16)
                        dc.link(v.tensor_copy(first_high, first_h))
                        v.tensor_tensor(first_low, first_h, first_high.bitcast(fp32), ALU.subtract).then_inc(K.h_split, 1)
                stats1(b, TB - 2)

            def boundary(f, has_last, has_next):
                p, nP, nF = f + 1, norm["P"], norm["F"]
                if not has_last:
                    v.tensor_copy(cur[:, 0], modc[:, 0, 0:2, :]).then_inc(cur_ready, 1)
                    split_keys(p, 0)
                    split_keys(p, 1)
                    queries_low(p, 0)
                    queries_low(p, 1)
                if has_last:
                    residual(f, TB - 1, False)
                    dc.hold(stats1(f, TB - 1), idle)
                    aggregate(v, dc, nF, TC, TB, fvar_ready)
                if has_next:
                    queries_low(p, 2)
                    queries_low(p, 3)
                if has_last and not has_next:
                    dve.wait_ge(K.c_ps, 1)
                    v.tensor_scalar(K.negc[:], c_once, -1.0, None, ALU.mult)
                    v.tensor_scalar(K.cb[:, 0:1], K.b2c[:, 0:1], 0.1, None, ALU.mult)
                    dc.link(v.tensor_tensor(K.cb[:, 1:], c_once, K.b2c[:, 1:], ALU.add))
                    v.reduce_sum(K.call[:], K.cb[:], AX).then_inc(K.c_made, 1)
                if has_last:
                    dve.wait_ge(frstd_ready, 2 * f + 2)
                    shift(v, nF, TC, TB, fshift_ready)
                if has_last:
                    split_ffn(f, 0)
                if has_next:
                    values_low(p, 0)
                    values_low(p, 1)
                    values_low(p, 2)
                if has_last:
                    split_ffn(f, 1)
                if has_next:
                    values_low(p, 3)
                    row_max(p, 0)
                    row_max(p, 1)
                if has_last and not has_next:
                    dve.wait_ge(K.gf_ready, 1)
                    dc.link(v.tensor_copy(K.g0h[:], first_g))
                    v.tensor_tensor(K.g0l[:], first_g, K.g0h[:].bitcast(fp32), ALU.subtract).then_inc(K.g_ready, 1)
                if has_last:
                    take_logits(f)
                else:
                    dve.sem_inc(lt_read, 1)
                if not has_last:
                    dve.wait_ge(K.x_in, 16 * (B - 1))
                    dve.wait_ge(ga_in, 16)

            boundary(-1, False, True)
            tiles(0, False, True)
            n0 = dc.n
            with dve.Fori(0, B - 2) as f:
                dc.base, dc.n = f * DVE_LINKS_A + n0, 0
                boundary(f, True, True)
                tiles(f + 1, True, True)
                assert dc.n == DVE_LINKS_A, dc.n
            dc.base, dc.n = (B - 2) * DVE_LINKS_A + n0, 0
            boundary(B - 2, True, True)
            tiles(B - 1, True, False)
            boundary(B - 1, True, False)

        @block.scalar
        def _(act):
            sa = nc.scalar.activation

            def softmax(b, t):
                act.wait_ge(negm_ready, b * TB + t + 1)
                if t >= 2:
                    act.wait_ge(pt_ready, 2 * (b * TB + t - 1))
                sa(prob[:, t % 2, :], sc[:, t % 2, :], ACT.Exp, bias=negm[:, t:t + 1], scale=SCORE_SCALE,
                   accum_out=rsum[:, t:t + 1]).then_inc(p_ready, 1)

            def ffn_stored(count):
                for half in range(HB):
                    act.wait_ge(stored[half], count * 16)

            def modulate_keys(p, half):
                if half == 0:
                    act.wait_ge(cur_ready, 2 * p + 1)
                    if not (isinstance(p, int) and p < 2):
                        ffn_stored(p - 1)
                for c in range(DC):
                    n = 2 * half + c
                    act.wait_ge(turned, p * 4 + n + 1)
                    if half:
                        act.wait_ge(ht_ready, p * 4 + c + 1)
                    sa(hfull[:, c, :], quad[n], ACT.Identity, scale=cur[:, 0, 1, c:c + 1],
                       bias=cur[:, 0, 0, c:c + 1]).then_inc(hfull_ready, 1)

            def modulate_ffn(f, half, has_next):
                if half == 0:
                    act.wait_ge(cur_ready, 2 * f + 2)
                    if has_next:
                        act.wait_ge(ht_ready, f * 4 + 8)
                    else:
                        ffn_stored(f)
                for c in range(DC):
                    n = 2 * half + c
                    act.wait_ge(fturned, f * 4 + n + 1)
                    sa(hff[half][:, c, :], quad[n], ACT.Identity, scale=cur[:, 1, 1, c:c + 1],
                       bias=cur[:, 1, 0, c:c + 1]).then_inc(hff_ready, 1)
                act.wait_ge(hff_ready, f * 4 + 2 * half + 2)
                act.dma_start(K.hf_dram[bass.ds(f * HB + half, 1)].rearrange("a p c t -> p (a c) t"), hff[half][:]).then_inc(stored[half], 16)

            def queries_high(p, n):
                half, c = n // 2, n % 2
                act.wait_ge(q_ps, p * 4 + n + 1)
                sa(qh[:, c, half * CH:(half + 1) * CH], quad[n], ACT.Identity, bias=bqk[:, c:c + 1]).then_inc(qh_ready, 1)

            def values_high(p, n):
                act.wait_ge(v_ps, p * 4 + n + 1)
                sa(vh[:, 2 * n:2 * n + 2, :].rearrange("p t d -> p (t d)"), vbank[n], ACT.Copy).then_inc(vh_ready, 1)

            def logits(f, half):
                act.wait_ge(lg_ps, f * HB + half + 1)
                if half:
                    act.wait_ge(lt_ready, f * HB + half)
                sa(lg[:], lg_bank[half][0:2 * E, :], ACT.Copy).then_inc(lg_ready, 1)

            def normalise_next(p, lo, hi):
                act.wait_ge(xshift_ready, p + 1)
                for t in range(lo, hi):
                    normalise(nc, norm["P"], xhat[:, t, :], t, row(p * TB + t), xhat_ready)

            def normalise_ffn(f, half):
                act.wait_ge(fshift_ready, 2 * f + half + 1)
                for t in range(half * TC, (half + 1) * TC):
                    normalise(nc, norm["F"], xhat[:, t, :], t, row(f * TB + t), xhatF_ready)

            def tiles(b, routed, more):
                softmax(b, 0)
                for t in range(TB):
                    for n, (high, low, bank) in enumerate(turned_halves):
                        act.wait_ge(pt_ready, 2 * (b * TB + t) + n + 1)
                        sa(high, bank, ACT.Copy).then_inc(pth_ready, 1)
                    if routed and t in (1, 2):
                        route_exp(nc, act, K, b - 1, t - 1)
                    if more and t >= TB - 2:
                        modulate_keys(b + 1, t - TB + 2)
                    if t + 1 < TB:
                        softmax(b, t + 1)
                    if more and t in (5, 6):
                        normalise_next(b + 1, (t - 5) * TC, (t - 4) * TC)
                    if t == (TB - 1 if more else TB - 2):
                        normalise_ffn(b, 0)
                    if not more and t == TB - 1:
                        modulate_ffn(b, 0, False)
                    if more and t == TB - 1:
                        queries_high(b + 1, 0)
                        queries_high(b + 1, 1)
                    if routed and t == 5:
                        store_gates(act, K, b - 1)
                    if routed and t == TB - 1:
                        act.wait_ge(K.gt_stored, 16 * b)

            def boundary(f, has_last, has_next):
                p = f + 1
                if not has_last:
                    modulate_keys(p, 0)
                    modulate_keys(p, 1)
                    act.wait_ge(K.rows_stored, 16)
                    queries_high(p, 0)
                    queries_high(p, 1)
                if has_next:
                    queries_high(p, 2)
                    queries_high(p, 3)
                if has_last and has_next:
                    modulate_ffn(f, 0, True)
                if has_next:
                    values_high(p, 0)
                    values_high(p, 1)
                if has_last:
                    normalise_ffn(f, 1)
                if has_next:
                    values_high(p, 2)
                if has_last and has_next:
                    logits(f, 0)
                if has_last:
                    modulate_ffn(f, 1, has_next)
                if has_last and not has_next:
                    logits(f, 0)
                    act.wait_ge(K.dn_ps, 1)
                    sa(first_g, vbank[1], ACT.Gelu, bias=K.downbc[:]).then_inc(K.gf_ready, 1)
                if has_next:
                    values_high(p, 3)
                if has_last:
                    logits(f, 1)

            sequences(act, boundary, tiles)
            ffn_stored(B)
            act.wait_ge(K.gt_stored, (B - 1) * 16)

        @block.tensor
        def _(pe):
            mm = nc.tensor.matmul
            idle = K.idle["pe"]

            def ht(c, cols):
                return hTh[:, c, cols], hTl[:, c, cols]

            def turn(src, half, wait_sem, count, sem):
                for c in range(DC):
                    for t in range(TC):
                        if c == 0:
                            pe.wait_ge(wait_sem, count - TC + t + 1)
                        last = nc.tensor.transpose(quad[2 * half + c][:, t * P:(t + 1) * P],
                                                   src[:, t, c * P:(c + 1) * P], ident[:])
                    last.then_inc(sem, 1)

            def turn_keys(p, half):
                turn(xhat[:, half * TC:(half + 1) * TC, :], half, xhat_ready, p * TB + (half + 1) * TC, turned)

            def turn_ffn(f, half):
                turn(xhat[:, half * TC:(half + 1) * TC, :], half, xhatF_ready, f * TB + (half + 1) * TC, fturned)

            def queries(p, half):
                pe.wait_ge(ht_ready, p * 4 + 2 * half + 2)
                for c in range(DC):
                    for k in range(DC):
                        last = matmul3(nc, quad[2 * half + c], (K.Ah[:, k, c * P:(c + 1) * P], K.Al[:, k, c * P:(c + 1) * P]),
                                       ht(k, slice(half * CH, (half + 1) * CH)), k == 0, k == DC - 1)
                    last.then_inc(q_ps, 1)

            def values(p, n):
                for j in range(2):
                    t = 2 * n + j
                    for k in range(DC):
                        last = matmul3(nc, vbank[n][:, j * D:(j + 1) * D], ht(k, slice(t * P, (t + 1) * P)),
                                       (K.Mh[:, k, :], K.Ml[:, k, :]), k == 0, k == DC - 1)
                last.then_inc(v_ps, 1)

            def scores(b, t):
                for half in range(HB):
                    for k in range(DC):
                        cols = slice(t * P, (t + 1) * P)
                        last = matmul3(nc, sc[:, t % 2, half * CH:(half + 1) * CH], (qh[:, k, cols], ql[:, k, cols]),
                                       ht(k, slice(half * CH, (half + 1) * CH)), k == 0, k == DC - 1)
                last.then_inc(sc_ready, 1)

            def router(f, half):
                pe.wait_ge(f_ready, f * 4 + 2 * half + 2)
                for k in range(DC):
                    mm(lg_bank[half], K.rwp[:, k, :], fh[:, k, :], start=(k == 0), stop=False)
                    last = mm(lg_bank[half], K.rwh[:, k, :], fl[:, k, :], start=False, stop=(k == DC - 1))
                last.then_inc(lg_ps, 1)

            def turn_logits(f, half):
                hold(pe, lg_ready, f * HB + half + 1, idle)
                for t in range(TC):
                    n = half * TC + t
                    last = nc.tensor.transpose(ob[0][:, n * 2 * E:(n + 1) * 2 * E], lg[:, t * P:(t + 1) * P],
                                               ident[0:2 * E, 0:2 * E])
                last.then_inc(lt_ready, 1)

            def tiles(b, routed, more):
                for t in range(TB):
                    pe.wait_ge(p_ready, b * TB + t + 1)
                    if t == 0:
                        pe.wait_ge(vl_ready, b * 4 + 4)
                    else:
                        pe.wait_ge(ptl_ready, 2 * (b * TB + t))
                    for k in range(TB):
                        last = nc.tensor.transpose(ptp[:, k * P:(k + 1) * P], prob[:, t % 2, k * P:(k + 1) * P], ident[:])
                        if k % TC == TC - 1:
                            last.then_inc(pt_ready, 1)
                    if t + 2 < TB:
                        scores(b, t + 2)
                    elif more:
                        turn_keys(b + 1, t + 2 - TB)
                    elif t == TB - 1:
                        turn_ffn(b, 0)
                    if more and t == TB - 1:
                        queries(b + 1, 0)
                    if t >= 2:
                        pe.wait_ge(x1_ready, b * TB + t - 1)
                    if t == 0:
                        pe.wait_ge(lt_read, b + 1)
                    if routed and t == GATES_TILE:
                        turn_gates(nc, pe, K, b - 1, gt_bank)
                    for k in range(TB):
                        if k % TC == 0:
                            pe.wait_ge(ptl_ready, 2 * (b * TB + t) + k // TC + 1)
                        last = matmul3(nc, ob[t % 2][:, 0:D], (pTh[:, k, :], pTl[:, k, :]),
                                       (vh[:, k, :], vl[:, k, :]), k == 0, k == TB - 1)
                    last.then_inc(pv_ready, 1)

            def boundary(f, has_last, has_next):
                p = f + 1
                if not has_last:
                    turn_keys(p, 0)
                    turn_keys(p, 1)
                    queries(p, 0)
                if has_next:
                    queries(p, 1)
                    pe.wait_ge(ql_ready, p * 4 + 2)
                if has_last and has_next:
                    turn_ffn(f, 0)
                if has_next:
                    values(p, 0)
                    values(p, 1)
                if has_last and not has_next:
                    pe.wait_ge(w_taken, len(pieces))
                    for e in range(E):
                        last = mm(c_cols[:, 2 * e:2 * e + 2], K.u0[:, e, :], K.ones2[:], start=True, stop=True)
                    last.then_inc(K.c_ps, 1)
                    pe.wait_ge(K.h_split, 1)
                    pe.wait_ge(K.c_made, 1)
                    down(nc, K, vbank[1], lambda k: first_high[:, k, :], lambda k: first_low[:, k, :])
                    turn_ffn(f, 1)
                if has_last:
                    pe.wait_ge(x1_ready, f * TB + TB)
                if has_next:
                    values(p, 2)
                    values(p, 3)
                if has_last:
                    router(f, 0)
                if has_next:
                    pe.wait_ge(ql_ready, p * 4 + 4)
                elif has_last:
                    turn_logits(f, 0)
                if has_last and has_next:
                    turn_ffn(f, 1)
                if has_last and has_next:
                    pe.wait_ge(vl_ready, p * 4 + 3)
                    turn_logits(f, 0)
                if has_next:
                    scores(p, 0)
                if has_last:
                    router(f, 1)
                if has_next:
                    scores(p, 1)
                if has_last:
                    turn_logits(f, 1)

            sequences(pe, boundary, tiles)
    psc.close()


def experts(nc, out, K, ctx):
    def sbt(name, shape, dt=fp32):
        return ctx.enter_context(nc.sbuf_tensor(name, shape, dt))

    x_all, b1c, b2c = K.x_all, K.b1c, K.b2c
    negc, call = K.negc, K.call
    gh = (K.g0h, sbt("g1h", [P, CH], fp32r))
    gl = (K.g0l, sbt("g1l", [P, CH], fp32r))
    h_split, dn_ps, gf_ready, g_ready = K.h_split, K.dn_ps, K.gf_ready, K.g_ready
    w1h, w1l, w2h, w2l = K.w1h, K.w1l, K.w2h, K.w2l
    NA, NPRE, NG, LAG = 6, 3, 3, 4
    assert NU % NPRE == 0 and GROUPS % NG == 0 and (HB * NU) % NA == 0
    GX_AT, GX_SPLIT_AT, H_AT, DOWN_AT, GF_AT, GF_SPLIT_AT = (11, 18), (13, 20), (7, 12), 15, 16, 17
    Y_AT, OUT_AT, OD_AT = LAG + 2, LAG + 4, LAG + 5

    hin = sbt("hin", [P, HB, DC, CH])
    hh = sbt("hh", [P, DC, CH], fp32r)
    hl = sbt("hl", [P, DC, CH], fp32r)
    gf = sbt("gf", [P, CH])
    gxf = sbt("gxf", [P, DC, CH])
    gxh = sbt("gxh", [P, DC, CH], fp32r)
    gxl = sbt("gxl", [P, DC, CH], fp32r)
    af = sbt("af", [P, NA, CH])
    ah = sbt("ah", [P, NA, CH], fp32r)
    al = sbt("al", [P, NA, CH], fp32r)
    gbc = sbt("gbc", [P, E, CH])
    y = sbt("y", [P, HB, CH])
    yh = sbt("yh", [P, CH], fp32r)
    yl = sbt("yl", [P, CH], fp32r)
    te = sbt("te", [P, NG, CH])
    od = sbt("od", [P, TC, D])
    mod_bc = sbt("mod_bc", [P, B, 2, D])

    psc = ExitStack()
    pre = psc.enter_context(nc.psum_tensor("pre", [P, NPRE, CH], fp32))
    acc = psc.enter_context(nc.psum_tensor("acc", [P, NG, CH], fp32))
    op = psc.enter_context(nc.psum_tensor("op", [P, 2, CH], fp32))
    dn = op[:, 0, :]

    gates_in = K.sems(*[f"gates_in{e}" for e in range(E)])
    (mod_in, h_in, gxf_ready, gx_ready, pre_ps, af_ready, al_ready, a_used,
     te_ready, y0_ready, add_ready, yl_ready, out_ps, od_ready, xr_ready, of_ready, sent, last_ready,
     d2_s) = K.sems(
        "mod_in", "h_in", "gxf_ready", "gx_ready", "pre_ps", "af_ready",
        "al_ready", "a_used", "te_ready", "y0_ready", "add_ready", "yl_ready", "out_ps", "od_ready", "xr_ready", "of_ready",
        "sent", "last_ready", "d2_s")

    ROUTE_AT, GATES_AT = (0, 5, 7), 10
    gt_bank = op[0:TB * E, 1, 0:P]
    SPILLS = {g: LAST_UNIT[g] + LAG + 1 >= NU for g in range(GROUPS)}

    def slot(half, u):
        return (half * NU + u) % NA

    def chunks(eng, body):
        for half in range(HB):
            body(0, half, half > 0, True)
        with eng.Fori(1, B - 1) as b:
            for half in range(HB):
                body(b, half, True, True)
        for half in range(HB):
            body(B - 1, half, True, half < HB - 1)

    def following(b, half):
        return (b, half + 1) if half + 1 < HB else (b + 1, 0)

    def preceding(b, half):
        return (b, half - 1) if half else (b - 1, HB - 1)

    def hf_at(b, half):
        return K.hf_dram[bass.ds(b * HB + half, 1)].rearrange("a p c t -> p (a c) t")

    def gates_at(b, half, e):
        return K.gates_dram[bass.ds(b * HB + half, 1), :, e, :].rearrange("a t p -> (a t) p").partition_broadcast(P)

    def gate_rows(e):
        return gbc[:, e, :].rearrange("q (t p) -> q t p", t=TC)

    def out_at(b, half):
        o = out.rearrange("b (p h t) d -> b h p t d", h=HB, t=TC)
        return o[bass.ds(b, 1), half].rearrange("a p t d -> p (a t) d")

    with nc.Block() as block:
        @block.sync
        def _(sp):
            for e in range(E):
                sp.dma_start(gate_rows(e), gates_at(0, 0, e)).then_inc(gates_in[e], 16)
            sp.dma_start(hin[:, 0], hf_at(0, 0)).then_inc(h_in, 16)
            sp.dma_start(mod_bc[:], K.rows_dram[:, 1:3, :].partition_broadcast(P)).then_inc(mod_in, 16)

            def store(b, half):
                hold(sp, of_ready, b * HB + half + 1, K.idle["sp"])
                sp.dma_start(out_at(b, half), od[:]).then_inc(sent, 16)

            def body(b, half, prev, more):
                i = b * HB + half
                if more:
                    hold(sp, h_in, 16 * (i + 1), K.idle["sp"])
                    hold(sp, g_ready, i + 1, K.idle["sp"])
                    if prev:
                        hold(sp, gxf_ready, i * DC, K.idle["sp"])
                    sp.dma_start(hin[:, 1 - half], hf_at(*following(b, half))).then_inc(h_in, 16)
                if prev:
                    store(*preceding(b, half))
                if more:
                    if prev:
                        sp.wait_ge(K.gt_stored, 16 * B)
                    for e in range(E):
                        hold(sp, te_ready, i * E + e + 1, K.idle["sp"])
                        sp.dma_start(gate_rows(e), gates_at(*following(b, half), e)).then_inc(gates_in[e], 16)

            chunks(sp, body)
            for n in range(2):
                sp.wait_ge(last_ready, n + 1)
                sp.dma_start(out_at(B - 1, HB - 1)[:, 2 * n:2 * n + 2, :], od[:, 2 * n:2 * n + 2, :]).then_inc(sent, 16)
            sp.wait_ge(sent, 16 * (NCH + 1))

        @block.scalar
        def _(act):
            sa = nc.scalar.activation
            def body(b, half, prev, more):
                i = b * HB + half
                for u in range(NU):
                    s = slot(half, u)
                    act.wait_ge(pre_ps, i * NU + u + 1)
                    if prev or u >= NA:
                        act.wait_ge(a_used, i * NU + u - NA + 1)
                    sa(af[:, s, :], pre[:, u % NPRE, :], ACT.Gelu, bias=b1c[:, u:u + 1])
                    sa(ah[:, s, :], pre[:, u % NPRE, :], ACT.Gelu, bias=b1c[:, u:u + 1]).then_inc(af_ready, 1)
                    if isinstance(i, int) and i == 0 and u == GATES_AT + 1:
                        act.wait_ge(K.gt_ps, B)
                        sa(K.gt[:], gt_bank, ACT.Copy).then_inc(K.gt_made, 1)
                        store_gates(act, K, B - 1)
                    if isinstance(i, int) and i == 0 and u == ROUTE_AT[1] - 1:
                        route_exp(nc, act, K, B - 1, 0)
                        route_exp(nc, act, K, B - 1, 1)
                    if u in GX_AT:
                        c = GX_AT.index(u)
                        if c == 0:
                            act.wait_ge(h_in, (i + 1) * 16)
                        if c == 0 and prev:
                            act.wait_ge(gx_ready, i * DC)
                        sa(gxf[:, c, :], hin[:, half, c, :], ACT.Gelu).then_inc(gxf_ready, 1)
                    if u == GF_AT and more:
                        act.wait_ge(dn_ps, i + 2)
                        act.wait_ge(g_ready, i + 1)
                        sa(gf[:], dn[:], ACT.Gelu, bias=K.downbc[:]).then_inc(gf_ready, 1)

            chunks(act, body)

        @block.vector
        def _(dve):
            v = nc.vector
            dc = Chain(dve, d2_s)

            def split(hi, lo, full, sem):
                dc.link(v.tensor_copy(hi, full))
                v.tensor_tensor(lo, full, hi.bitcast(fp32), ALU.subtract).then_inc(sem, 1)

            links = [dc.n]

            def group(b, half, g, prev=True):
                i = b * HB + half
                dve.wait_ge(a_used, i * NU + LAST_UNIT[g] + 1)
                if g == 0:
                    v.tensor_scalar(y[:, half, :], acc[:, 0, :], call[:], None, ALU.add).then_inc(y0_ready, 1)
                else:
                    e = g - 1
                    dve.wait_ge(gates_in[e], (i + 1) * 16)
                    if g > NG:
                        dve.wait_ge(add_ready, i * E + g - NG)
                    elif prev:
                        dve.wait_ge(add_ready, i * E + min(g - (NG - 1), 0))
                    v.scalar_tensor_tensor(te[:, g % NG, :], acc[:, g % NG, :], negc[:, e:e + 1], gbc[:, e, :],
                                           ALU.add, ALU.mult).then_inc(te_ready, 1)

            def sum_parts(b, half):
                dve.wait_ge(add_ready, (b * HB + half + 1) * E)
                split(yh[:], yl[:], y[:, half, :], yl_ready)

            def outputs(b, half, n):
                i = b * HB + half
                dve.wait_ge(out_ps, i * 2 + n + 1)
                v.tensor_tensor(od[:, 2 * n:2 * n + 2, :].rearrange("p t d -> p t d"),
                                op[:, n, :].rearrange("p (t d) -> p t d", t=2),
                                mod_bc[:, bass.ds(b, 1), 0, :].to_broadcast([P, 2, D]), ALU.mult).then_inc(od_ready, 1)

            def body(b, half, prev, more):
                i = b * HB + half
                first = links[0] if not prev else links[0] + FIRST_LINKS + (i - 1) * DVE_LINKS_B
                dc.base, dc.n = first, 0
                for u in range(NU):
                    s = slot(half, u)
                    for g in range(GROUPS):
                        due = LAST_UNIT[g] + LAG + 1
                        if due == u:
                            group(b, half, g, prev)
                        if due - NU == u and prev:
                            group(*preceding(b, half), g)
                    if not prev and u in ROUTE_AT:
                        route(v, dve, dc, K, B - 1, ROUTE_AT.index(u))
                    dve.wait_ge(af_ready, i * NU + u + 1)
                    v.tensor_tensor(al[:, s, :], af[:, s, :], ah[:, s, :].bitcast(fp32), ALU.subtract).then_inc(al_ready, 1)
                    if prev and u == Y_AT:
                        sum_parts(*preceding(b, half))
                    if prev and u == OD_AT:
                        if isinstance(i, int) and i == 1:
                            dve.wait_ge(mod_in, 16)
                        else:
                            dve.wait_ge(sent, 16 * (i - 1))
                        outputs(*preceding(b, half), 0)
                    if prev and u == OD_AT + 1:
                        outputs(*preceding(b, half), 1)
                    if u in GX_SPLIT_AT:
                        c = GX_SPLIT_AT.index(u)
                        dve.wait_ge(gxf_ready, i * DC + c + 1)
                        split(gxh[:, c, :], gxl[:, c, :], gxf[:, c, :], gx_ready)
                    if u in H_AT and more:
                        c = H_AT.index(u)
                        if c == 0:
                            dve.wait_ge(h_in, (i + 2) * 16)
                        dc.link(v.tensor_copy(hh[:, c, :], hin[:, 1 - half, c, :]))
                        ins = v.tensor_tensor(hl[:, c, :], hin[:, 1 - half, c, :], hh[:, c, :].bitcast(fp32), ALU.subtract)
                        if c == DC - 1:
                            ins.then_inc(h_split, 1)
                    if u == GF_SPLIT_AT and more:
                        dve.wait_ge(gf_ready, i + 2)
                        split(gh[1 - half][:], gl[1 - half][:], gf[:], g_ready)
                assert dc.n == (DVE_LINKS_B if prev and more else FIRST_LINKS if more else dc.n), (dc.n, prev, more)
                dc.base = dc.base + dc.n
                dc.n = 0

            chunks(dve, body)
            b, half = B - 1, HB - 1
            for g in range(GROUPS):
                if SPILLS[g]:
                    group(b, half, g)
            dve.wait_ge(te_ready, NCH * E)
            dve.wait_ge(add_ready, NCH * E - 1)
            v.tensor_tensor(y[:, half, :], y[:, half, :], te[:, (GROUPS - 1) % NG, :], ALU.add).then_inc(add_ready, 1)
            sum_parts(b, half)
            dve.wait_ge(sent, 16 * (NCH - 1))
            dve.wait_ge(xr_ready, NCH)
            for n in range(2):
                pair, start = slice(2 * n, 2 * n + 2), (b * HB + half) * TC + 2 * n
                dve.wait_ge(out_ps, (NCH - 1) * 2 + n + 1)
                dc.link(v.tensor_tensor(od[:, pair, :], op[:, n, :].rearrange("p (t d) -> p t d", t=2),
                                        mod_bc[:, b:b + 1, 0, :].to_broadcast([P, 2, D]), ALU.mult))
                v.tensor_tensor(od[:, pair, :], od[:, pair, :], x_all[:, start:start + 2, :], ALU.add).then_inc(last_ready, 1)

        @block.gpsimd
        def _(pool):
            g = nc.gpsimd
            pool.wait_ge(mod_in, 16)

            def add(b, half, e):
                i = b * HB + half
                if e:
                    pool.wait_ge(add_ready, i * E + e)
                else:
                    pool.wait_ge(y0_ready, i + 1)
                pool.wait_ge(te_ready, i * E + e + 1)
                g.tensor_tensor(y[:, half, :], y[:, half, :], te[:, (e + 1) % NG, :], ALU.add).then_inc(add_ready, 1)

            def rows(b, half):
                return x_all[:, bass.ds((b * HB + half) * TC, TC), :]

            def finish(b, half):
                i = b * HB + half
                hold(pool, xr_ready, i + 1, K.idle["pool"])
                hold(pool, od_ready, 2 * (i + 1), K.idle["pool"])
                g.tensor_tensor(od[:], od[:], rows(b, half), ALU.add).then_inc(of_ready, 1)

            def residual(b, half):
                g.tensor_tensor(rows(b, half), rows(b, half),
                                mod_bc[:, bass.ds(b, 1), 1, :].to_broadcast([P, TC, D]), ALU.add).then_inc(xr_ready, 1)

            def body(b, half, prev, more):
                if prev:
                    for e in range(E):
                        if SPILLS[e + 1]:
                            add(*preceding(b, half), e)
                own = [e for e in range(E) if not SPILLS[e + 1]]
                for e in own[:2]:
                    add(b, half, e)
                if prev:
                    finish(*preceding(b, half))
                residual(b, half)
                for e in own[2:]:
                    add(b, half, e)

            chunks(pool, body)
            for e in range(E - 1):
                if SPILLS[e + 1]:
                    add(B - 1, HB - 1, e)

        @block.tensor
        def _(pe):
            mm = nc.tensor.matmul

            def second(b, half, u):
                i, g, s = b * HB + half, UNITS[u][0], slot(half, u)
                pe.wait_ge(al_ready, i * NU + u + 1)
                if u == FIRST_UNIT[g]:
                    if g > NG:
                        pe.wait_ge(te_ready, i * E + g - NG)
                    elif g == NG:
                        pe.wait_ge(y0_ready, i + 1)
                    elif prev_any(i):
                        pe.wait_ge(te_ready, i * E + g - (NG - 1))
                last = matmul3(nc, acc[:, g % NG, :], (w2h[:, u, :], w2l[:, u, :]), (ah[:, s, :], al[:, s, :]),
                               u == FIRST_UNIT[g], u == LAST_UNIT[g])
                last.then_inc(a_used, 1)

            def prev_any(i):
                return not (isinstance(i, int) and i == 0)

            def outputs(b, half, more=True):
                i = b * HB + half
                pe.wait_ge(gx_ready, (i + 1) * DC)
                pe.wait_ge(gf_ready, i + 2 if more else NCH)
                place = lambda t: (slice(t * P, (t + 1) * P), op[:, t // 2, (t % 2) * D:(t % 2 + 1) * D])
                for t in range(TC):
                    cols, dst = place(t)
                    for k in range(DC):
                        matmul3(nc, dst, (gxh[:, k, cols], gxl[:, k, cols]), (K.coreh[:, k, :], K.corel[:, k, :]),
                                k == 0 and t % 2 == 0, False)
                pe.wait_ge(yl_ready, i + 1)
                for t in range(TC):
                    cols, dst = place(t)
                    last = matmul3(nc, dst, (yh[:, cols], yl[:, cols]), (K.uph[:], K.upl[:]), False, t % 2 == 1)
                    if t % 2:
                        last.then_inc(out_ps, 1)

            def body(b, half, prev, more):
                i = b * HB + half
                for u in range(NU):
                    if u == 0:
                        pe.wait_ge(g_ready, i + 1)
                    if prev or u >= NPRE:
                        pe.wait_ge(af_ready, i * NU + u - NPRE + 1)
                    matmul3(nc, pre[:, u % NPRE, :], (w1h[:, u, :], w1l[:, u, :]), (gh[half][:], gl[half][:]),
                            True, True).then_inc(pre_ps, 1)
                    if u >= LAG:
                        second(b, half, u - LAG)
                    elif prev:
                        second(*preceding(b, half), u - LAG + NU)
                    if u == OUT_AT and prev:
                        outputs(*preceding(b, half))
                    if u == GATES_AT and not prev:
                        turn_gates(nc, pe, K, B - 1, gt_bank)
                    if u == DOWN_AT and more:
                        pe.wait_ge(h_split, i + 2)
                        if prev:
                            pe.wait_ge(od_ready, 2 * i)
                        down(nc, K, dn, lambda k: hh[:, k, :], lambda k: hl[:, k, :])

            chunks(pe, body)
            for u in range(NU - LAG, NU):
                second(B - 1, HB - 1, u)
            outputs(B - 1, HB - 1, False)
    psc.close()


DVE_LINKS_A = 50
DVE_LINKS_B = 6
FIRST_LINKS = 18


_ARGS = {'x': 'L0_attn_hidden_states', 'w_qkv': 'L0_attn_w_qkv', 'b_qkv': 'L0_attn_b_qkv', 'w_out': 'L0_attn_w_out',
         'b_out': 'L0_attn_b_out', 'c': 'L0_c', 'wmod': 'L0_wmod'}
for _n in ('down_w', 'down_b', 'up_w', 'up_b', 'router_w', 'router_b', 'shared_w1', 'shared_b1', 'shared_w2',
           'shared_b2', 'core_w', 'core_b'):
    _ARGS[_n] = 'L0_ffn_' + _n
for _e in range(E):
    for _n in ('w1', 'b1', 'w2', 'b2'):
        _ARGS[f'e{_e}_{_n}'] = f'L0_ffn_e{_e}_{_n}'


def kernel(**inputs):
    import numpy as _np
    import concourse.bacc as _bacc
    from concourse import mybir as _mybir
    from concourse.bass_utils import run_bass_kernel_spmd as _run

    nc = _bacc.Bacc("TRN2", target_bir_lowering=False, num_devices=1)
    arrays, args = {}, {}
    for short, name in _ARGS.items():
        v = _np.ascontiguousarray(inputs[name])
        arrays[f"in_{short}_dram"] = v
        args[short] = nc.dram_tensor(f"in_{short}_dram", v.shape, _mybir.dt.from_np(v.dtype), kind="ExternalInput").ap()
    o = nc.dram_tensor("out_0_dram", (B, S, D), _mybir.dt.float32, kind="ExternalOutput").ap()
    adaln_block(nc, args, o)
    r = _run(nc, [arrays], core_ids=[0])
    return r.results[0]["out_0_dram"]
```
